# Optimizing a Trainium2 kernel written in Bass

```python
import numpy as np
import jax
import jax.numpy as jnp

def _softmax(x, axis=-1):
    return jax.nn.softmax(x, axis=axis)

def _gelu(x):
    return jax.nn.gelu(x, approximate=True)

def _silu(x):
    return jax.nn.silu(x)

def _sigmoid(x):
    return jax.nn.sigmoid(x)

def _layernorm(x, axis=-1, eps=1e-05):
    m = jnp.mean(x, axis=axis, keepdims=True)
    v = jnp.var(x, axis=axis, keepdims=True)
    return (x - m) / jnp.sqrt(v + eps)

def _scatter_add(tgt, idx, src, axis=0):
    return tgt.at[idx].add(src)

def _segment_sum(src, seg, n):
    return jax.ops.segment_sum(src, seg, n)
kernel_name = 'mk_prb_d1_jaxref_r4_c3cc49'

def setup_inputs(seed: int=0):
    np.random.seed(seed)
    _w = jnp.asarray

    def _L0_attn_setup():
        import jax, jax.numpy as jnp
        import numpy as np
        N_HEAD = 16
        N_EMBED = 512
        N_BLOCK = 512
        THETA = 10000.0

        def _rope_cos_sin(n_head, head_dim):
            freqs = THETA ** (-(jnp.arange(0, head_dim, 2, dtype=jnp.float32) / head_dim))
            t = jnp.arange(n_head, dtype=jnp.float32)
            ang = jnp.outer(t, freqs)
            return (jnp.cos(ang)[None, :, None, :], jnp.sin(ang)[None, :, None, :])

        def _apply_rope(x, cos, sin):
            B, H, T, hd = x.shape
            xp = x.reshape(B, H, T, hd // 2, 2)
            a, b = (xp[..., 0], xp[..., 1])
            out = jnp.stack([a * cos - b * sin, a * sin + b * cos], axis=-1)
            return out.reshape(B, H, T, hd)
        key = jax.random.key(seed)
        ks = jax.random.split(key, 5)
        E = N_EMBED
        x = jax.random.normal(ks[0], (2, 512, E), dtype=jnp.float32)
        s = 1.0 / np.sqrt(E)
        w_attn = jax.random.normal(ks[1], (E, 3 * E), dtype=jnp.float32) * s
        b_attn = jnp.zeros((3 * E,), dtype=jnp.float32)
        w_proj = jax.random.normal(ks[2], (E, E), dtype=jnp.float32) * s
        b_proj = jnp.zeros((E,), dtype=jnp.float32)
        return {'x': x, 'w_attn': w_attn, 'b_attn': b_attn, 'w_proj': w_proj, 'b_proj': b_proj}
    _L0_attn_in = _L0_attn_setup()

    def _L0_ffn_setup():
        import jax, jax.numpy as jnp
        import numpy as np
        TOP_K = 2
        key = jax.random.key(seed)
        k1, k2, k3, k4 = jax.random.split(key, 4)
        B, S, H, I, E = (2, 256, 512, 352, 8)
        hidden_states = jax.random.normal(k1, (B, S, H), dtype=jnp.float32)
        gate_w = jax.random.normal(k2, (E, H), dtype=jnp.float32) * (1.0 / np.sqrt(H))
        w1 = jax.random.normal(k3, (E, 2 * I, H), dtype=jnp.float32) * (1.0 / np.sqrt(H))
        w2 = jax.random.normal(k4, (E, H, I), dtype=jnp.float32) * (1.0 / np.sqrt(I))
        return {'hidden_states': hidden_states, 'gate_w': gate_w, 'w1': w1, 'w2': w2}
    _L0_ffn_in = _L0_ffn_setup()
    _d = {'L0_attn_x': _L0_attn_in['x'], 'L0_attn_w_attn': _L0_attn_in['w_attn'], 'L0_attn_b_attn': _L0_attn_in['b_attn'], 'L0_attn_w_proj': _L0_attn_in['w_proj'], 'L0_attn_b_proj': _L0_attn_in['b_proj'], 'L0_ffn_gate_w': _L0_ffn_in['gate_w'], 'L0_ffn_w1': _L0_ffn_in['w1'], 'L0_ffn_w2': _L0_ffn_in['w2']}
    _x0 = _d['L0_attn_x']
    _d['L0_attn_x'] = jax.random.normal(jax.random.fold_in(jax.random.key(seed), 1), (2, 1024, 512), dtype=_x0.dtype)
    del _x0
    return _d

def reference(L0_attn_x, L0_attn_w_attn, L0_attn_b_attn, L0_attn_w_proj, L0_attn_b_proj, L0_ffn_gate_w, L0_ffn_w1, L0_ffn_w2):

    def _L0_attn_ref(x, w_attn, b_attn, w_proj, b_proj):
        import jax, jax.numpy as jnp
        import numpy as np
        N_HEAD = 16
        N_EMBED = 512
        N_BLOCK = 512
        THETA = 10000.0

        def _rope_cos_sin(n_head, head_dim):
            freqs = THETA ** (-(jnp.arange(0, head_dim, 2, dtype=jnp.float32) / head_dim))
            t = jnp.arange(n_head, dtype=jnp.float32)
            ang = jnp.outer(t, freqs)
            return (jnp.cos(ang)[None, :, None, :], jnp.sin(ang)[None, :, None, :])

        def _apply_rope(x, cos, sin):
            B, H, T, hd = x.shape
            xp = x.reshape(B, H, T, hd // 2, 2)
            a, b = (xp[..., 0], xp[..., 1])
            out = jnp.stack([a * cos - b * sin, a * sin + b * cos], axis=-1)
            return out.reshape(B, H, T, hd)
        B, T, E = x.shape
        H = N_HEAD
        hd = E // H
        qkv = x @ w_attn + b_attn
        q, k, v = jnp.split(qkv, 3, axis=-1)
        q = q.reshape(B, T, H, hd).transpose(0, 2, 1, 3)
        k = k.reshape(B, T, H, hd).transpose(0, 2, 1, 3)
        v = v.reshape(B, T, H, hd).transpose(0, 2, 1, 3)
        cos, sin = _rope_cos_sin(H, hd)
        q = _apply_rope(q, cos, sin)
        k = _apply_rope(k, cos, sin)
        scores = jnp.einsum('bhtd,bhsd->bhts', q, k)
        causal = jnp.tril(jnp.ones((T, T), dtype=bool))
        scores = jnp.where(causal[None, None], scores, jnp.float32(-jnp.inf))
        attn = jax.nn.softmax(scores, axis=-1) * E ** (-0.5)
        o = jnp.einsum('bhts,bhsd->bhtd', attn, v)
        o = o.transpose(0, 2, 1, 3).reshape(B, T, E)
        return o @ w_proj + b_proj

    def _L0_ffn_ref(hidden_states, gate_w, w1, w2):
        import jax, jax.numpy as jnp
        import numpy as np
        TOP_K = 2
        B, S, H = hidden_states.shape
        E = gate_w.shape[0]
        T = B * S
        x = hidden_states.reshape(T, H)
        logits = jnp.einsum('th,eh->te', x, gate_w)
        probs = jax.nn.softmax(logits, axis=-1)
        topw, sel = jax.lax.top_k(probs, TOP_K)
        topw = topw / jnp.sum(topw, axis=-1, keepdims=True)
        combine = jnp.zeros((T, E), dtype=x.dtype).at[jnp.arange(T)[:, None], sel].add(topw)
        gate_up = jnp.einsum('th,eoh->eto', x, w1)
        g, u = jnp.split(gate_up, 2, axis=-1)
        act = jax.nn.silu(g) * u
        expert_out = jnp.einsum('eti,ehi->eth', act, w2)
        out = jnp.einsum('eth,te->th', expert_out, combine)
        return out.reshape(B, S, H)
    x = L0_attn_x
    xn = _layernorm(x, axis=-1)
    x = x + _L0_attn_ref(xn, L0_attn_w_attn, L0_attn_b_attn, L0_attn_w_proj, L0_attn_b_proj) + _L0_ffn_ref(xn, L0_ffn_gate_w, L0_ffn_w1, L0_ffn_w2)
    return x

_drawn_inputs = setup_inputs


def setup_inputs(seed=0):
    import zlib

    import numpy as np

    out = dict(_drawn_inputs(seed))
    spreads = {'L0_attn_b_attn': (0.0, 0.8), 'L0_attn_b_proj': (0.0, 0.1)}
    factors = {}
    for name, (base, spread) in spreads.items():
        noise = np.random.default_rng([zlib.crc32(name.encode()), seed]).standard_normal(out[name].shape)
        drawn = base * np.exp(spread * noise) if base else spread * noise
        out[name] = jnp.asarray(drawn.astype(out[name].dtype))
    for name, factor in factors.items():
        out[name] = (out[name] * factor).astype(out[name].dtype)
    return out
```

```python
import concourse.bass as bass
from concourse import mybir
from contextlib import ExitStack

F32 = mybir.dt.float32
F32R = mybir.dt.float32r
BF16 = mybir.dt.bfloat16
U32 = mybir.dt.uint32
I32 = mybir.dt.int32
ALU = mybir.AluOpType
ACT = mybir.ActivationFunctionType
AX = mybir.AxisListType

P = 128
B, S, D = 2, 1024, 512
T = B * S
H, HD = 16, 32
DK = D // P
CH = 512
NCH = T // CH
TPC = CH // P
NT = T // P
E, I, TOPK = 8, 352, 2
HG = P // HD
NG = H // HG
QK_TILES = 2 * NG
EPS = 1e-5
SCALE = float(D) ** -0.5
NEG = -3.0e38
SLOT_TILES = T * TOPK // P + E - 1
I_TILES = [(0, 128), (128, 128), (256, 96)]


def as_f32(ap):
    return ap.bitcast(F32)


class Memory:

    def __init__(self, nc, ctx):
        self.nc, self.ctx = nc, ctx

    def sbuf(self, name, shape, dtype):
        return self.ctx.enter_context(self.nc.sbuf_tensor(name, shape, dtype))

    def psum(self, name, shape, dtype=F32):
        return self.ctx.enter_context(self.nc.psum_tensor(name, shape, dtype))

    def sem(self, name):
        return self.ctx.enter_context(self.nc.semaphore(name))


def project_qkv(nc, keep, scratch, x, w_attn, bias_qk, bias_qk_pair, bias_v, gate_t, rope_cos, rope_sin,
                rope_cos_col, rope_sin_col):
    ctx = ExitStack()
    with ctx:
        m = Memory(nc, ctx)
        w_raw = m.sbuf("w_raw", [P, DK, 3 * D], F32)
        w_hi = m.sbuf("w_hi", [P, DK, 3 * D], F32R)
        w_lo = m.sbuf("w_lo", [P, DK, 3 * D], F32R)
        cos_row = m.sbuf("cos_row", [P, D], F32)
        sin_row = m.sbuf("sin_row", [P, D], F32)
        turned = m.sbuf("turned", [P, DK, D], F32)
        gate_raw = m.sbuf("gate_raw", [P, DK, E], F32)
        gate_hi = m.sbuf("gate_hi", [P, DK, E], F32R)
        gate_lo = m.sbuf("gate_lo", [P, DK, E], F32R)
        small = m.sbuf("small", [P, 8, QK_TILES], F32)
        bias_col, bias_pair, cos_col, sin_col, bias_rot, bias_tmp = (small[:, i, :] for i in range(6))
        bias_v_row = m.sbuf("bias_v_row", [P, D], F32)
        stats = m.sbuf("stats", [P, NT, 6], F32)
        mean_var = m.sbuf("mean_var", [P, NT, 2], F32)
        zeros = m.sbuf("zeros", [P, D], F32)
        eps = m.sbuf("eps", [P, 1], F32)
        root = m.sbuf("root", [P, NT], F32)
        newton = m.sbuf("newton", [P, NT], F32)
        rstd = m.sbuf("rstd", [P, NT], F32)
        shift = m.sbuf("shift", [P, TPC], F32)
        xt_hi = m.sbuf("xt_hi", [P, DK, CH], F32R)
        xt_lo = m.sbuf("xt_lo", [P, DK, CH], F32R)
        logits_t = m.sbuf("logits_t", [P, CH], F32)
        STG = 4
        st_hi = m.sbuf("st_hi", [P, STG, CH], F32R)
        st_lo = m.sbuf("st_lo", [P, STG, CH], F32R)
        st_v = m.sbuf("st_v", [P, TPC, D], F32)
        x_raw = m.sbuf("x_raw", [P, NT, D], F32)
        xn = m.sbuf("xn", [P, TPC, D], F32)
        ident, logits = m.sbuf("ident", [P, P], F32), keep["logits"]

        RING = 6
        banks = [m.psum(f"bank{i}", [P, CH]) for i in range(RING)]
        USES = DK + 1 + TPC + QK_TILES + 1
        U_GATE, U_V, U_QK, U_LT = DK, DK + 1, DK + 1 + TPC, DK + 1 + TPC + QK_TILES

        x_in = [m.sem(f"x_in{c}") for c in range(NCH)]
        w_in = [m.sem(f"w_in{i}") for i in range(3)]
        rope_in = m.sem("rope_in")
        small_in = m.sem("small_in")
        gate_in = m.sem("gate_in")
        chain = m.sem("dve_chain")
        stats_done = m.sem("stats_done")
        zeros_done = m.sem("zeros_done")
        cleared = m.sem("cleared")
        eps_done = m.sem("eps_done")
        root_done = m.sem("root_done")
        rstd_done = m.sem("rstd_done")
        shift_done = m.sem("shift_done")
        xn_done = m.sem("xn_done")
        pool_chain = m.sem("pool_chain")
        ident_done = m.sem("ident_done")
        whi_done = m.sem("whi_done")
        wlo_done = m.sem("wlo_done")
        wqk_done = m.sem("wqk_done")
        bias_done = m.sem("bias_done")
        bank_full = m.sem("bank_full")
        hi_done = m.sem("hi_done")
        bank_free = m.sem("bank_free")
        xn_stored = m.sem("xn_stored")
        st_free = [m.sem(f"st_free{i}") for i in range(STG)]
        v_free = [m.sem(f"v_free{a}") for a in range(TPC)]
        st_ready = m.sem("st_ready")
        v_ready = m.sem("v_ready")

        w_view = w_attn.rearrange("(k p) n -> p k n", p=P)
        x_view = x.rearrange("b (c a p) d -> (b c) p a d", p=P, a=TPC)
        qk_hi_view = scratch["qk_hi"].rearrange("(m p) t -> m p t", p=P)
        qk_lo_view = scratch["qk_lo"].rearrange("(m p) t -> m p t", p=P)
        xn_view = scratch["xn"].rearrange("(c a p) d -> c p a d", p=P, a=TPC)
        v_view = scratch["v"].rearrange("(a p) d -> p a d", p=P)
        parts = [(2 * D, 3 * D), (0, D), (D, 2 * D)]
        block = ctx.enter_context(nc.Block())

        @block.sync
        def _(sp):
            sp.sem_inc(bank_free, 1)
            for s in st_free:
                sp.sem_inc(s, 32)
            for s in v_free:
                sp.sem_inc(s, 16)
            for c in range(NCH):
                sp.dma_start(x_raw[:, c * TPC:(c + 1) * TPC, :], x_view[c]).then_inc(x_in[c], 16)
            with sp.Fori(0, NCH) as c:
                sp.wait_ge(xn_done, (c + 1) * TPC)
                sp.dma_start(xn_view[bass.ds(c, 1)].rearrange("c p a d -> (c p) a d"), xn[:]).then_inc(xn_stored, 16)
                for a in range(TPC):
                    sp.wait_ge(v_ready, c * TPC + (a + 1))
                    sp.dma_start(v_view[:, bass.ds(c * TPC + a, 1), :], st_v[:, a:a + 1, :]).then_inc(v_free[a], 16)
                for i in range(QK_TILES):
                    sp.wait_ge(st_ready, c * QK_TILES + (i + 1))
                    sp.dma_start(qk_hi_view[i, :, bass.ds(c * CH, CH)], as_f32(st_hi[:, i % STG, :])).then_inc(st_free[i % STG], 16)
                    sp.dma_start(qk_lo_view[i, :, bass.ds(c * CH, CH)], as_f32(st_lo[:, i % STG, :])).then_inc(st_free[i % STG], 16)
            for s in st_free:
                sp.wait_ge(s, 32 + 32 * NCH * QK_TILES // STG)
            for s in v_free:
                sp.wait_ge(s, 16 + 16 * NCH)
            sp.wait_ge(cleared, 16)
            sp.wait_ge(xn_stored, 16 * NCH)

        @block.gpsimd
        def _(pool):
            nc.gpsimd.memset(ident[:], 0.0).then_inc(pool_chain, 1)
            pool.wait_ge(pool_chain, 1)
            nc.gpsimd.affine_select(out=ident[:], in_=ident[:], compare_op=ALU.not_equal, fill=1.0, base=0,
                                    pattern=[[-1, P]], channel_multiplier=1).then_inc(ident_done, 1)
            done = 1
            pool.wait_ge(rope_in, 32)
            sign = sin_row[:].rearrange("p (n two) -> p n two", two=2)
            t = turned[:].rearrange("p k (n two) -> p k n two", two=2)
            for i, (lo, hi) in enumerate(parts[1:]):
                w = w_raw[:, :, lo:hi]
                pair = w.rearrange("p k (n two) -> p k n two", two=2)
                pool.wait_ge(w_in[1 + i], 16)
                if i:
                    pool.wait_ge(wqk_done, i)
                for k in range(DK):
                    for j in range(2):
                        last = nc.gpsimd.tensor_tensor(t[:, k, :, j], pair[:, k, :, 1 - j], sign[:, :, j], ALU.mult)
                last.then_inc(pool_chain, 1)
                done += 1
                pool.wait_ge(pool_chain, done)
                for k in range(DK):
                    last = nc.gpsimd.tensor_tensor(w[:, k, :], w[:, k, :], cos_row[:], ALU.mult)
                last.then_inc(pool_chain, 1)
                done += 1
                pool.wait_ge(pool_chain, done)
                nc.gpsimd.tensor_tensor(w, w, turned[:], ALU.add).then_inc(pool_chain, 1)
                done += 1
                pool.wait_ge(pool_chain, done)
                nc.gpsimd.tensor_copy(w_hi[:, :, lo:hi], w).then_inc(pool_chain, 1)
                done += 1
                pool.wait_ge(pool_chain, done)
                nc.gpsimd.tensor_tensor(w_lo[:, :, lo:hi], w, as_f32(w_hi[:, :, lo:hi]), ALU.subtract).then_inc(wqk_done, 1)
            for c in range(1, NCH):
                pool.wait_ge(rstd_done, 2)
                pool.wait_ge(bank_full, (c - 1) * USES + DK)
                pool.wait_ge(xn_stored, c * 16)
                for a in range(TPC):
                    t = c * TPC + a
                    nc.gpsimd.tensor_scalar(xn[:, a, :], x_raw[:, t, :], mean_var[:, t, 0:1], rstd[:, t:t + 1],
                                            ALU.subtract, ALU.mult).then_inc(xn_done, 1)

        @block.scalar
        def _(act):
            act.dma_start(small[:, 0, :], bias_qk).then_inc(small_in, 16)
            act.dma_start(small[:, 1, :], bias_qk_pair).then_inc(small_in, 16)
            act.dma_start(small[:, 2, :], rope_cos_col).then_inc(small_in, 16)
            act.dma_start(small[:, 3, :], rope_sin_col).then_inc(small_in, 16)
            act.dma_start(bias_v_row[:], bias_v.partition_broadcast(P)).then_inc(small_in, 16)
            act.dma_start(gate_raw[:], gate_t.rearrange("(k p) e -> p k e", p=P)).then_inc(gate_in, 16)
            act.dma_start(cos_row[:], rope_cos.partition_broadcast(P)).then_inc(rope_in, 16)
            act.dma_start(sin_row[:], rope_sin.partition_broadcast(P)).then_inc(rope_in, 16)
            for i in (1, 0, 2):
                lo, hi = parts[i]
                act.dma_start(w_raw[:, :, lo:hi], w_view[:, :, lo:hi]).then_inc(w_in[i], 16)
            act.wait_ge(zeros_done, 1)
            act.dma_start(scratch["routed"].rearrange("(i p) d -> p i d", p=P),
                          zeros[:].unsqueeze(1).to_broadcast([P, SLOT_TILES, D])).then_inc(cleared, 16)
            act.wait_ge(gate_in, 16)
            nc.scalar.copy(gate_hi[:], gate_raw[:]).then_inc(whi_done, 1)
            act.wait_ge(stats_done, 1)
            act.wait_ge(eps_done, 1)
            nc.scalar.activation(root[:, 0:TPC], mean_var[:, 0:TPC, 1], ACT.Sqrt, bias=eps[:]).then_inc(root_done, 1)
            act.wait_ge(shift_done, 1)
            for a in range(TPC):
                nc.scalar.activation(xn[:, a, :], x_raw[:, a, :], ACT.Identity, bias=shift[:, a:a + 1],
                                     scale=rstd[:, a:a + 1]).then_inc(xn_done, 1)
            act.wait_ge(stats_done, NCH)
            nc.scalar.activation(root[:, TPC:NT], mean_var[:, TPC:NT, 1], ACT.Sqrt, bias=eps[:]).then_inc(root_done, 1)
            act.wait_ge(w_in[0], 16)
            nc.scalar.copy(w_hi[:, :, 2 * D:3 * D], w_raw[:, :, 2 * D:3 * D]).then_inc(whi_done, 1)
            act.wait_ge(bias_done, 1)
            with act.Fori(0, NCH) as c:
                for k in range(DK):
                    act.wait_ge(bank_full, c * USES + (k + 1))
                    nc.scalar.copy(xt_hi[:, k, :], banks[k % RING][:]).then_inc(hi_done, 1)
                for i in range(QK_TILES):
                    u = U_QK + i
                    act.wait_ge(bank_full, c * USES + (u + 1))
                    act.wait_ge(st_free[i % STG], (c * (QK_TILES // STG) + (i // STG + 1)) * 32)
                    nc.scalar.activation(st_hi[:, i % STG, :], banks[u % RING][:], ACT.Identity,
                                         bias=bias_rot[:, i:i + 1]).then_inc(hi_done, 1)

        @block.vector
        def _(dve):
            n = [0]

            def link(ins):
                n[0] += 1
                ins.then_inc(chain, 1)
                dve.wait_ge(chain, n[0])

            def invert(lo, hi, number):
                r, v, t = rstd[:, lo:hi], mean_var[:, lo:hi, 1], newton[:, lo:hi]
                dve.wait_ge(root_done, number)
                link(nc.vector.reciprocal(r, root[:, lo:hi]))
                link(nc.vector.tensor_tensor(t, r, r, ALU.mult))
                link(nc.vector.scalar_tensor_tensor(t, v, EPS, t, ALU.add, ALU.mult))
                link(nc.vector.tensor_scalar(t, t, -0.5, 1.5, ALU.mult, ALU.add))
                nc.vector.tensor_tensor(r, r, t, ALU.mult).then_inc(rstd_done, 1)
                dve.wait_ge(rstd_done, number)

            nc.vector.memset(zeros[:], 0.0).then_inc(zeros_done, 1)
            link(nc.vector.memset(logits_t[:], 0.0))
            nc.vector.memset(eps[:], EPS).then_inc(eps_done, 1)
            for c in range(NCH):
                dve.wait_ge(x_in[c], 16)
                for a in range(TPC):
                    last = nc.vector.bn_stats(stats[:, c * TPC + a, :], x_raw[:, c * TPC + a, :])
                link(last)
                for a in range(TPC):
                    last = nc.vector.bn_aggr(mean_var[:, c * TPC + a, :], stats[:, c * TPC + a, :])
                last.then_inc(stats_done, 1)
                if c == 0:
                    invert(0, TPC, 1)
                    nc.vector.scalar_tensor_tensor(shift[:], mean_var[:, 0:TPC, 0], -1.0, rstd[:, 0:TPC],
                                                   ALU.mult, ALU.mult).then_inc(shift_done, 1)
            invert(TPC, NT, 2)
            dve.wait_ge(whi_done, 1)
            nc.vector.tensor_tensor(gate_lo[:], gate_raw[:], as_f32(gate_hi[:]), ALU.subtract).then_inc(wlo_done, 1)
            dve.wait_ge(whi_done, 2)
            nc.vector.tensor_tensor(w_lo[:, :, 2 * D:3 * D], w_raw[:, :, 2 * D:3 * D], as_f32(w_hi[:, :, 2 * D:3 * D]),
                                    ALU.subtract).then_inc(wlo_done, 1)
            dve.wait_ge(small_in, 80)
            link(nc.vector.tensor_tensor(bias_tmp, bias_pair, sin_col, ALU.mult))
            link(nc.vector.tensor_tensor(bias_rot, bias_col, cos_col, ALU.mult))
            nc.vector.tensor_tensor(bias_rot, bias_rot, bias_tmp, ALU.add).then_inc(bias_done, 1)
            dve.wait_ge(bias_done, 1)
            with dve.Fori(0, NCH) as c:
                HI = DK + QK_TILES
                for k in range(DK):
                    dve.wait_ge(hi_done, c * HI + (k + 1))
                    nc.vector.tensor_tensor(xt_lo[:, k, :], banks[k % RING][:], as_f32(xt_hi[:, k, :]),
                                            ALU.subtract).then_inc(bank_free, 1)
                u = U_GATE
                dve.wait_ge(bank_full, c * USES + (u + 1))
                nc.vector.tensor_copy(logits_t[0:E, :], banks[u % RING][0:E, :]).then_inc(bank_free, 1)
                for a in range(TPC):
                    u = U_V + a
                    dve.wait_ge(bank_full, c * USES + (u + 1))
                    dve.wait_ge(v_free[a], (c + 1) * 16)
                    nc.vector.tensor_tensor(st_v[:, a, :], banks[u % RING][:], bias_v_row[:], ALU.add).then_inc(v_ready, 1)
                for i in range(QK_TILES):
                    u = U_QK + i
                    dve.wait_ge(hi_done, c * HI + (DK + i + 1))
                    nc.vector.scalar_tensor_tensor(st_lo[:, i % STG, :], banks[u % RING][:], bias_rot[:, i:i + 1],
                                                   as_f32(st_hi[:, i % STG, :]), ALU.add, ALU.subtract).then_inc(st_ready, 1)
                u = U_LT
                dve.wait_ge(bank_full, c * USES + (u + 1))
                nc.vector.tensor_copy(logits[:, bass.ds(c * TPC, TPC), :],
                                      banks[u % RING][:].rearrange("p (a q) -> p a q", q=P)[:, :, 0:E]).then_inc(bank_free, 1)

        @block.tensor
        def _(pe):
            reads = ([(bank_free, DK + 2, k + 1) for k in range(DK)] + [(bank_free, DK + 2, DK + 1)]
                     + [(v_ready, TPC, a + 1) for a in range(TPC)]
                     + [(st_ready, QK_TILES, i + 1) for i in range(QK_TILES)] + [(bank_free, DK + 2, DK + 2)])

            def claim(c, u):
                if u >= RING:
                    sem, per, number = reads[u - RING]
                    pe.wait_ge(sem, c * per + number + (sem is bank_free))
                else:
                    pe.wait_ge(bank_free, c * (DK + 2) + 1)

            def split_product(out, a_hi, a_lo, b_hi, b_lo):
                for k in range(DK):
                    nc.tensor.matmul(out, a_hi(k), b_hi(k), start=(k == 0), stop=False)
                    nc.tensor.matmul(out, a_hi(k), b_lo(k), start=False, stop=False)
                    last = nc.tensor.matmul(out, a_lo(k), b_hi(k), start=False, stop=(k == DK - 1))
                return last

            pe.wait_ge(ident_done, 1)
            pe.wait_ge(wlo_done, 2)
            with pe.Fori(0, NCH) as c:
                pe.wait_ge(xn_done, (c + 1) * TPC)
                for k in range(DK):
                    claim(c, k)
                    for a in range(TPC):
                        last = nc.tensor.transpose(banks[k % RING][:, a * P:(a + 1) * P], xn[:, a, k * P:(k + 1) * P], ident[:])
                    last.then_inc(bank_full, 1)
                pe.wait_ge(bank_free, c * (DK + 2) + DK + 1)
                u = U_GATE
                claim(c, u)
                split_product(banks[u % RING][0:E, :], lambda k: gate_hi[:, k, :], lambda k: gate_lo[:, k, :],
                              lambda k: xt_hi[:, k, :], lambda k: xt_lo[:, k, :]).then_inc(bank_full, 1)
                for a in range(TPC):
                    u = U_V + a
                    claim(c, u)
                    split_product(banks[u % RING][:], lambda k: xt_hi[:, k, a * P:(a + 1) * P],
                                  lambda k: xt_lo[:, k, a * P:(a + 1) * P], lambda k: w_hi[:, k, 2 * D:3 * D],
                                  lambda k: w_lo[:, k, 2 * D:3 * D]).then_inc(bank_full, 1)
                for i in range(QK_TILES):
                    u = U_QK + i
                    if i % NG == 0:
                        pe.wait_ge(wqk_done, i // NG + 1)
                    claim(c, u)
                    split_product(banks[u % RING][:], lambda k: w_hi[:, k, i * P:(i + 1) * P],
                                  lambda k: w_lo[:, k, i * P:(i + 1) * P], lambda k: xt_hi[:, k, :],
                                  lambda k: xt_lo[:, k, :]).then_inc(bank_full, 1)
                u = U_LT
                claim(c, u)
                pe.wait_ge(bank_free, c * (DK + 2) + DK + 2)
                for a in range(TPC):
                    last = nc.tensor.transpose(banks[u % RING][:, a * P:(a + 1) * P], logits_t[:, a * P:(a + 1) * P], ident[:])
                last.then_inc(bank_full, 1)


def route(nc, keep, scratch):
    ctx = ExitStack()
    with ctx:
        m = Memory(nc, ctx)
        logits = keep["logits"]
        iota_e = m.sbuf("iota_e", [P, E], F32)
        iota_rows = m.sbuf("iota_rows", [P, NT], F32)
        iota_tile = m.sbuf("iota_tile", [1, SLOT_TILES], F32)
        before = m.sbuf("before", [P, P], BF16)
        ones = m.sbuf("ones16", [P, P], BF16)
        top1 = m.sbuf("top1", [P, NT], F32)
        shifted = m.sbuf("shifted", [P, NT, E], F32)
        expd = m.sbuf("expd", [P, NT, E], F32)
        denom = m.sbuf("denom", [P, 2, NT], F32)
        prob = m.sbuf("prob", [P, NT, E], F32)
        best = m.sbuf("best", [P, NT, 8], F32)
        best_at = m.sbuf("best_at", [P, NT, 8], U32)
        chosen = m.sbuf("chosen", [P, NT, TOPK], F32)
        mask = m.sbuf("mask", [P, TOPK, NT, E], F32)
        both = m.sbuf("both", [P, NT, E], BF16)
        total = m.sbuf("total", [P, NT, E], F32)
        prefix = m.sbuf("prefix", [P, NT + 1, E], F32)
        over = m.sbuf("over", [P, E, NT], F32)
        tiles = m.sbuf("tiles", [P, E], F32)
        upto = m.sbuf("upto", [P, E], F32)
        base = m.sbuf("base", [P, E], F32)
        place = m.sbuf("place", [P, NT, E], F32)
        picked = m.sbuf("picked", [P, TOPK, NT, E], F32)
        slot_f = m.sbuf("slot_f", [P, TOPK, NT], F32)
        pair_sum = m.sbuf("pair_sum", [P, 2, NT], F32)
        passed = m.sbuf("passed", [1, SLOT_TILES, E], F32)
        owner = m.sbuf("owner", [1, 2, SLOT_TILES], F32)
        rank_ps, total_ps = m.psum("rank_ps", [P, CH]), m.psum("total_ps", [P, CH])
        consts, pool_chain = m.sem("consts_r"), m.sem("pool_chain_r")
        chain, shift_done, exp_done = m.sem("chain_r"), m.sem("shift_done_r"), m.sem("exp_done_r")
        both_done, counted = m.sem("both_done"), m.sem("counted")
        block = ctx.enter_context(nc.Block())

        @block.gpsimd
        def _(pool):
            nc.gpsimd.iota(iota_e[:], pattern=[[1, E]], base=0, channel_multiplier=0,
                           allow_small_or_imprecise_dtypes=True).then_inc(consts, 1)
            nc.gpsimd.iota(iota_rows[:], pattern=[[P, NT]], base=0, channel_multiplier=0,
                           allow_small_or_imprecise_dtypes=True).then_inc(consts, 1)
            nc.gpsimd.iota(iota_tile[:], pattern=[[1, SLOT_TILES]], base=0, channel_multiplier=0,
                           allow_small_or_imprecise_dtypes=True).then_inc(consts, 1)
            pool.wait_ge(consts, 3)
            nc.gpsimd.memset(ones[:], 1.0).then_inc(consts, 1)
            nc.gpsimd.memset(before[:], 0.0).then_inc(pool_chain, 1)
            pool.wait_ge(pool_chain, 1)
            nc.gpsimd.affine_select(out=before[:], in_=before[:], compare_op=ALU.is_ge, fill=1.0, base=0,
                                    pattern=[[-1, P]], channel_multiplier=1).then_inc(consts, 1)

        @block.scalar
        def _(act):
            act.wait_ge(shift_done, 1)
            nc.scalar.activation(expd[:], shifted[:], ACT.Exp).then_inc(exp_done, 1)

        @block.tensor
        def _(pe):
            pe.wait_ge(consts, 5)
            pe.wait_ge(both_done, 1)
            rows = both[:].rearrange("p a e -> p (a e)")
            nc.tensor.matmul(rank_ps[:, 0:NT * E], before[:], rows, start=True, stop=True).then_inc(counted, 1)
            nc.tensor.matmul(total_ps[:, 0:NT * E], ones[:], rows, start=True, stop=True).then_inc(counted, 1)

        @block.vector
        def _(dve):
            n = [0]

            def link(ins):
                n[0] += 1
                ins.then_inc(chain, 1)
                dve.wait_ge(chain, n[0])

            V = nc.vector

            def per_tile(ap):
                return ap.unsqueeze(2).to_broadcast([P, NT, E])

            link(V.tensor_reduce(top1[:], logits[:], AX.X, ALU.max))
            V.tensor_tensor(shifted[:], logits[:], per_tile(top1[:]), ALU.subtract).then_inc(shift_done, 1)
            dve.wait_ge(exp_done, 1)
            link(V.tensor_reduce(denom[:, 0, :], expd[:], AX.X, ALU.add))
            link(V.reciprocal(denom[:, 1, :], denom[:, 0, :]))
            link(V.tensor_tensor(prob[:], expd[:], per_tile(denom[:, 1, :]), ALU.mult))
            for a in range(NT):
                last = V.max(best[:, a, :], prob[:, a, :])
            link(last)
            for a in range(NT):
                last = V.max_index(best_at[:, a, :], best[:, a, :], prob[:, a, :])
            link(last)
            link(V.tensor_copy(chosen[:], best_at[:, :, 0:TOPK]))
            dve.wait_ge(consts, 5)
            for j in range(TOPK):
                last = V.tensor_tensor(mask[:, j], iota_e[:].unsqueeze(1).to_broadcast([P, NT, E]),
                                       per_tile(chosen[:, :, j]), ALU.is_equal)
            link(last)
            V.tensor_tensor(both[:], mask[:, 0], mask[:, 1], ALU.add).then_inc(both_done, 1)
            link(V.tensor_tensor(pair_sum[:, 0, :], best[:, :, 0], best[:, :, 1], ALU.add))
            link(V.reciprocal(pair_sum[:, 1, :], pair_sum[:, 0, :]))
            for j in range(TOPK):
                V.tensor_tensor(keep["weight"][:, j, :], best[:, :, j], pair_sum[:, 1, :], ALU.mult)
            link(V.memset(prefix[:, 0, :], 0.0))
            dve.wait_ge(counted, 2)
            link(V.tensor_copy(total[:], total_ps[:, 0:NT * E].rearrange("p (a e) -> p a e", e=E)))
            for a in range(NT):
                link(V.tensor_tensor(prefix[:, a + 1, :], prefix[:, a, :], total[:, a, :], ALU.add))
            link(V.tensor_tensor(over[:], prefix[:, NT, :].unsqueeze(2).to_broadcast([P, E, NT]),
                                 iota_rows[:].unsqueeze(1).to_broadcast([P, E, NT]), ALU.is_gt))
            link(V.tensor_reduce(tiles[:], over[:], AX.X, ALU.add))
            link(V.tensor_copy(upto[:, 0:1], tiles[:, 0:1]))
            for e in range(1, E):
                link(V.tensor_tensor(upto[:, e:e + 1], upto[:, e - 1:e], tiles[:, e:e + 1], ALU.add))
            link(V.tensor_tensor(base[:], upto[:], tiles[:], ALU.subtract))
            link(V.scalar_tensor_tensor(place[:], base[:].unsqueeze(1).to_broadcast([P, NT, E]), float(P),
                                        prefix[:, 0:NT, :], ALU.mult, ALU.add))
            link(V.tensor_tensor(place[:], rank_ps[:, 0:NT * E].rearrange("p (a e) -> p a e", e=E), place[:], ALU.add))
            for j in range(TOPK):
                last = V.tensor_tensor(picked[:, j], mask[:, j], place[:], ALU.mult)
            link(last)
            link(V.tensor_reduce(slot_f[:].rearrange("p j a -> p (j a)"), picked[:].rearrange("p j a e -> p (j a) e"), AX.X, ALU.add))
            V.tensor_copy(keep["slot"][:], slot_f[:])
            link(V.tensor_tensor(passed[:], upto[0:1, :].unsqueeze(1).to_broadcast([1, SLOT_TILES, E]),
                                 iota_tile[:].unsqueeze(2).to_broadcast([1, SLOT_TILES, E]), ALU.is_le))
            link(V.tensor_reduce(owner[:, 0, :], passed[:], AX.X, ALU.add))
            link(V.tensor_scalar(owner[:, 1, :], owner[:, 0, :], float(E - 1), None, ALU.min))
            link(V.tensor_copy(keep["tile_expert"][:], owner[:, 1, :]))


def experts(nc, keep, scratch, x, w_proj, b_proj, w1_t, w2_t):
    ctx = ExitStack()
    with ctx:
        m = Memory(nc, ctx)
        o_t, tile_expert = keep["o_t"], keep["tile_expert"]
        w1 = m.sbuf("w1", [P, E, DK, 2 * I], F32)
        w2 = m.sbuf("w2", [P, E, len(I_TILES), D], F32)
        wp = m.sbuf("wp", [P, NG, D], F32)
        bp = m.sbuf("bp", [P, D], F32)
        ident = m.sbuf("ident3", [P, P], F32)
        res = m.sbuf("res", [P, 2, D], F32)
        rows = m.sbuf("rows", [P, 2, D], F32)
        rows_t = [m.sbuf(f"rows_t{r}", [P, D], F32) for r in range(2)]
        gated = m.sbuf("gated", [P, 2, I], F32)
        hidden = [m.sbuf(f"hidden{r}", [P, I], F32) for r in range(2)]
        hidden_t = [m.sbuf(f"hidden_t{r}", [P, len(I_TILES), P], F32) for r in range(2)]
        y = m.sbuf("y", [P, 2, D], F32)
        gu = [[m.psum(f"gu{r}{j}", [P, CH]) for j in range(2)] for r in range(2)]
        turn_ps, hid_ps = m.psum("turn_ps", [P, CH]), m.psum("hid_ps", [P, CH])
        down = [m.psum(f"down{r}", [P, CH]) for r in range(2)]

        ident_done, pool_chain = m.sem("ident3_done"), m.sem("pool_chain3")
        wp_in, bp_in, weights_in = m.sem("wp_in"), m.sem("bp_in"), m.sem("weights_in")
        res_in = [m.sem(f"res_in{r}") for r in range(2)]
        res_out = [m.sem(f"res_out{r}") for r in range(2)]
        biased, proj_full, res_done = m.sem("biased"), m.sem("proj_full"), m.sem("res_done")
        rows_in = [m.sem(f"rows_in{r}") for r in range(2)]
        y_out = [m.sem(f"y_out{r}") for r in range(2)]
        turned, turned_read = m.sem("rows_turned"), m.sem("rows_t_done")
        gu_full, silu_done, hidden_done = m.sem("gu_full"), m.sem("silu_done"), m.sem("hidden_done")
        hid_turned, hid_read = m.sem("hid_turned"), m.sem("hid_t_done")
        y_full, y_read = m.sem("y_full"), m.sem("y_read")
        WEIGHT_DMAS = 3 * E

        x_rows = x.rearrange("b (a p) d -> (b a) p d", p=P)
        res_rows = scratch["res"].rearrange("(a p) d -> a p d", p=P)
        in_rows = scratch["routed"].rearrange("(a p) d -> a p d", p=P)
        y_rows = scratch["y"].rearrange("(a p) d -> a p d", p=P)
        block = ctx.enter_context(nc.Block())

        def run_tiles(engine, tile):
            tile(0, 0, 0)
            tile(1, 1, 0)
            with engine.Fori(1, (SLOT_TILES - 1) // 2) as pairs:
                tile(pairs * 2, 0, pairs)
                tile(pairs * 2 + 1, 1, pairs)
            tile(SLOT_TILES - 1, 0, (SLOT_TILES - 1) // 2)

        def early(i):
            return isinstance(i, int) and i < 2

        @block.sync
        def _(sp):
            sp.dma_start(wp[:], w_proj.rearrange("(g p) d -> p g d", p=P)).then_inc(wp_in, 16)
            for a in range(NT + 1):
                if a < NT:
                    r = a % 2
                    if a >= 2:
                        sp.wait_ge(res_out[r], 16 * (a // 2))
                    sp.dma_start(res[:, r, :], x_rows[a]).then_inc(res_in[r], 16)
                if a >= 1:
                    sp.wait_ge(res_done, a)
                    sp.dma_start(res_rows[a - 1], res[:, (a - 1) % 2, :]).then_inc(res_out[(a - 1) % 2], 16)

            def tile(i, r, half):
                if not early(i):
                    sp.wait_ge(turned, i - 1)
                sp.dma_start(rows[:, r:r + 1, :], in_rows[bass.ds(i, 1)].rearrange("a p d -> p a d")).then_inc(rows_in[r], 16)

            run_tiles(sp, tile)
            for s in res_out:
                sp.wait_ge(s, 16 * NT // 2)

        @block.gpsimd
        def _(pool):
            nc.gpsimd.memset(ident[:], 0.0).then_inc(pool_chain, 1)
            pool.wait_ge(pool_chain, 1)
            nc.gpsimd.affine_select(out=ident[:], in_=ident[:], compare_op=ALU.not_equal, fill=1.0, base=0,
                                    pattern=[[-1, P]], channel_multiplier=1).then_inc(ident_done, 1)
            pool.wait_ge(bp_in, 16)
            for a in range(NT):
                pool.wait_ge(res_in[a % 2], 16 * (a // 2 + 1))
                nc.gpsimd.tensor_tensor(res[:, a % 2, :], res[:, a % 2, :], bp[:], ALU.add).then_inc(biased, 1)

            def tile(i, r, half):
                pool.wait_ge(y_read, i + 1)
                pool.dma_start(y_rows[bass.ds(i, 1)].rearrange("a p d -> p a d"), y[:, r:r + 1, :]).then_inc(y_out[r], 16)

            run_tiles(pool, tile)
            pool.wait_ge(y_out[0], 16 * ((SLOT_TILES + 1) // 2))
            pool.wait_ge(y_out[1], 16 * (SLOT_TILES // 2))

        @block.scalar
        def _(act):
            act.dma_start(bp[:], b_proj.partition_broadcast(P)).then_inc(bp_in, 16)
            for e in range(E):
                act.dma_start(w1[:, e], w1_t[e].rearrange("(k p) n -> p k n", p=P)).then_inc(weights_in, 16)
                act.dma_start(w2[:, e, 0:2, :], w2_t[e, 0:2 * P, :].rearrange("(k p) n -> p k n", p=P)).then_inc(weights_in, 16)
                act.dma_start(w2[0:I - 2 * P, e, 2, :], w2_t[e, 2 * P:I, :]).then_inc(weights_in, 16)

            def rows_to_sbuf(i, r):
                act.wait_ge(turned, i + 1)
                if not early(i):
                    act.wait_ge(gu_full, 2 * (i - 1))
                nc.scalar.copy(rows_t[r][:], turn_ps[:]).then_inc(turned_read, 1)

            def y_to_sbuf(i, r, half):
                act.wait_ge(y_full, i + 1)
                if not early(i):
                    act.wait_ge(y_out[r], half * 16)
                nc.scalar.copy(y[:, r, :], down[r][:]).then_inc(y_read, 1)

            def tile(i, r, half):
                act.wait_ge(gu_full, i * 2 + 1)
                if not early(i):
                    act.wait_ge(hidden_done, i - 1)
                nc.scalar.activation(gated[:, r, :], gu[r][0][:, 0:I], ACT.Silu).then_inc(silu_done, 1)
                if not (isinstance(i, int) and i == 0):
                    y_to_sbuf(i - 1, 1 - r, half - 1 if (r == 0) else half)
                if not (isinstance(i, int) and i == SLOT_TILES - 1):
                    rows_to_sbuf(i + 1, 1 - r)

            rows_to_sbuf(0, 0)
            run_tiles(act, tile)
            y_to_sbuf(SLOT_TILES - 1, 0, (SLOT_TILES - 1) // 2)

        @block.vector
        def _(dve):
            for a in range(NT):
                dve.wait_ge(proj_full, a + 1)
                dve.wait_ge(biased, a + 1)
                nc.vector.tensor_tensor(res[:, a % 2, :], gu[a % 2][0][:], res[:, a % 2, :], ALU.add).then_inc(res_done, 1)

            def hidden_to_sbuf(i, r):
                dve.wait_ge(hid_turned, i + 1)
                if not early(i):
                    dve.wait_ge(y_full, i - 1)
                nc.vector.tensor_copy(hidden_t[r][:, 0:2, :], hid_ps[:, 0:2 * P].rearrange("p (k t) -> p k t", t=P))
                nc.vector.tensor_copy(hidden_t[r][0:I - 2 * P, 2, :], hid_ps[0:I - 2 * P, 2 * P:3 * P]).then_inc(hid_read, 1)

            def tile(i, r, half):
                if not (isinstance(i, int) and i == 0):
                    hidden_to_sbuf(i - 1, 1 - r)
                dve.wait_ge(silu_done, i + 1)
                dve.wait_ge(gu_full, i * 2 + 2)
                if not early(i):
                    dve.wait_ge(hid_turned, i - 1)
                nc.vector.tensor_tensor(hidden[r][:], gu[r][1][:, 0:I], gated[:, r, :], ALU.mult).then_inc(hidden_done, 1)

            run_tiles(dve, tile)
            hidden_to_sbuf(SLOT_TILES - 1, 0)

        @block.tensor
        def _(pe):
            pe.wait_ge(wp_in, 16)
            for a in range(NT):
                if a >= 2:
                    pe.wait_ge(res_done, a - 1)
                for g in range(NG):
                    last = nc.tensor.matmul(gu[a % 2][0][:], o_t[:, g, a * P:(a + 1) * P], wp[:, g, :],
                                            start=(g == 0), stop=(g == NG - 1))
                last.then_inc(proj_full, 1)
            pe.wait_ge(ident_done, 1)
            pe.wait_ge(res_done, NT)

            def turn_rows(i, r, half):
                pe.wait_ge(rows_in[r], (half + 1) * 16)
                if not (isinstance(i, int) and i == 0):
                    pe.wait_ge(turned_read, i)
                for k in range(DK):
                    last = nc.tensor.transpose(turn_ps[:, k * P:(k + 1) * P], rows[:, r, k * P:(k + 1) * P], ident[:])
                last.then_inc(turned, 1)

            def up(i, r, e, j):
                for k in range(DK):
                    last = nc.tensor.matmul(gu[r][j][:, 0:I], rows_t[r][:, k * P:(k + 1) * P],
                                            w1[:, bass.ds(e, 1), k, j * I:(j + 1) * I].rearrange("p o n -> p (o n)"),
                                            start=(k == 0), stop=(k == DK - 1))
                last.then_inc(gu_full, 1)

            def turn_hidden(i, r):
                pe.wait_ge(hidden_done, i + 1)
                if not (isinstance(i, int) and i == 0):
                    pe.wait_ge(hid_read, i)
                for k, (at, n) in enumerate(I_TILES):
                    last = nc.tensor.transpose(hid_ps[0:n, k * P:(k + 1) * P], hidden[r][:, at:at + n], ident[:])
                last.then_inc(hid_turned, 1)

            def down_product(i, r, e):
                pe.wait_ge(hid_read, i + 1)
                if not early(i):
                    pe.wait_ge(y_read, i - 1)
                for k, (at, n) in enumerate(I_TILES):
                    last = nc.tensor.matmul(down[r][:], hidden_t[r][0:n, k, :],
                                            w2[0:n, bass.ds(e, 1), k, :].rearrange("p o n -> p (o n)"),
                                            start=(k == 0), stop=(k == len(I_TILES) - 1))
                last.then_inc(y_full, 1)

            def expert_of(i):
                return pe.value_load(tile_expert[0:1, bass.ds(i, 1)], min_val=0, max_val=E - 1)

            def tile(i, r, half):
                pe.wait_ge(turned_read, i + 1)
                if not early(i):
                    pe.wait_ge(hidden_done, i - 1)
                e = expert_of(i)
                up(i, r, e, 0)
                first = isinstance(i, int) and i == 0
                if not first:
                    turn_hidden(i - 1, 1 - r)
                up(i, r, e, 1)
                if not first:
                    down_product(i - 1, 1 - r, expert_of(i - 1))
                if not (isinstance(i, int) and i == SLOT_TILES - 1):
                    turn_rows(i + 1, 1 - r, half if r == 0 else half + 1)

            turn_rows(0, 0, 0)
            pe.wait_ge(weights_in, 16 * WEIGHT_DMAS)
            run_tiles(pe, tile)
            turn_hidden(SLOT_TILES - 1, 0)
            down_product(SLOT_TILES - 1, 0, expert_of(SLOT_TILES - 1))


def combine(nc, keep, scratch, out):
    RINGS = 4
    ctx = ExitStack()
    with ctx:
        m = Memory(nc, ctx)
        first = m.sbuf("first", [P, RINGS, D], F32)
        second = m.sbuf("second", [P, RINGS, D], F32)
        total = m.sbuf("total_out", [P, RINGS, D], F32)
        weight, slot = keep["weight"], keep["slot"]
        got = [[m.sem(f"got{j}{r}") for r in range(RINGS)] for j in range(TOPK)]
        res_in = [m.sem(f"res_back{r}") for r in range(RINGS)]
        stored = [m.sem(f"stored{r}") for r in range(RINGS)]
        one_added, both_added = m.sem("one_added"), m.sem("both_added")
        res_rows = scratch["res"].rearrange("(a p) d -> a p d", p=P)
        out_rows = out.rearrange("b (a p) d -> (b a) p d", p=P)
        block = ctx.enter_context(nc.Block())

        @block.gpsimd
        def _(pool):
            for a in range(NT):
                r = a % RINGS
                if a >= RINGS:
                    pool.wait_ge(both_added, a - RINGS + 1)
                for j, row in enumerate((first, second)):
                    pool.indirect_dma_start(out=row[:, r, :], out_offset=None, in_=scratch["y"],
                                            in_offset=bass.IndirectOffsetOnAxis(ap=slot[:, j, a:a + 1], axis=0)).then_inc(got[j][r], 16)

        @block.sync
        def _(sp):
            for a in range(NT + 2):
                if a < NT:
                    r = a % RINGS
                    if a >= RINGS:
                        sp.wait_ge(stored[r], 16 * (a // RINGS))
                    sp.dma_start(total[:, r, :], res_rows[a]).then_inc(res_in[r], 16)
                if a >= 2:
                    sp.wait_ge(both_added, a - 1)
                    sp.dma_start(out_rows[a - 2], total[:, (a - 2) % RINGS, :]).then_inc(stored[(a - 2) % RINGS], 16)
            for s in stored:
                sp.wait_ge(s, 16 * NT // RINGS)

        @block.vector
        def _(dve):
            for a in range(NT):
                r, nth = a % RINGS, 16 * (a // RINGS + 1)
                dve.wait_ge(res_in[r], nth)
                dve.wait_ge(got[0][r], nth)
                nc.vector.scalar_tensor_tensor(total[:, r, :], first[:, r, :], weight[:, 0, a:a + 1], total[:, r, :],
                                               ALU.mult, ALU.add).then_inc(one_added, 1)
                dve.wait_ge(got[1][r], nth)
                dve.wait_ge(one_added, a + 1)
                nc.vector.scalar_tensor_tensor(total[:, r, :], second[:, r, :], weight[:, 1, a:a + 1], total[:, r, :],
                                               ALU.mult, ALU.add).then_inc(both_added, 1)


def attend(nc, keep, scratch, extra=None):
    ROUNDS = B * NG
    TQ = S // P
    STACK = 3 * HD + 2
    steps = [(c, pair, j) for c in range(S // CH) for pair in range(HG // 2) for j in range((c + 1) * TPC)]
    NS = len(steps)
    units = [(h, i, c) for h in range(HG) for i in range(TQ) for c in range(i // TPC + 1)]
    NU = len(units)
    FIRST, PER = 5, 3
    USES = NU + 2
    TURN = FIRST + (NU + PER - 1) // PER
    ctx = ExitStack()
    with ctx:
        m = Memory(nc, ctx)
        q_st = [m.sbuf(f"q_stack{b}", [P, HG, S], F32R) for b in range(B)]
        k_st = [m.sbuf(f"k_stack{b}", [P, HG, S], F32R) for b in range(B)]
        v_st = [m.sbuf(f"v_ones{b}", [P, TQ, HG, 2 * HD], F32) for b in range(B)]
        PR = 3
        probs = m.sbuf("probs", [P, PR, 2, CH], F32)
        o_raw = m.sbuf("o_raw", [P, 2, CH], F32)
        sums = m.sbuf("sums", [P, 2, CH], F32)
        inv = m.sbuf("inv", [P, 2, CH], F32)
        mx = m.sbuf("mx", [P, HG, TQ], F32)
        mx_far = m.sbuf("mx_far", [P, HG, TQ - TPC], F32)
        row_hi = m.sbuf("row_hi", [HG * TQ, P], F32R)
        row_lo = m.sbuf("row_lo", [HG * TQ, P], F32R)
        ident = m.sbuf("ident2", [P, P], F32)
        ident16 = m.sbuf("ident16", [P, P], BF16)
        mask_m = m.sbuf("mask_m", [P, P], BF16)
        mask_t = m.sbuf("mask_t", [P, P], BF16)
        o_t = keep["o_t"]

        st = [[m.psum(f"scores_t{r}{h}", [P, CH]) for h in range(2)] for r in range(2)]
        ot = [m.psum(f"o_acc{r}", [P, CH]) for r in range(2)]
        mb = [m.psum(f"maxima{r}", [P, CH]) for r in range(2)]

        x_rows = m.sbuf("x_rows", [P, 2, D], F32)
        x_rows_in = [m.sem(f"x_rows_in{r}") for r in range(2)]
        scattered = [m.sem(f"scattered{r}") for r in range(2)]
        xn_rows = scratch["xn"].rearrange("(a p) d -> a p d", p=P)
        consts = m.sem("consts")
        minus_ones = m.sem("minus_ones")
        pool_chain = m.sem("pool_chain2")
        loaded = [m.sem(f"stack_in{b}") for b in range(B)]
        row_in = m.sem("row_in")
        m_full = m.sem("m_full")
        m_free = m.sem("m_free")
        mx_done = m.sem("mx_done")
        far_done = m.sem("far_done")
        row_hi_done = m.sem("row_hi_done")
        st_full = m.sem("st_full")
        exp_done = m.sem("exp_done")
        pv_done = m.sem("pv_done")
        ot_free = m.sem("ot_free")
        norm_done = m.sem("norm_done")
        inv_done = m.sem("inv_done")
        LOADS = 6 + TQ

        def stack_rows(name):
            return scratch[name].rearrange("(r h d) t -> r d h t", r=2, d=HD)

        v_rows = scratch["v"].rearrange("(a p) (h d) -> p a h d", p=P, d=HD)
        block = ctx.enter_context(nc.Block())

        @block.sync
        def _(sp):
            for s, n in ((m_free, 2), (exp_done, 4), (pv_done, 3), (ot_free, 2), (norm_done, 8)):
                sp.sem_inc(s, n)

            def load(g, b):
                heads, toks = bass.ds(g * HG, HG), slice(b * S, (b + 1) * S)
                for part, r, (hi0, hi1, lo) in ((q_st[b], 0, (0, 2, 1)), (k_st[b], 1, (0, 1, 2))):
                    for at, name in ((hi0, "qk_hi"), (lo, "qk_lo"), (hi1, "qk_hi")):
                        sp.dma_start(as_f32(part[at * HD:(at + 1) * HD, :, :]), stack_rows(name)[r, :, heads, toks]).then_inc(loaded[b], 16)
                for a in range(TQ):
                    sp.dma_start(v_st[b][:, a, :, 0:HD], v_rows[:, b * TQ + a, heads, :]).then_inc(loaded[b], 16)

            def rows(n, b):
                sp.wait_ge(m_free, n * USES + (USES + 2))
                for at, row in ((3 * HD, row_hi), (3 * HD + 1, row_lo)):
                    sp.dma_start(as_f32(q_st[b][at:at + 1, :, :].rearrange("o h (i t) -> o (h i) t", t=P)),
                                 as_f32(row[:])).then_inc(row_in, 16)

            load(0, 0)
            load(0, 1)
            rows(0, 0)
            with sp.Fori(0, NG - 1) as g:
                for b in range(B):
                    n = g * B + b
                    rows(n + 1, 1 - b)
                    sp.wait_ge(pv_done, n * NS + (NS + 3))
                    load(g + 1, b)
            rows(ROUNDS - 1, 1)

        @block.gpsimd
        def _(pool):
            nc.gpsimd.memset(ident[:], 0.0).then_inc(pool_chain, 1)
            nc.gpsimd.memset(ident16[:], 0.0).then_inc(pool_chain, 1)
            nc.gpsimd.memset(mask_m[:], 0.0).then_inc(pool_chain, 1)
            nc.gpsimd.memset(mask_t[:], 0.0).then_inc(pool_chain, 1)
            for b in range(B):
                nc.gpsimd.memset(v_st[b][:, :, :, HD:2 * HD], 1.0).then_inc(consts, 1)
            pool.wait_ge(pool_chain, 4)
            for t in (ident, ident16):
                nc.gpsimd.affine_select(out=t[:], in_=t[:], compare_op=ALU.not_equal, fill=1.0, base=0,
                                        pattern=[[-1, P]], channel_multiplier=1).then_inc(consts, 1)
            nc.gpsimd.affine_select(out=mask_m[:], in_=mask_m[:], compare_op=ALU.is_ge, fill=NEG, base=0,
                                    pattern=[[-1, P]], channel_multiplier=1).then_inc(consts, 1)
            nc.gpsimd.affine_select(out=mask_t[:], in_=mask_t[:], compare_op=ALU.is_ge, fill=NEG, base=0,
                                    pattern=[[1, P]], channel_multiplier=-1).then_inc(consts, 1)
            for a in range(NT):
                r = a % 2
                if a >= 2:
                    pool.wait_ge(scattered[r], 16 * TOPK * (a // 2))
                pool.dma_start(x_rows[:, r, :], xn_rows[a]).then_inc(x_rows_in[r], 16)
                pool.wait_ge(x_rows_in[r], 16 * (a // 2 + 1))
                for j in range(TOPK):
                    pool.indirect_dma_start(out=scratch["routed"], out_offset=bass.IndirectOffsetOnAxis(
                        ap=keep["slot"][:, j, a:a + 1], axis=0), in_=x_rows[:, r, :], in_offset=None).then_inc(scattered[r], 16)
            for s in scattered:
                pool.wait_ge(s, 16 * TOPK * NT // 2)

        @block.scalar
        def _(act):
            def row_high(n):
                act.wait_ge(m_full, n * (NU + 1) + (NU + 1))
                if not (isinstance(n, int) and n == 0):
                    act.wait_ge(row_in, n * 32)
                nc.scalar.copy(row_hi[:], mb[NU % 2][0:HG * TQ, 0:P]).then_inc(row_hi_done, 1)

            def round_(n, b, more):
                for k, (c, pair, j) in enumerate(steps):
                    w = min(CH, (c + 1) * CH - j * P)
                    r, slot = k % 2, k % PR
                    for h in range(2):
                        act.wait_ge(st_full, n * (2 * NS) + (2 * k + h + 1))
                        act.wait_ge(pv_done, n * NS + (k + 1))
                        nc.scalar.activation(probs[:, slot, h, 0:w], st[r][h][:, 0:w], ACT.Exp).then_inc(exp_done, 1)
                    for e, (ce, pe_, je) in enumerate(steps):
                        if je == (ce + 1) * TPC - 1 and (k == e + 1 or (k == e == NS - 1)):
                            o_out(n, ce, pe_, e)
                    if more and k == TURN:
                        row_high(n + 1)

            def o_out(n, c, pair, e):
                seg = 2 * c + pair
                act.wait_ge(pv_done, n * NS + (e + 4))
                act.wait_ge(norm_done, n * 8 + (4 * c + 4))
                for h in range(2):
                    at = (2 * pair + h) * HD
                    nc.scalar.copy(o_raw[at:at + HD, c, :], ot[seg % 2][2 * HD * h:2 * HD * h + HD, :])
                    last = nc.scalar.copy(sums[at:at + HD, c, :], ot[seg % 2][2 * HD * h + HD:2 * HD * (h + 1), :])
                last.then_inc(ot_free, 1)

            row_high(0)
            with act.Fori(0, NG - 1) as g:
                for b in range(B):
                    round_(g * B + b, b, True)
            round_(ROUNDS - 2, 0, True)
            round_(ROUNDS - 1, 1, False)

        @block.vector
        def _(dve):
            def unit(n, u):
                h, i, c = units[u]
                w = min(CH, (i + 1) * P - c * CH)
                dve.wait_ge(m_full, n * (NU + 1) + (u + 1))
                to = mx[:, h, i:i + 1] if c == 0 else mx_far[:, h, i - TPC:i - TPC + 1]
                nc.vector.tensor_reduce(to, mb[u % 2][:, 0:w], AX.X, ALU.max).then_inc(m_free, 1)

            def join(n):
                dve.wait_ge(m_free, n * USES + (NU + 2))
                nc.vector.tensor_tensor(mx[:, :, TPC:TQ], mx[:, :, TPC:TQ], mx_far[:], ALU.max).then_inc(mx_done, 1)

            def row_low(n):
                dve.wait_ge(row_hi_done, n + 1)
                if not (isinstance(n, int) and n == 0):
                    dve.wait_ge(row_in, n * 32)
                nc.vector.tensor_tensor(row_lo[:], mb[NU % 2][0:HG * TQ, 0:P], as_f32(row_hi[:]), ALU.subtract).then_inc(m_free, 2)

            def norm(n, g, b, c, q):
                cols = slice(q * P, (q + 1) * P)
                dve.wait_ge(ot_free, n * 4 + (2 * c + 2 + 2))
                dve.wait_ge(norm_done, n * 8 + (4 * c + q + 1))
                nc.vector.reciprocal(inv[:, c, cols], sums[:, c, cols]).then_inc(inv_done, 1)
                dve.wait_ge(inv_done, n * 8 + (4 * c + q + 1))
                nc.vector.scalar_tensor_tensor(o_t[:, bass.ds(g, 1), b * S + c * CH + q * P:b * S + c * CH + (q + 1) * P],
                                               o_raw[:, c:c + 1, cols], SCALE, inv[:, c:c + 1, cols], ALU.mult, ALU.mult).then_inc(norm_done, 1)

            def round_(n, g, b, more):
                for k in range(NS):
                    if more:
                        for u in range((k - FIRST) * PER, (k - FIRST + 1) * PER):
                            if 0 <= u < NU:
                                unit(n + 1, u)
                        if k == TURN - 1:
                            join(n + 1)
                    if 9 <= k < 13:
                        norm(n, g, b, 0, k - 9)
                if more:
                    row_low(n + 1)
                for q in range(4):
                    norm(n, g, b, 1, q)

            for b in range(B):
                nc.vector.memset(as_f32(k_st[b][3 * HD:STACK, :, :]), -1.0).then_inc(minus_ones, 1)
            for u in range(NU):
                unit(0, u)
            join(0)
            row_low(0)
            with dve.Fori(0, NG - 1) as g:
                for b in range(B):
                    round_(g * B + b, g, b, True)
            round_(ROUNDS - 2, NG - 1, 0, True)
            round_(ROUNDS - 1, NG - 1, 1, False)

        @block.tensor
        def _(pe):
            def unit(n, b, u):
                h, i, c = units[u]
                w = min(CH, (i + 1) * P - c * CH)
                diag = i // TPC == c
                pe.wait_ge(m_free, n * USES + max(u + 1, 2))
                out = mb[u % 2]
                last = nc.tensor.matmul(out[:, 0:w], q_st[b][0:3 * HD, h, i * P:(i + 1) * P],
                                        k_st[b][0:3 * HD, h, c * CH:c * CH + w], start=True, stop=not diag)
                if diag:
                    last = nc.tensor.matmul(out[:, w - P:w], ident16[:], mask_m[:], start=False, stop=True)
                last.then_inc(m_full, 1)

            def turn(n):
                pe.wait_ge(mx_done, n + 1)
                pe.wait_ge(m_free, n * USES + (NU + 1))
                nc.tensor.transpose(mb[NU % 2][0:HG * TQ, 0:P], mx[:].rearrange("p h i -> p (h i)"), ident[:]).then_inc(m_full, 1)

            def scores(n, b, k):
                c, pair, j = steps[k]
                t0 = max(c * CH, j * P)
                w = (c + 1) * CH - t0
                diag = j >= c * TPC
                pe.wait_ge(exp_done, n * (2 * NS) + (2 * k + 2))
                for h in range(2):
                    out = st[k % 2][h]
                    head = 2 * pair + h
                    last = nc.tensor.matmul(out[:, 0:w], k_st[b][0:STACK, head, j * P:(j + 1) * P],
                                            q_st[b][0:STACK, head, t0:t0 + w], start=True, stop=not diag)
                    if diag:
                        last = nc.tensor.matmul(out[:, 0:P], ident16[:], mask_t[:], start=False, stop=True)
                    last.then_inc(st_full, 1)

            def values(n, b, k):
                c, pair, j = steps[k]
                w = min(CH, (c + 1) * CH - j * P)
                seg = 2 * c + pair
                if j == 0:
                    pe.wait_ge(ot_free, n * 4 + (seg + 1))
                pe.wait_ge(exp_done, n * (2 * NS) + (2 * k + 2 + 4))
                for h in range(2):
                    last = nc.tensor.matmul(ot[seg % 2][2 * HD * h:2 * HD * (h + 1), CH - w:CH], v_st[b][:, j, 2 * pair + h, :],
                                            probs[:, k % PR, h, 0:w], start=(j == 0), stop=(j == (c + 1) * TPC - 1))
                last.then_inc(pv_done, 1)

            def round_(n, g, b, more):
                pe.wait_ge(row_in, n * 32 + 32)
                scores(n, b, 0)
                for k in range(NS):
                    if k + 1 < NS:
                        scores(n, b, k + 1)
                    if more:
                        if k == FIRST:
                            pe.wait_ge(loaded[1 - b], (g + b + 1) * 16 * LOADS)
                        for u in range((k - FIRST) * PER, (k - FIRST + 1) * PER):
                            if 0 <= u < NU:
                                unit(n + 1, 1 - b, u)
                        if k == TURN:
                            turn(n + 1)
                    values(n, b, k)

            pe.wait_ge(consts, 6)
            pe.wait_ge(minus_ones, 2)
            pe.wait_ge(loaded[0], 16 * LOADS)
            for u in range(NU):
                unit(0, 0, u)
            turn(0)
            with pe.Fori(0, NG - 1) as g:
                for b in range(B):
                    round_(g * B + b, g, b, True)
            round_(ROUNDS - 2, NG - 1, 0, True)
            round_(ROUNDS - 1, NG - 1, 1, False)


def attention_and_experts(nc, x, w_attn, bias_qk, bias_qk_pair, bias_v, w_proj, b_proj, gate_t, w1_t, w2_t,
                          rope_cos, rope_sin, rope_cos_col, rope_sin_col, out):
    scratch = {
        "qk_hi": nc.dram_tensor("qk_hi", [2 * D, T], F32).ap(),
        "qk_lo": nc.dram_tensor("qk_lo", [2 * D, T], F32).ap(),
        "v": nc.dram_tensor("v_all", [T, D], F32).ap(),
        "routed": nc.dram_tensor("routed", [SLOT_TILES * P, D], F32).ap(),
        "y": nc.dram_tensor("y_all", [SLOT_TILES * P, D], F32).ap(),
        "res": nc.dram_tensor("res_all", [T, D], F32).ap(),
        "xn": nc.dram_tensor("xn_all", [T, D], F32).ap(),
    }
    ctx = ExitStack()
    with ctx:
        m = Memory(nc, ctx)
        keep = {"logits": m.sbuf("logits", [P, NT, E], F32)}
        project_qkv(nc, keep, scratch, x, w_attn, bias_qk, bias_qk_pair, bias_v, gate_t, rope_cos, rope_sin,
                    rope_cos_col, rope_sin_col)
        keep["slot"] = m.sbuf("slot", [P, TOPK, NT], U32)
        keep["weight"] = m.sbuf("weight", [P, TOPK, NT], F32)
        keep["tile_expert"] = m.sbuf("tile_expert", [1, SLOT_TILES], I32)
        keep["o_t"] = m.sbuf("o_t", [P, NG, T], F32)
        route(nc, keep, scratch)
        attend(nc, keep, scratch)
        experts(nc, keep, scratch, x, w_proj, b_proj, w1_t, w2_t)
        combine(nc, keep, scratch, out)


def kernel(L0_attn_x, L0_attn_w_attn, L0_attn_b_attn, L0_attn_w_proj, L0_attn_b_proj, L0_ffn_gate_w, L0_ffn_w1, L0_ffn_w2):
    import numpy as np
    import concourse.bacc as bacc
    from concourse.bass_utils import run_bass_kernel_spmd

    half = HD // 2
    freqs = np.float32(10000.0) ** (-(np.arange(0, HD, 2, dtype=np.float32) / np.float32(HD)))
    angle = np.outer(np.arange(H, dtype=np.float32), freqs).astype(np.float32)
    cos = np.repeat(np.cos(angle).reshape(-1), 2).astype(np.float32)
    sin = (np.repeat(np.sin(angle).reshape(-1), 2) * np.tile([-1.0, 1.0], H * half)).astype(np.float32)

    def columns(v):
        return v.reshape(QK_TILES, P).T

    b = np.asarray(L0_attn_b_attn)
    b_qk = b[:2 * D]
    pair = b_qk.reshape(-1, 2)[:, ::-1].reshape(-1)
    laid_out = {
        "x": L0_attn_x, "w_attn": L0_attn_w_attn, "bias_qk": columns(b_qk), "bias_qk_pair": columns(pair),
        "bias_v": b[2 * D:], "w_proj": L0_attn_w_proj, "b_proj": L0_attn_b_proj,
        "gate_t": np.asarray(L0_ffn_gate_w).T, "w1_t": np.asarray(L0_ffn_w1).transpose(0, 2, 1),
        "w2_t": np.asarray(L0_ffn_w2).transpose(0, 2, 1), "rope_cos": cos, "rope_sin": sin,
        "rope_cos_col": columns(np.tile(cos, 2)), "rope_sin_col": columns(np.tile(sin, 2)),
    }
    nc = bacc.Bacc("TRN2", target_bir_lowering=False, num_devices=1)
    arrays, args = {}, []
    for name, value in laid_out.items():
        a = np.ascontiguousarray(value)
        arrays[f"in_{name}"] = a
        args.append(nc.dram_tensor(f"in_{name}", a.shape, mybir.dt.from_np(a.dtype), kind="ExternalInput").ap())
    args.append(nc.dram_tensor("out_0", (B, S, D), F32, kind="ExternalOutput").ap())
    attention_and_experts(nc, *args)
    r = run_bass_kernel_spmd(nc, [arrays], core_ids=[0])
    return r.results[0]["out_0"]
```

```python
import concourse.bass as bass
from concourse import mybir
from contextlib import ExitStack

F32 = mybir.dt.float32
F32R = mybir.dt.float32r
BF16 = mybir.dt.bfloat16
U32 = mybir.dt.uint32
I32 = mybir.dt.int32
ALU = mybir.AluOpType
ACT = mybir.ActivationFunctionType
AX = mybir.AxisListType

P = 128
B, S, D = 2, 1024, 512
T = B * S
H, HD = 16, 32
DK = D // P
CH = 512
NCH = T // CH
TPC = CH // P
NT = T // P
E, I, TOPK = 8, 352, 2
HG = P // HD
NG = H // HG
QK_TILES = 2 * NG
EPS = 1e-5
SCALE = float(D) ** -0.5
NEG = -3.0e38
SLOT_TILES = T * TOPK // P + E - 1
I_TILES = [(0, 128), (128, 128), (256, 96)]


def as_f32(ap):
    return ap.bitcast(F32)


class Memory:

    def __init__(self, nc, ctx):
        self.nc, self.ctx = nc, ctx

    def sbuf(self, name, shape, dtype):
        return self.ctx.enter_context(self.nc.sbuf_tensor(name, shape, dtype))

    def psum(self, name, shape, dtype=F32):
        return self.ctx.enter_context(self.nc.psum_tensor(name, shape, dtype))

    def sem(self, name):
        return self.ctx.enter_context(self.nc.semaphore(name))


def project_qkv(nc, keep, scratch, x, w_attn, bias_qk, bias_qk_pair, bias_v, gate_t, rope_cos, rope_sin,
                rope_cos_col, rope_sin_col):
    ctx = ExitStack()
    with ctx:
        m = Memory(nc, ctx)
        w_raw = m.sbuf("w_raw", [P, DK, 3 * D], F32)
        w_hi = m.sbuf("w_hi", [P, DK, 3 * D], F32R)
        w_lo = m.sbuf("w_lo", [P, DK, 3 * D], F32R)
        cos_row = m.sbuf("cos_row", [P, D], F32)
        sin_row = m.sbuf("sin_row", [P, D], F32)
        turned = m.sbuf("turned", [P, DK, D], F32)
        gate_raw = m.sbuf("gate_raw", [P, DK, E], F32)
        gate_hi = m.sbuf("gate_hi", [P, DK, E], F32R)
        gate_lo = m.sbuf("gate_lo", [P, DK, E], F32R)
        small = m.sbuf("small", [P, 8, QK_TILES], F32)
        bias_col, bias_pair, cos_col, sin_col, bias_rot, bias_tmp = (small[:, i, :] for i in range(6))
        bias_v_row = m.sbuf("bias_v_row", [P, D], F32)
        stats = m.sbuf("stats", [P, NT, 6], F32)
        mean_var = m.sbuf("mean_var", [P, NT, 2], F32)
        zeros = m.sbuf("zeros", [P, D], F32)
        eps = m.sbuf("eps", [P, 1], F32)
        root = m.sbuf("root", [P, NT], F32)
        newton = m.sbuf("newton", [P, NT], F32)
        rstd = m.sbuf("rstd", [P, NT], F32)
        shift = m.sbuf("shift", [P, TPC], F32)
        xt_hi = m.sbuf("xt_hi", [P, DK, CH], F32R)
        xt_lo = m.sbuf("xt_lo", [P, DK, CH], F32R)
        logits_t = m.sbuf("logits_t", [P, CH], F32)
        STG = 4
        st_hi = m.sbuf("st_hi", [P, STG, CH], F32R)
        st_lo = m.sbuf("st_lo", [P, STG, CH], F32R)
        st_v = m.sbuf("st_v", [P, TPC, D], F32)
        x_raw = keep["x_rows"]
        xn = m.sbuf("xn", [P, TPC, D], F32)
        ident, logits = m.sbuf("ident", [P, P], F32), keep["logits"]

        RING = 6
        banks = [m.psum(f"bank{i}", [P, CH]) for i in range(RING)]
        USES = DK + 1 + TPC + QK_TILES + 1
        U_GATE, U_V, U_QK, U_LT = DK, DK + 1, DK + 1 + TPC, DK + 1 + TPC + QK_TILES

        x_in = [m.sem(f"x_in{c}") for c in range(NCH)]
        w_in = [m.sem(f"w_in{i}") for i in range(3)]
        rope_in = m.sem("rope_in")
        small_in = m.sem("small_in")
        gate_in = m.sem("gate_in")
        chain = m.sem("dve_chain")
        stats_done = m.sem("stats_done")
        zeros_done = m.sem("zeros_done")
        cleared = m.sem("cleared")
        eps_done = m.sem("eps_done")
        root_done = m.sem("root_done")
        rstd_done = m.sem("rstd_done")
        shift_done = m.sem("shift_done")
        xn_done = m.sem("xn_done")
        pool_chain = m.sem("pool_chain")
        ident_done = m.sem("ident_done")
        whi_done = m.sem("whi_done")
        wlo_done = m.sem("wlo_done")
        wqk_done = m.sem("wqk_done")
        bias_done = m.sem("bias_done")
        bank_full = m.sem("bank_full")
        hi_done = m.sem("hi_done")
        bank_free = m.sem("bank_free")
        xn_stored = m.sem("xn_stored")
        st_free = [m.sem(f"st_free{i}") for i in range(STG)]
        v_free = [m.sem(f"v_free{a}") for a in range(TPC)]
        st_ready = m.sem("st_ready")
        v_ready = m.sem("v_ready")

        w_view = w_attn.rearrange("(k p) n -> p k n", p=P)
        x_view = x.rearrange("b (c a p) d -> (b c) p a d", p=P, a=TPC)
        qk_hi_view = scratch["qk_hi"].rearrange("(m p) t -> m p t", p=P)
        qk_lo_view = scratch["qk_lo"].rearrange("(m p) t -> m p t", p=P)
        v_view = scratch["v"].rearrange("(a p) d -> p a d", p=P)
        parts = [(2 * D, 3 * D), (0, D), (D, 2 * D)]
        block = ctx.enter_context(nc.Block())

        @block.sync
        def _(sp):
            sp.sem_inc(bank_free, 1)
            for s in st_free:
                sp.sem_inc(s, 32)
            for s in v_free:
                sp.sem_inc(s, 16)
            for c in range(NCH):
                sp.dma_start(x_raw[:, c * TPC:(c + 1) * TPC, :], x_view[c]).then_inc(x_in[c], 16)
            with sp.Fori(0, NCH) as c:
                sp.wait_ge(xn_done, (c + 1) * TPC)
                sp.dma_start(x_raw[:, bass.ds(c * TPC, TPC), :], xn[:]).then_inc(xn_stored, 16)
                for a in range(TPC):
                    sp.wait_ge(v_ready, c * TPC + (a + 1))
                    sp.dma_start(v_view[:, bass.ds(c * TPC + a, 1), :], st_v[:, a:a + 1, :]).then_inc(v_free[a], 16)
                for i in range(QK_TILES):
                    sp.wait_ge(st_ready, c * QK_TILES + (i + 1))
                    sp.dma_start(qk_hi_view[i, :, bass.ds(c * CH, CH)], as_f32(st_hi[:, i % STG, :])).then_inc(st_free[i % STG], 16)
                    sp.dma_start(qk_lo_view[i, :, bass.ds(c * CH, CH)], as_f32(st_lo[:, i % STG, :])).then_inc(st_free[i % STG], 16)
            for s in st_free:
                sp.wait_ge(s, 32 + 32 * NCH * QK_TILES // STG)
            for s in v_free:
                sp.wait_ge(s, 16 + 16 * NCH)
            sp.wait_ge(cleared, 16)
            sp.wait_ge(xn_stored, 16 * NCH)

        @block.gpsimd
        def _(pool):
            nc.gpsimd.memset(ident[:], 0.0).then_inc(pool_chain, 1)
            pool.wait_ge(pool_chain, 1)
            nc.gpsimd.affine_select(out=ident[:], in_=ident[:], compare_op=ALU.not_equal, fill=1.0, base=0,
                                    pattern=[[-1, P]], channel_multiplier=1).then_inc(ident_done, 1)
            done = 1
            pool.wait_ge(rope_in, 32)
            sign = sin_row[:].rearrange("p (n two) -> p n two", two=2)
            t = turned[:].rearrange("p k (n two) -> p k n two", two=2)
            for i, (lo, hi) in enumerate(parts[1:]):
                w = w_raw[:, :, lo:hi]
                pair = w.rearrange("p k (n two) -> p k n two", two=2)
                pool.wait_ge(w_in[1 + i], 16)
                if i:
                    pool.wait_ge(wqk_done, i)
                for k in range(DK):
                    for j in range(2):
                        last = nc.gpsimd.tensor_tensor(t[:, k, :, j], pair[:, k, :, 1 - j], sign[:, :, j], ALU.mult)
                last.then_inc(pool_chain, 1)
                done += 1
                pool.wait_ge(pool_chain, done)
                for k in range(DK):
                    last = nc.gpsimd.tensor_tensor(w[:, k, :], w[:, k, :], cos_row[:], ALU.mult)
                last.then_inc(pool_chain, 1)
                done += 1
                pool.wait_ge(pool_chain, done)
                nc.gpsimd.tensor_tensor(w, w, turned[:], ALU.add).then_inc(pool_chain, 1)
                done += 1
                pool.wait_ge(pool_chain, done)
                nc.gpsimd.tensor_copy(w_hi[:, :, lo:hi], w).then_inc(pool_chain, 1)
                done += 1
                pool.wait_ge(pool_chain, done)
                nc.gpsimd.tensor_tensor(w_lo[:, :, lo:hi], w, as_f32(w_hi[:, :, lo:hi]), ALU.subtract).then_inc(wqk_done, 1)
            for c in range(1, NCH):
                pool.wait_ge(rstd_done, 2)
                pool.wait_ge(bank_full, (c - 1) * USES + DK)
                pool.wait_ge(xn_stored, c * 16)
                for a in range(TPC):
                    t = c * TPC + a
                    nc.gpsimd.tensor_scalar(xn[:, a, :], x_raw[:, t, :], mean_var[:, t, 0:1], rstd[:, t:t + 1],
                                            ALU.subtract, ALU.mult).then_inc(xn_done, 1)

        @block.scalar
        def _(act):
            act.dma_start(small[:, 0, :], bias_qk).then_inc(small_in, 16)
            act.dma_start(small[:, 1, :], bias_qk_pair).then_inc(small_in, 16)
            act.dma_start(small[:, 2, :], rope_cos_col).then_inc(small_in, 16)
            act.dma_start(small[:, 3, :], rope_sin_col).then_inc(small_in, 16)
            act.dma_start(bias_v_row[:], bias_v.partition_broadcast(P)).then_inc(small_in, 16)
            act.dma_start(gate_raw[:], gate_t.rearrange("(k p) e -> p k e", p=P)).then_inc(gate_in, 16)
            act.dma_start(cos_row[:], rope_cos.partition_broadcast(P)).then_inc(rope_in, 16)
            act.dma_start(sin_row[:], rope_sin.partition_broadcast(P)).then_inc(rope_in, 16)
            for i in (1, 0, 2):
                lo, hi = parts[i]
                act.dma_start(w_raw[:, :, lo:hi], w_view[:, :, lo:hi]).then_inc(w_in[i], 16)
            act.wait_ge(zeros_done, 1)
            act.dma_start(scratch["routed"].rearrange("(i p) d -> p i d", p=P),
                          zeros[:].unsqueeze(1).to_broadcast([P, SLOT_TILES, D])).then_inc(cleared, 16)
            act.wait_ge(gate_in, 16)
            nc.scalar.copy(gate_hi[:], gate_raw[:]).then_inc(whi_done, 1)
            act.wait_ge(stats_done, 1)
            act.wait_ge(eps_done, 1)
            nc.scalar.activation(root[:, 0:TPC], mean_var[:, 0:TPC, 1], ACT.Sqrt, bias=eps[:]).then_inc(root_done, 1)
            act.wait_ge(shift_done, 1)
            for a in range(TPC):
                nc.scalar.activation(xn[:, a, :], x_raw[:, a, :], ACT.Identity, bias=shift[:, a:a + 1],
                                     scale=rstd[:, a:a + 1]).then_inc(xn_done, 1)
            act.wait_ge(stats_done, NCH)
            nc.scalar.activation(root[:, TPC:NT], mean_var[:, TPC:NT, 1], ACT.Sqrt, bias=eps[:]).then_inc(root_done, 1)
            act.wait_ge(w_in[0], 16)
            nc.scalar.copy(w_hi[:, :, 2 * D:3 * D], w_raw[:, :, 2 * D:3 * D]).then_inc(whi_done, 1)
            act.wait_ge(bias_done, 1)
            with act.Fori(0, NCH) as c:
                for k in range(DK):
                    act.wait_ge(bank_full, c * USES + (k + 1))
                    nc.scalar.copy(xt_hi[:, k, :], banks[k % RING][:]).then_inc(hi_done, 1)
                for i in range(QK_TILES):
                    u = U_QK + i
                    act.wait_ge(bank_full, c * USES + (u + 1))
                    act.wait_ge(st_free[i % STG], (c * (QK_TILES // STG) + (i // STG + 1)) * 32)
                    nc.scalar.activation(st_hi[:, i % STG, :], banks[u % RING][:], ACT.Identity,
                                         bias=bias_rot[:, i:i + 1]).then_inc(hi_done, 1)

        @block.vector
        def _(dve):
            n = [0]

            def link(ins):
                n[0] += 1
                ins.then_inc(chain, 1)
                dve.wait_ge(chain, n[0])

            def invert(lo, hi, number):
                r, v, t = rstd[:, lo:hi], mean_var[:, lo:hi, 1], newton[:, lo:hi]
                dve.wait_ge(root_done, number)
                link(nc.vector.reciprocal(r, root[:, lo:hi]))
                link(nc.vector.tensor_tensor(t, r, r, ALU.mult))
                link(nc.vector.scalar_tensor_tensor(t, v, EPS, t, ALU.add, ALU.mult))
                link(nc.vector.tensor_scalar(t, t, -0.5, 1.5, ALU.mult, ALU.add))
                nc.vector.tensor_tensor(r, r, t, ALU.mult).then_inc(rstd_done, 1)
                dve.wait_ge(rstd_done, number)

            nc.vector.memset(zeros[:], 0.0).then_inc(zeros_done, 1)
            link(nc.vector.memset(logits_t[:], 0.0))
            nc.vector.memset(eps[:], EPS).then_inc(eps_done, 1)
            for c in range(NCH):
                dve.wait_ge(x_in[c], 16)
                for a in range(TPC):
                    last = nc.vector.bn_stats(stats[:, c * TPC + a, :], x_raw[:, c * TPC + a, :])
                link(last)
                for a in range(TPC):
                    last = nc.vector.bn_aggr(mean_var[:, c * TPC + a, :], stats[:, c * TPC + a, :])
                last.then_inc(stats_done, 1)
                if c == 0:
                    invert(0, TPC, 1)
                    nc.vector.scalar_tensor_tensor(shift[:], mean_var[:, 0:TPC, 0], -1.0, rstd[:, 0:TPC],
                                                   ALU.mult, ALU.mult).then_inc(shift_done, 1)
            invert(TPC, NT, 2)
            dve.wait_ge(whi_done, 1)
            nc.vector.tensor_tensor(gate_lo[:], gate_raw[:], as_f32(gate_hi[:]), ALU.subtract).then_inc(wlo_done, 1)
            dve.wait_ge(whi_done, 2)
            nc.vector.tensor_tensor(w_lo[:, :, 2 * D:3 * D], w_raw[:, :, 2 * D:3 * D], as_f32(w_hi[:, :, 2 * D:3 * D]),
                                    ALU.subtract).then_inc(wlo_done, 1)
            dve.wait_ge(small_in, 80)
            link(nc.vector.tensor_tensor(bias_tmp, bias_pair, sin_col, ALU.mult))
            link(nc.vector.tensor_tensor(bias_rot, bias_col, cos_col, ALU.mult))
            nc.vector.tensor_tensor(bias_rot, bias_rot, bias_tmp, ALU.add).then_inc(bias_done, 1)
            dve.wait_ge(bias_done, 1)
            with dve.Fori(0, NCH) as c:
                HI = DK + QK_TILES
                for k in range(DK):
                    dve.wait_ge(hi_done, c * HI + (k + 1))
                    nc.vector.tensor_tensor(xt_lo[:, k, :], banks[k % RING][:], as_f32(xt_hi[:, k, :]),
                                            ALU.subtract).then_inc(bank_free, 1)
                u = U_GATE
                dve.wait_ge(bank_full, c * USES + (u + 1))
                nc.vector.tensor_copy(logits_t[0:E, :], banks[u % RING][0:E, :]).then_inc(bank_free, 1)
                for a in range(TPC):
                    u = U_V + a
                    dve.wait_ge(bank_full, c * USES + (u + 1))
                    dve.wait_ge(v_free[a], (c + 1) * 16)
                    nc.vector.tensor_tensor(st_v[:, a, :], banks[u % RING][:], bias_v_row[:], ALU.add).then_inc(v_ready, 1)
                for i in range(QK_TILES):
                    u = U_QK + i
                    dve.wait_ge(hi_done, c * HI + (DK + i + 1))
                    nc.vector.scalar_tensor_tensor(st_lo[:, i % STG, :], banks[u % RING][:], bias_rot[:, i:i + 1],
                                                   as_f32(st_hi[:, i % STG, :]), ALU.add, ALU.subtract).then_inc(st_ready, 1)
                u = U_LT
                dve.wait_ge(bank_full, c * USES + (u + 1))
                nc.vector.tensor_copy(logits[:, bass.ds(c * TPC, TPC), :],
                                      banks[u % RING][:].rearrange("p (a q) -> p a q", q=P)[:, :, 0:E]).then_inc(bank_free, 1)

        @block.tensor
        def _(pe):
            reads = ([(bank_free, DK + 2, k + 1) for k in range(DK)] + [(bank_free, DK + 2, DK + 1)]
                     + [(v_ready, TPC, a + 1) for a in range(TPC)]
                     + [(st_ready, QK_TILES, i + 1) for i in range(QK_TILES)] + [(bank_free, DK + 2, DK + 2)])

            def claim(c, u):
                if u >= RING:
                    sem, per, number = reads[u - RING]
                    pe.wait_ge(sem, c * per + number + (sem is bank_free))
                else:
                    pe.wait_ge(bank_free, c * (DK + 2) + 1)

            def split_product(out, a_hi, a_lo, b_hi, b_lo):
                for k in range(DK):
                    nc.tensor.matmul(out, a_hi(k), b_hi(k), start=(k == 0), stop=False)
                    nc.tensor.matmul(out, a_hi(k), b_lo(k), start=False, stop=False)
                    last = nc.tensor.matmul(out, a_lo(k), b_hi(k), start=False, stop=(k == DK - 1))
                return last

            pe.wait_ge(ident_done, 1)
            pe.wait_ge(wlo_done, 2)
            with pe.Fori(0, NCH) as c:
                pe.wait_ge(xn_done, (c + 1) * TPC)
                for k in range(DK):
                    claim(c, k)
                    for a in range(TPC):
                        last = nc.tensor.transpose(banks[k % RING][:, a * P:(a + 1) * P], xn[:, a, k * P:(k + 1) * P], ident[:])
                    last.then_inc(bank_full, 1)
                pe.wait_ge(bank_free, c * (DK + 2) + DK + 1)
                u = U_GATE
                claim(c, u)
                split_product(banks[u % RING][0:E, :], lambda k: gate_hi[:, k, :], lambda k: gate_lo[:, k, :],
                              lambda k: xt_hi[:, k, :], lambda k: xt_lo[:, k, :]).then_inc(bank_full, 1)
                for a in range(TPC):
                    u = U_V + a
                    claim(c, u)
                    split_product(banks[u % RING][:], lambda k: xt_hi[:, k, a * P:(a + 1) * P],
                                  lambda k: xt_lo[:, k, a * P:(a + 1) * P], lambda k: w_hi[:, k, 2 * D:3 * D],
                                  lambda k: w_lo[:, k, 2 * D:3 * D]).then_inc(bank_full, 1)
                for i in range(QK_TILES):
                    u = U_QK + i
                    if i % NG == 0:
                        pe.wait_ge(wqk_done, i // NG + 1)
                    claim(c, u)
                    split_product(banks[u % RING][:], lambda k: w_hi[:, k, i * P:(i + 1) * P],
                                  lambda k: w_lo[:, k, i * P:(i + 1) * P], lambda k: xt_hi[:, k, :],
                                  lambda k: xt_lo[:, k, :]).then_inc(bank_full, 1)
                u = U_LT
                claim(c, u)
                pe.wait_ge(bank_free, c * (DK + 2) + DK + 2)
                for a in range(TPC):
                    last = nc.tensor.transpose(banks[u % RING][:, a * P:(a + 1) * P], logits_t[:, a * P:(a + 1) * P], ident[:])
                last.then_inc(bank_full, 1)


def route(nc, m, keep, count_banks):
    rank_ps, total_ps = count_banks
    logits = keep["logits"]
    iota_e = m.sbuf("iota_e", [P, E], F32)
    iota_rows = m.sbuf("iota_rows", [P, NT], F32)
    iota_tile = m.sbuf("iota_tile", [1, SLOT_TILES], F32)
    before = m.sbuf("before", [P, P], BF16)
    ones = m.sbuf("ones16", [P, P], BF16)
    top1 = m.sbuf("top1", [P, NT], F32)
    shifted = m.sbuf("shifted", [P, NT, E], F32)
    expd = m.sbuf("expd", [P, NT, E], F32)
    denom = m.sbuf("denom", [P, 2, NT], F32)
    prob = m.sbuf("prob", [P, NT, E], F32)
    best = m.sbuf("best", [P, NT, 8], F32)
    best_at = m.sbuf("best_at", [P, NT, 8], U32)
    chosen = m.sbuf("chosen", [P, NT, TOPK], F32)
    mask = m.sbuf("mask", [P, TOPK, NT, E], F32)
    both = m.sbuf("both", [P, NT, E], BF16)
    total = m.sbuf("total", [P, NT, E], F32)
    prefix = m.sbuf("prefix", [P, NT + 1, E], F32)
    over = m.sbuf("over", [P, E, NT], F32)
    tiles = m.sbuf("tiles", [P, E], F32)
    upto = m.sbuf("upto", [P, E], F32)
    base = m.sbuf("base", [P, E], F32)
    place = m.sbuf("place", [P, NT, E], F32)
    picked = m.sbuf("picked", [P, TOPK, NT, E], F32)
    slot_f = m.sbuf("slot_f", [P, TOPK, NT], F32)
    pair_sum = m.sbuf("pair_sum", [P, 2, NT], F32)
    passed = m.sbuf("passed", [1, SLOT_TILES, E], F32)
    owner = m.sbuf("owner", [1, 2, SLOT_TILES], F32)
    consts, pool_chain = m.sem("consts_r"), m.sem("pool_chain_r")
    chain, shift_done, exp_done = m.sem("chain_r"), m.sem("shift_done_r"), m.sem("exp_done_r")
    both_done, counted = m.sem("both_done"), m.sem("counted")
    route_done = m.sem("route_done")

    def pool_part(pool):
        nc.gpsimd.iota(iota_e[:], pattern=[[1, E]], base=0, channel_multiplier=0,
                       allow_small_or_imprecise_dtypes=True).then_inc(consts, 1)
        nc.gpsimd.iota(iota_rows[:], pattern=[[P, NT]], base=0, channel_multiplier=0,
                       allow_small_or_imprecise_dtypes=True).then_inc(consts, 1)
        nc.gpsimd.iota(iota_tile[:], pattern=[[1, SLOT_TILES]], base=0, channel_multiplier=0,
                       allow_small_or_imprecise_dtypes=True).then_inc(consts, 1)
        pool.wait_ge(consts, 3)
        nc.gpsimd.memset(ones[:], 1.0).then_inc(consts, 1)
        nc.gpsimd.memset(before[:], 0.0).then_inc(pool_chain, 1)
        pool.wait_ge(pool_chain, 1)
        nc.gpsimd.affine_select(out=before[:], in_=before[:], compare_op=ALU.is_ge, fill=1.0, base=0,
                                pattern=[[-1, P]], channel_multiplier=1).then_inc(consts, 1)

    def act_part(act):
        act.wait_ge(shift_done, 1)
        nc.scalar.activation(expd[:], shifted[:], ACT.Exp).then_inc(exp_done, 1)

    def pe_part(pe):
        pe.wait_ge(consts, 5)
        pe.wait_ge(both_done, 1)
        rows = both[:].rearrange("p a e -> p (a e)")
        nc.tensor.matmul(rank_ps[:, 0:NT * E], before[:], rows, start=True, stop=True).then_inc(counted, 1)
        nc.tensor.matmul(total_ps[:, 0:NT * E], ones[:], rows, start=True, stop=True).then_inc(counted, 1)

    def dve_part(dve):
        n = [0]

        def link(ins):
            n[0] += 1
            ins.then_inc(chain, 1)
            dve.wait_ge(chain, n[0])

        V = nc.vector

        def per_tile(ap):
            return ap.unsqueeze(2).to_broadcast([P, NT, E])

        link(V.tensor_reduce(top1[:], logits[:], AX.X, ALU.max))
        V.tensor_tensor(shifted[:], logits[:], per_tile(top1[:]), ALU.subtract).then_inc(shift_done, 1)
        dve.wait_ge(exp_done, 1)
        link(V.tensor_reduce(denom[:, 0, :], expd[:], AX.X, ALU.add))
        link(V.reciprocal(denom[:, 1, :], denom[:, 0, :]))
        link(V.tensor_tensor(prob[:], expd[:], per_tile(denom[:, 1, :]), ALU.mult))
        for a in range(NT):
            last = V.max(best[:, a, :], prob[:, a, :])
        link(last)
        for a in range(NT):
            last = V.max_index(best_at[:, a, :], best[:, a, :], prob[:, a, :])
        link(last)
        link(V.tensor_copy(chosen[:], best_at[:, :, 0:TOPK]))
        dve.wait_ge(consts, 5)
        for j in range(TOPK):
            last = V.tensor_tensor(mask[:, j], iota_e[:].unsqueeze(1).to_broadcast([P, NT, E]),
                                   per_tile(chosen[:, :, j]), ALU.is_equal)
        link(last)
        V.tensor_tensor(both[:], mask[:, 0], mask[:, 1], ALU.add).then_inc(both_done, 1)
        link(V.tensor_tensor(pair_sum[:, 0, :], best[:, :, 0], best[:, :, 1], ALU.add))
        link(V.reciprocal(pair_sum[:, 1, :], pair_sum[:, 0, :]))
        for j in range(TOPK):
            V.tensor_tensor(keep["weight"][:, j, :], best[:, :, j], pair_sum[:, 1, :], ALU.mult)
        link(V.memset(prefix[:, 0, :], 0.0))
        dve.wait_ge(counted, 2)
        link(V.tensor_copy(total[:], total_ps[:, 0:NT * E].rearrange("p (a e) -> p a e", e=E)))
        for a in range(NT):
            link(V.tensor_tensor(prefix[:, a + 1, :], prefix[:, a, :], total[:, a, :], ALU.add))
        link(V.tensor_tensor(over[:], prefix[:, NT, :].unsqueeze(2).to_broadcast([P, E, NT]),
                             iota_rows[:].unsqueeze(1).to_broadcast([P, E, NT]), ALU.is_gt))
        link(V.tensor_reduce(tiles[:], over[:], AX.X, ALU.add))
        link(V.tensor_copy(upto[:, 0:1], tiles[:, 0:1]))
        for e in range(1, E):
            link(V.tensor_tensor(upto[:, e:e + 1], upto[:, e - 1:e], tiles[:, e:e + 1], ALU.add))
        link(V.tensor_tensor(base[:], upto[:], tiles[:], ALU.subtract))
        link(V.scalar_tensor_tensor(place[:], base[:].unsqueeze(1).to_broadcast([P, NT, E]), float(P),
                                    prefix[:, 0:NT, :], ALU.mult, ALU.add))
        link(V.tensor_tensor(place[:], rank_ps[:, 0:NT * E].rearrange("p (a e) -> p a e", e=E), place[:], ALU.add))
        for j in range(TOPK):
            last = V.tensor_tensor(picked[:, j], mask[:, j], place[:], ALU.mult)
        link(last)
        link(V.tensor_reduce(slot_f[:].rearrange("p j a -> p (j a)"), picked[:].rearrange("p j a e -> p (j a) e"), AX.X, ALU.add))
        V.tensor_copy(keep["slot"][:], slot_f[:])
        link(V.tensor_tensor(passed[:], upto[0:1, :].unsqueeze(1).to_broadcast([1, SLOT_TILES, E]),
                             iota_tile[:].unsqueeze(2).to_broadcast([1, SLOT_TILES, E]), ALU.is_le))
        link(V.tensor_reduce(owner[:, 0, :], passed[:], AX.X, ALU.add))
        link(V.tensor_scalar(owner[:, 1, :], owner[:, 0, :], float(E - 1), None, ALU.min))
        V.tensor_copy(keep["tile_expert"][:], owner[:, 1, :]).then_inc(route_done, 1)

    return pool_part, act_part, pe_part, dve_part, route_done


def experts(nc, keep, scratch, x, w_proj, b_proj, w1_t, w2_t):
    ctx = ExitStack()
    with ctx:
        m = Memory(nc, ctx)
        o_t, tile_expert = keep["o_t"], keep["tile_expert"]
        w1 = m.sbuf("w1", [P, E, DK, 2 * I], F32)
        w2 = m.sbuf("w2", [P, E, len(I_TILES), D], F32)
        wp = m.sbuf("wp", [P, NG, D], F32)
        bp = m.sbuf("bp", [P, D], F32)
        ident = m.sbuf("ident3", [P, P], F32)
        RES = 4
        res = m.sbuf("res", [P, RES, D], F32)
        rows = m.sbuf("rows", [P, 2, D], F32)
        rows_t = [m.sbuf(f"rows_t{r}", [P, D], F32) for r in range(2)]
        gated = m.sbuf("gated", [P, I], F32)
        hidden = [m.sbuf(f"hidden{r}", [P, I], F32) for r in range(2)]
        hidden_t = [m.sbuf(f"hidden_t{r}", [P, len(I_TILES), P], F32) for r in range(2)]
        y = m.sbuf("y", [P, 2, D], F32)
        gu = [[m.psum(f"gu{r}{j}", [P, CH]) for j in range(2)] for r in range(2)]
        turn_ps, hid_ps = m.psum("turn_ps", [P, CH]), m.psum("hid_ps", [P, CH])
        down = [m.psum(f"down{r}", [P, CH]) for r in range(2)]

        ident_done, pool_chain = m.sem("ident3_done"), m.sem("pool_chain3")
        wp_in, bp_in, weights_in = m.sem("wp_in"), m.sem("bp_in"), [m.sem(f"weights_in{e}") for e in range(E)]
        expert_ready = m.sem("expert_ready")
        res_in = [m.sem(f"res_in{r}") for r in range(RES)]
        res_out = [m.sem(f"res_out{r}") for r in range(RES)]
        biased, proj_full, res_done = m.sem("biased"), m.sem("proj_full"), m.sem("res_done")
        rows_in = [m.sem(f"rows_in{r}") for r in range(2)]
        y_out = [m.sem(f"y_out{r}") for r in range(2)]
        turned, turned_read = m.sem("rows_turned"), m.sem("rows_t_done")
        gu_full, silu_done, hidden_done = m.sem("gu_full"), m.sem("silu_done"), m.sem("hidden_done")
        hid_turned, hid_read = m.sem("hid_turned"), m.sem("hid_t_done")
        y_full, y_read = m.sem("y_full"), m.sem("y_read")

        x_rows = x.rearrange("b (a p) d -> (b a) p d", p=P)
        res_rows = scratch["res"].rearrange("(a p) d -> a p d", p=P)
        in_rows = scratch["routed"].rearrange("(a p) d -> a p d", p=P)
        y_rows = scratch["y"].rearrange("(a p) d -> a p d", p=P)
        block = ctx.enter_context(nc.Block())

        def run_tiles(engine, tile):
            for i in range(4):
                tile(i, i % 2, i // 2)
            with engine.Fori(2, (SLOT_TILES - 1) // 2) as pairs:
                tile(pairs * 2, 0, pairs)
                tile(pairs * 2 + 1, 1, pairs)
            tile(SLOT_TILES - 1, 0, (SLOT_TILES - 1) // 2)

        def past(i, least):
            return not isinstance(i, int) or i >= least

        def early(i):
            return isinstance(i, int) and i < 2

        @block.sync
        def _(sp):
            sp.dma_start(wp[:], w_proj.rearrange("(g p) d -> p g d", p=P)).then_inc(wp_in, 16)
            for a in range(NT + 2):
                if a < NT:
                    r = a % RES
                    if a >= RES:
                        sp.wait_ge(res_out[r], 16 * (a // RES))
                    sp.dma_start(res[:, r, :], x_rows[a]).then_inc(res_in[r], 16)
                if a >= 2:
                    sp.wait_ge(res_done, a - 1)
                    sp.dma_start(res_rows[a - 2], res[:, (a - 2) % RES, :]).then_inc(res_out[(a - 2) % RES], 16)

            def tile(i, r, half):
                if not early(i):
                    sp.wait_ge(turned, i - 1)
                sp.dma_start(rows[:, r:r + 1, :], in_rows[bass.ds(i, 1)].rearrange("a p d -> p a d")).then_inc(rows_in[r], 16)

            run_tiles(sp, tile)
            for s in res_out:
                sp.wait_ge(s, 16 * NT // RES)

        @block.gpsimd
        def _(pool):
            nc.gpsimd.memset(ident[:], 0.0).then_inc(pool_chain, 1)
            pool.wait_ge(pool_chain, 1)
            nc.gpsimd.affine_select(out=ident[:], in_=ident[:], compare_op=ALU.not_equal, fill=1.0, base=0,
                                    pattern=[[-1, P]], channel_multiplier=1).then_inc(ident_done, 1)
            pool.wait_ge(bp_in, 16)
            for a in range(NT):
                pool.wait_ge(res_in[a % RES], 16 * (a // RES + 1))
                nc.gpsimd.tensor_tensor(res[:, a % RES, :], res[:, a % RES, :], bp[:], ALU.add).then_inc(biased, 1)

            for e in range(E):
                pool.wait_ge(weights_in[e], 3 * 16)
                pool.sem_inc(expert_ready, 1)

            def tile(i, r, half):
                pool.wait_ge(y_read, i + 1)
                pool.dma_start(y_rows[bass.ds(i, 1)].rearrange("a p d -> p a d"), y[:, r:r + 1, :]).then_inc(y_out[r], 16)

            run_tiles(pool, tile)
            pool.wait_ge(y_out[0], 16 * ((SLOT_TILES + 1) // 2))
            pool.wait_ge(y_out[1], 16 * (SLOT_TILES // 2))

        @block.scalar
        def _(act):
            act.dma_start(bp[:], b_proj.partition_broadcast(P)).then_inc(bp_in, 16)
            for e in range(E):
                if e:
                    act.wait_ge(res_done, min(3 * e, NT))
                act.dma_start(w1[:, e], w1_t[e].rearrange("(k p) n -> p k n", p=P)).then_inc(weights_in[e], 16)
                act.dma_start(w2[:, e, 0:2, :], w2_t[e, 0:2 * P, :].rearrange("(k p) n -> p k n", p=P)).then_inc(weights_in[e], 16)
                act.dma_start(w2[0:I - 2 * P, e, 2, :], w2_t[e, 2 * P:I, :]).then_inc(weights_in[e], 16)

            def rows_to_sbuf(i, r):
                act.wait_ge(turned, i + 1)
                if not early(i):
                    act.wait_ge(gu_full, 2 * (i - 1))
                nc.scalar.copy(rows_t[r][:], turn_ps[:]).then_inc(turned_read, 1)

            def y_to_sbuf(i, r, half):
                act.wait_ge(y_full, i + 1)
                if not early(i):
                    act.wait_ge(y_out[r], half * 16)
                nc.scalar.copy(y[:, r, :], down[r][:]).then_inc(y_read, 1)

            def tile(i, r, half):
                if past(i, 2):
                    y_to_sbuf(i - 2, r, half - 1)
                act.wait_ge(gu_full, i * 2 + 1)
                if past(i, 1):
                    act.wait_ge(hidden_done, i)
                nc.scalar.activation(gated[:], gu[r][0][:, 0:I], ACT.Silu).then_inc(silu_done, 1)
                if not (isinstance(i, int) and i == SLOT_TILES - 1):
                    rows_to_sbuf(i + 1, 1 - r)

            rows_to_sbuf(0, 0)
            run_tiles(act, tile)
            y_to_sbuf(SLOT_TILES - 2, 1, (SLOT_TILES - 2) // 2)
            y_to_sbuf(SLOT_TILES - 1, 0, (SLOT_TILES - 1) // 2)

        @block.vector
        def _(dve):
            for a in range(NT):
                dve.wait_ge(proj_full, a + 1)
                dve.wait_ge(biased, a + 1)
                nc.vector.tensor_tensor(res[:, a % RES, :], gu[a % 2][0][:], res[:, a % RES, :], ALU.add).then_inc(res_done, 1)

            def hidden_to_sbuf(i, r):
                dve.wait_ge(hid_turned, i + 1)
                if not early(i):
                    dve.wait_ge(y_full, i - 1)
                nc.vector.tensor_copy(hidden_t[r][:, 0:2, :], hid_ps[:, 0:2 * P].rearrange("p (k t) -> p k t", t=P))
                nc.vector.tensor_copy(hidden_t[r][0:I - 2 * P, 2, :], hid_ps[0:I - 2 * P, 2 * P:3 * P]).then_inc(hid_read, 1)

            def tile(i, r, half):
                if not (isinstance(i, int) and i == 0):
                    hidden_to_sbuf(i - 1, 1 - r)
                dve.wait_ge(silu_done, i + 1)
                dve.wait_ge(gu_full, i * 2 + 2)
                if not early(i):
                    dve.wait_ge(hid_turned, i - 1)
                nc.vector.tensor_tensor(hidden[r][:], gu[r][1][:, 0:I], gated[:], ALU.mult).then_inc(hidden_done, 1)

            run_tiles(dve, tile)
            hidden_to_sbuf(SLOT_TILES - 1, 0)

        @block.tensor
        def _(pe):
            pe.wait_ge(wp_in, 16)
            for a in range(NT):
                if a >= 2:
                    pe.wait_ge(res_done, a - 1)
                for g in range(NG):
                    last = nc.tensor.matmul(gu[a % 2][0][:], o_t[:, g, a * P:(a + 1) * P], wp[:, g, :],
                                            start=(g == 0), stop=(g == NG - 1))
                last.then_inc(proj_full, 1)
            pe.wait_ge(ident_done, 1)
            pe.wait_ge(res_done, NT)

            def turn_rows(i, r, half):
                pe.wait_ge(rows_in[r], (half + 1) * 16)
                if not (isinstance(i, int) and i == 0):
                    pe.wait_ge(turned_read, i)
                for k in range(DK):
                    last = nc.tensor.transpose(turn_ps[:, k * P:(k + 1) * P], rows[:, r, k * P:(k + 1) * P], ident[:])
                last.then_inc(turned, 1)

            def up(i, r, e, j):
                for k in range(DK):
                    last = nc.tensor.matmul(gu[r][j][:, 0:I], rows_t[r][:, k * P:(k + 1) * P],
                                            w1[:, bass.ds(e, 1), k, j * I:(j + 1) * I].rearrange("p o n -> p (o n)"),
                                            start=(k == 0), stop=(k == DK - 1))
                last.then_inc(gu_full, 1)

            def turn_hidden(i, r):
                pe.wait_ge(hidden_done, i + 1)
                if not (isinstance(i, int) and i == 0):
                    pe.wait_ge(hid_read, i)
                for k, (at, n) in enumerate(I_TILES):
                    last = nc.tensor.transpose(hid_ps[0:n, k * P:(k + 1) * P], hidden[r][:, at:at + n], ident[:])
                last.then_inc(hid_turned, 1)

            def down_product(i, r, e):
                pe.wait_ge(hid_read, i + 1)
                if not early(i):
                    pe.wait_ge(y_read, i - 1)
                for k, (at, n) in enumerate(I_TILES):
                    last = nc.tensor.matmul(down[r][:], hidden_t[r][0:n, k, :],
                                            w2[0:n, bass.ds(e, 1), k, :].rearrange("p o n -> p (o n)"),
                                            start=(k == 0), stop=(k == len(I_TILES) - 1))
                last.then_inc(y_full, 1)

            def expert_of(i):
                return pe.value_load(tile_expert[0:1, bass.ds(i, 1)], min_val=0, max_val=E - 1)

            def tile(i, r, half):
                if past(i, 2):
                    before = expert_of(i - 2)
                e = expert_of(i)
                if past(i, 2):
                    down_product(i - 2, r, before)
                pe.wait_ge(turned_read, i + 1)
                if past(i, 2):
                    pe.wait_ge(hidden_done, i - 1)
                pe.wait_ge(expert_ready, e + 1)
                up(i, r, e, 0)
                if past(i, 1):
                    turn_hidden(i - 1, 1 - r)
                if not (isinstance(i, int) and i == SLOT_TILES - 1):
                    turn_rows(i + 1, 1 - r, half if r == 0 else half + 1)
                up(i, r, e, 1)

            turn_rows(0, 0, 0)
            run_tiles(pe, tile)
            down_product(SLOT_TILES - 2, 1, expert_of(SLOT_TILES - 2))
            turn_hidden(SLOT_TILES - 1, 0)
            down_product(SLOT_TILES - 1, 0, expert_of(SLOT_TILES - 1))


def combine(nc, keep, scratch, out):
    RINGS = 4
    ctx = ExitStack()
    with ctx:
        m = Memory(nc, ctx)
        first = m.sbuf("first", [P, RINGS, D], F32)
        second = m.sbuf("second", [P, RINGS, D], F32)
        total = m.sbuf("total_out", [P, RINGS, D], F32)
        weight, slot = keep["weight"], keep["slot"]
        got = [[m.sem(f"got{j}{r}") for r in range(RINGS)] for j in range(TOPK)]
        res_in = [m.sem(f"res_back{r}") for r in range(RINGS)]
        stored = [m.sem(f"stored{r}") for r in range(RINGS)]
        one_added, both_added = m.sem("one_added"), m.sem("both_added")
        res_rows = scratch["res"].rearrange("(a p) d -> a p d", p=P)
        out_rows = out.rearrange("b (a p) d -> (b a) p d", p=P)
        block = ctx.enter_context(nc.Block())

        @block.gpsimd
        def _(pool):
            for a in range(NT):
                r = a % RINGS
                if a >= RINGS:
                    pool.wait_ge(both_added, a - RINGS + 1)
                for j, row in enumerate((first, second)):
                    pool.indirect_dma_start(out=row[:, r, :], out_offset=None, in_=scratch["y"],
                                            in_offset=bass.IndirectOffsetOnAxis(ap=slot[:, j, a:a + 1], axis=0)).then_inc(got[j][r], 16)

        @block.sync
        def _(sp):
            for a in range(NT + 2):
                if a < NT:
                    r = a % RINGS
                    if a >= RINGS:
                        sp.wait_ge(stored[r], 16 * (a // RINGS))
                    sp.dma_start(total[:, r, :], res_rows[a]).then_inc(res_in[r], 16)
                if a >= 2:
                    sp.wait_ge(both_added, a - 1)
                    sp.dma_start(out_rows[a - 2], total[:, (a - 2) % RINGS, :]).then_inc(stored[(a - 2) % RINGS], 16)
            for s in stored:
                sp.wait_ge(s, 16 * NT // RINGS)

        @block.vector
        def _(dve):
            for a in range(NT):
                r, nth = a % RINGS, 16 * (a // RINGS + 1)
                dve.wait_ge(res_in[r], nth)
                dve.wait_ge(got[0][r], nth)
                nc.vector.scalar_tensor_tensor(total[:, r, :], first[:, r, :], weight[:, 0, a:a + 1], total[:, r, :],
                                               ALU.mult, ALU.add).then_inc(one_added, 1)
                dve.wait_ge(got[1][r], nth)
                dve.wait_ge(one_added, a + 1)
                nc.vector.scalar_tensor_tensor(total[:, r, :], second[:, r, :], weight[:, 1, a:a + 1], total[:, r, :],
                                               ALU.mult, ALU.add).then_inc(both_added, 1)


def attend(nc, keep, scratch):
    PAIR = 2
    PAIRS = HG // PAIR
    SETS = B * PAIRS
    ROUNDS = NG * SETS
    TQ = S // P
    NC = S // CH
    STACK = 3 * HD + 2
    steps = [(c, j) for c in range(NC) for j in range((c + 1) * TPC)]
    NS = len(steps)
    units = [(h, i, c) for h in range(PAIR) for i in range(TQ) for c in range(i // TPC + 1)]
    NU = len(units)
    PER = NU // NS
    RING = 3
    TURN_STEP = 2
    TURN_AT = TURN_STEP * PER
    TURN_BANK = TURN_AT % RING

    def place(u):
        return u + (u >= TURN_AT)

    def bank_at(at):
        return 1 if at == NU else at % RING

    def bank_before(at, turned):
        back, bank = 0, bank_at(at)
        while True:
            at -= 1
            if at < 0:
                back, at = back + 1, NU
            if bank_at(at) == bank and (turned or at != TURN_AT):
                return back, at

    ctx = ExitStack()
    with ctx:
        m = Memory(nc, ctx)
        q_st = [m.sbuf(f"q_stack{i}", [P, PAIR, S], F32R) for i in range(SETS)]
        k_st = [m.sbuf(f"k_stack{i}", [P, PAIR, S], F32R) for i in range(SETS)]
        v_st = [m.sbuf(f"v_ones{i}", [P, TQ, PAIR, 2 * HD], F32) for i in range(SETS)]
        PR = 3
        probs = m.sbuf("probs", [P, PR, PAIR, CH], F32)
        o_raw = m.sbuf("o_raw", [P, NC, CH], F32)
        sums = m.sbuf("sums", [P, NC, CH], F32)
        inv = m.sbuf("inv", [P, NC, CH], F32)
        mx = [m.sbuf(f"mx{i}", [P, PAIR, TQ], F32) for i in range(2)]
        mx_far = m.sbuf("mx_far", [P, PAIR, TQ - TPC], F32)
        row_hi = m.sbuf("row_hi", [PAIR * TQ, P], F32R)
        row_lo = m.sbuf("row_lo", [PAIR * TQ, P], F32R)
        ident = m.sbuf("ident2", [P, P], F32)
        ident16 = m.sbuf("ident16", [P, P], BF16)
        mask_m = m.sbuf("mask_m", [P, P], BF16)
        mask_t = m.sbuf("mask_t", [P, P], BF16)
        o_t = keep["o_t"]

        scores_t = [m.psum(f"scores_t{r}", [P, CH]) for r in range(RING)]
        o_acc = [m.psum(f"o_acc{c}", [P, CH]) for c in range(NC)]
        mb = [m.psum(f"maxima{r}", [P, CH]) for r in range(RING)]

        scattered = m.sem("scattered")
        blank, consts, minus_ones = m.sem("blank"), m.sem("consts"), m.sem("minus_ones")
        loaded = [m.sem(f"stack_in{i}") for i in range(SETS)]
        row_in = m.sem("row_in")
        m_full = m.sem("m_full")
        m_free = m.sem("m_free")
        mx_done, turned = m.sem("mx_done"), m.sem("mx_turned")
        row_hi_done, row_lo_done = m.sem("row_hi_done"), m.sem("row_lo_done")
        st_full = m.sem("st_full")
        exp_done = m.sem("exp_done")
        pv_done = m.sem("pv_done")
        o_read = m.sem("o_read")
        norm_done = m.sem("norm_done")
        inv_done = m.sem("inv_done")
        PIECES = 8
        LOADS = 6 + PAIR
        NORMS = NC * PIECES

        def stack_rows(name):
            return scratch[name].rearrange("(r h d) t -> r d h t", r=2, d=HD)

        v_rows = scratch["v"].rearrange("(a p) (h d) -> h p a d", p=P, d=HD)
        route_pool, route_act, route_pe, route_dve, route_done = route(nc, m, keep, scores_t[0:2])
        block = ctx.enter_context(nc.Block())

        def run_rounds(engine, round_):
            round_(0, 0, 0)
            with engine.Fori(0, NG - 1) as g:
                for s in range(1, SETS + 1):
                    round_(g * SETS + s, s % SETS, g + s // SETS)
            for s in range(1, SETS):
                round_((NG - 1) * SETS + s, s, NG - 1)

        def below(n, number):
            return n < number if isinstance(n, int) else number > 1

        PW = CH // PIECES
        NORM_FROM = TPC + 3
        NORM_LATE = NS - NORM_FROM

        def norm_number(n, c, q):
            return (n - 1) * (NORMS // PAIRS) + (c * PIECES + q + 1)

        def norm_at(n, i, g, k, norm):
            if i % PAIRS == PAIRS - 1:
                if k >= NORM_FROM:
                    norm(n, i, g, 0, k - NORM_FROM)
            elif not (isinstance(n, int) and n == 0):
                c, q = divmod(k + NORM_LATE, PIECES)
                if c < NC:
                    norm(n - 1, (i - 1) % SETS, g - (i == 0), c, q)

        @block.sync
        def _(sp):
            for s, n in ((exp_done, RING), (pv_done, PR), (o_read, NC), (norm_done, NORMS)):
                sp.sem_inc(s, n)

            def load(i, g):
                b, pair = i // PAIRS, i % PAIRS
                toks = slice(b * S, (b + 1) * S)
                for part, r, (hi0, hi1, lo) in ((q_st[i], 0, (0, 2, 1)), (k_st[i], 1, (0, 1, 2))):
                    for at, name in ((hi0, "qk_hi"), (lo, "qk_lo"), (hi1, "qk_hi")):
                        sp.dma_start(as_f32(part[at * HD:(at + 1) * HD, :, :]),
                                     stack_rows(name)[r, :, bass.ds(g * HG + pair * PAIR, PAIR), toks]).then_inc(loaded[i], 16)
                for h in range(PAIR):
                    src = v_rows[bass.ds(g * HG + pair * PAIR + h, 1), :, b * TQ:(b + 1) * TQ, :]
                    sp.dma_start(v_st[i][:, :, h, 0:HD], src.rearrange("o p a d -> (o p) a d")).then_inc(loaded[i], 16)

            def rows(n, i):
                sp.wait_ge(row_lo_done, n + 1)
                for at, row in ((3 * HD, row_hi), (3 * HD + 1, row_lo)):
                    sp.dma_start(as_f32(q_st[i][at:at + 1, :, :].rearrange("o h (i t) -> o (h i) t", t=P)),
                                 as_f32(row[:])).then_inc(row_in, 16)

            def round_(n, i, g):
                if below(n, ROUNDS - 3):
                    if not (isinstance(n, int) and n == 0):
                        sp.wait_ge(pv_done, n * NS + PR)
                    load((i + 3) % SETS, g + (i + 3) // SETS)
                if below(n, ROUNDS - 1):
                    rows(n + 1, (i + 1) % SETS)

            for i in range(3):
                load(i, 0)
            rows(0, 0)
            run_rounds(sp, round_)

        @block.gpsimd
        def _(pool):
            route_pool(pool)
            for t in (ident, ident16, mask_m, mask_t):
                nc.gpsimd.memset(t[:], 0.0).then_inc(blank, 1)
            for i in range(SETS):
                nc.gpsimd.memset(v_st[i][:, :, :, HD:2 * HD], 1.0).then_inc(consts, 1)
            pool.wait_ge(blank, 4)
            for t in (ident, ident16):
                nc.gpsimd.affine_select(out=t[:], in_=t[:], compare_op=ALU.not_equal, fill=1.0, base=0,
                                        pattern=[[-1, P]], channel_multiplier=1).then_inc(consts, 1)
            nc.gpsimd.affine_select(out=mask_m[:], in_=mask_m[:], compare_op=ALU.is_ge, fill=NEG, base=0,
                                    pattern=[[-1, P]], channel_multiplier=1).then_inc(consts, 1)
            nc.gpsimd.affine_select(out=mask_t[:], in_=mask_t[:], compare_op=ALU.is_ge, fill=NEG, base=0,
                                    pattern=[[1, P]], channel_multiplier=-1).then_inc(consts, 1)
            pool.wait_ge(route_done, 1)
            for a in range(NT):
                for j in range(TOPK):
                    pool.indirect_dma_start(out=scratch["routed"], out_offset=bass.IndirectOffsetOnAxis(
                        ap=keep["slot"][:, j, a:a + 1], axis=0), in_=keep["x_rows"][:, a, :], in_offset=None).then_inc(scattered, 16)

            def norm(n, i, g, c, q):
                b, cols = i // PAIRS, slice(q * PW, (q + 1) * PW)
                pool.wait_ge(inv_done, norm_number(n, c, q))
                nc.gpsimd.tensor_tensor(o_t[:, bass.ds(g, 1), b * S + c * CH + q * PW:b * S + c * CH + (q + 1) * PW],
                                        o_raw[:, c:c + 1, cols], inv[:, c:c + 1, cols], ALU.mult).then_inc(norm_done, 1)

            def round_(n, i, g):
                for k in range(NS):
                    norm_at(n, i, g, k, norm)

            run_rounds(pool, round_)
            for q in range(NORM_LATE, PIECES):
                norm(ROUNDS - 1, SETS - 1, NG - 1, 0, q)
            for q in range(PIECES):
                norm(ROUNDS - 1, SETS - 1, NG - 1, 1, q)
            pool.wait_ge(scattered, 16 * TOPK * NT)

        @block.scalar
        def _(act):
            def row_high(n):
                act.wait_ge(turned, n + 1)
                if not (isinstance(n, int) and n == 0):
                    act.wait_ge(row_in, n * 32)
                nc.scalar.copy(row_hi[:], mb[TURN_BANK][0:PAIR * TQ, 0:P]).then_inc(row_hi_done, 1)

            def o_out(n, i, c, h, row):
                at = (i % PAIRS * PAIR + h) * HD
                to = (o_raw, sums)[row][at:at + HD, c, :]
                if h == 0 and row == 0:
                    act.wait_ge(pv_done, n * NS + ((c + 1) * (c + 2) // 2 * TPC + PR))
                    if i % PAIRS == 0:
                        act.wait_ge(norm_done, n * (NORMS // PAIRS) + (c + 1) * PIECES)
                ins = nc.scalar.activation(to, o_acc[c][(2 * h + row) * HD:(2 * h + row + 1) * HD, :], ACT.Copy,
                                           scale=1.0 if row else SCALE)
                if h == 1 and row == 1:
                    ins.then_inc(o_read, 1)

            def round_(n, i, g):
                for k, (c, j) in enumerate(steps):
                    w = min(CH, (c + 1) * CH - j * P)
                    for h in range(PAIR):
                        e = PAIR * k + h
                        act.wait_ge(st_full, n * (PAIR * NS) + (e + 1))
                        if h == 0:
                            act.wait_ge(pv_done, n * NS + (k + 1))
                        nc.scalar.activation(probs[:, k % PR, h, 0:w], scores_t[e % RING][:, 0:w], ACT.Exp).then_inc(exp_done, 1)
                        if k in (1, 2) and not (isinstance(n, int) and n == 0):
                            o_out(n - 1, (i - 1) % SETS, 1, k - 1, h)
                        if k in (TPC + 1, TPC + 2):
                            o_out(n, i, 0, k - TPC - 1, h)
                    if k == TURN_STEP and below(n, ROUNDS - 1):
                        row_high(n + 1)

            route_act(act)
            row_high(0)
            run_rounds(act, round_)
            for h in range(PAIR):
                for row in range(2):
                    o_out(ROUNDS - 1, SETS - 1, 1, h, row)

        @block.vector
        def _(dve):
            def unit(n, i, u):
                h, t, c = units[u]
                w = min(CH, (t + 1) * P - c * CH)
                dve.wait_ge(m_full, n * NU + (u + 1))
                to = mx[i % 2][:, h, t:t + 1] if c == 0 else mx_far[:, h, t - TPC:t - TPC + 1]
                nc.vector.tensor_reduce(to, mb[bank_at(place(u))][:, 0:w], AX.X, ALU.max).then_inc(m_free, 1)

            def join(n, i):
                dve.wait_ge(m_free, n * NU + NU)
                far = mx[i % 2][:, :, TPC:TQ]
                nc.vector.tensor_tensor(far, far, mx_far[:], ALU.max).then_inc(mx_done, 1)

            def row_low(n):
                dve.wait_ge(row_hi_done, n + 1)
                nc.vector.tensor_tensor(row_lo[:], mb[TURN_BANK][0:PAIR * TQ, 0:P], as_f32(row_hi[:]), ALU.subtract).then_inc(row_lo_done, 1)

            def invert(n, i, g, c, q):
                cols = slice(q * PW, (q + 1) * PW)
                dve.wait_ge(o_read, n * NC + (c + 1 + NC))
                dve.wait_ge(norm_done, norm_number(n, c, q))
                nc.vector.reciprocal(inv[:, c, cols], sums[:, c, cols]).then_inc(inv_done, 1)

            def round_(n, i, g):
                for k in range(NS):
                    if k == TURN_STEP + 1 and below(n, ROUNDS - 1):
                        row_low(n + 1)
                    if below(n, ROUNDS - 2):
                        for u in range(k * PER, (k + 1) * PER):
                            unit(n + 2, (i + 2) % SETS, u)
                    norm_at(n, i, g, k, invert)
                if below(n, ROUNDS - 2):
                    join(n + 2, (i + 2) % SETS)

            route_dve(dve)
            for i in range(SETS):
                nc.vector.memset(as_f32(k_st[i][3 * HD:STACK, :, :]), -1.0).then_inc(minus_ones, 1)
            for u in range(NU):
                unit(0, 0, u)
            join(0, 0)
            for u in range(NU):
                if u == TURN_AT + 2:
                    row_low(0)
                unit(1, 1, u)
            join(1, 1)
            run_rounds(dve, round_)
            for q in range(NORM_LATE, PIECES):
                invert(ROUNDS - 1, SETS - 1, NG - 1, 0, q)
            for q in range(PIECES):
                invert(ROUNDS - 1, SETS - 1, NG - 1, 1, q)

        @block.tensor
        def _(pe):
            def claim(n, at):
                back, before = bank_before(at, not (isinstance(n, int) and n == 0))
                if isinstance(n, int) and n < back:
                    return
                if before == TURN_AT:
                    pe.wait_ge(row_lo_done, n - back)
                else:
                    number = before - (before > TURN_AT) + 1
                    pe.wait_ge(m_free, min(n * NU - back * NU + number, ROUNDS * NU) if isinstance(n, int) else n * NU + (number - back * NU))

            def unit(n, i, u):
                h, t, c = units[u]
                w = min(CH, (t + 1) * P - c * CH)
                diag = t // TPC == c
                claim(n, place(u))
                out = mb[bank_at(place(u))]
                last = nc.tensor.matmul(out[:, 0:w], q_st[i][0:3 * HD, h, t * P:(t + 1) * P],
                                        k_st[i][0:3 * HD, h, c * CH:c * CH + w], start=True, stop=not diag)
                if diag:
                    last = nc.tensor.matmul(out[:, w - P:w], ident16[:], mask_m[:], start=False, stop=True)
                last.then_inc(m_full, 1)

            def turn(n, i, frame):
                pe.wait_ge(mx_done, n + 1)
                claim(frame, TURN_AT)
                nc.tensor.transpose(mb[TURN_BANK][0:PAIR * TQ, 0:P], mx[i % 2][:].rearrange("p h i -> p (h i)"), ident[:]).then_inc(turned, 1)

            def scores(n, i, k, h):
                c, j = steps[k]
                t0 = max(c * CH, j * P)
                w = (c + 1) * CH - t0
                diag = j >= c * TPC
                e = PAIR * k + h
                pe.wait_ge(exp_done, n * (PAIR * NS) + (e + 1))
                out = scores_t[e % RING]
                last = nc.tensor.matmul(out[:, 0:w], k_st[i][0:STACK, h, j * P:(j + 1) * P],
                                        q_st[i][0:STACK, h, t0:t0 + w], start=True, stop=not diag)
                if diag:
                    last = nc.tensor.matmul(out[:, 0:P], ident16[:], mask_t[:], start=False, stop=True)
                last.then_inc(st_full, 1)

            def values(n, i, k):
                c, j = steps[k]
                w = min(CH, (c + 1) * CH - j * P)
                if j == 0:
                    pe.wait_ge(o_read, n * NC + (c + 1))
                pe.wait_ge(exp_done, n * (PAIR * NS) + (PAIR * (k + 1) + RING))
                for h in range(PAIR):
                    last = nc.tensor.matmul(o_acc[c][2 * HD * h:2 * HD * (h + 1), CH - w:CH], v_st[i][:, j, h, :],
                                            probs[:, k % PR, h, 0:w], start=(j == 0), stop=(j == (c + 1) * TPC - 1))
                last.then_inc(pv_done, 1)

            def round_(n, i, g):
                if below(n, ROUNDS - 2):
                    pe.wait_ge(loaded[(i + 2) % SETS], (g + ((i + 2) // SETS + 1)) * 16 * LOADS)
                for k in range(NS):
                    if k == TURN_STEP and below(n, ROUNDS - 1):
                        turn(n + 1, (i + 1) % SETS, n + 2)
                    for h in range(PAIR):
                        if k + 1 < NS:
                            scores(n, i, k + 1, h)
                        elif below(n, ROUNDS - 1):
                            if h == 0:
                                pe.wait_ge(row_in, n * 32 + 64)
                            scores(n + 1, (i + 1) % SETS, 0, h)
                        if below(n, ROUNDS - 2):
                            unit(n + 2, (i + 2) % SETS, k * PER + h)
                    values(n, i, k)

            route_pe(pe)
            pe.wait_ge(consts, SETS + 4)
            pe.wait_ge(minus_ones, SETS)
            pe.wait_ge(loaded[0], 16 * LOADS)
            for u in range(NU):
                unit(0, 0, u)
            pe.wait_ge(loaded[1], 16 * LOADS)
            for u in range(NU):
                if u == TURN_AT:
                    turn(0, 0, 1)
                unit(1, 1, u)
            pe.wait_ge(row_in, 32)
            pe.wait_ge(route_done, 1)
            for h in range(PAIR):
                scores(0, 0, 0, h)
            nc.disable_value_cache = True
            run_rounds(pe, round_)
            nc.disable_value_cache = False


def attention_and_experts(nc, x, w_attn, bias_qk, bias_qk_pair, bias_v, w_proj, b_proj, gate_t, w1_t, w2_t,
                          rope_cos, rope_sin, rope_cos_col, rope_sin_col, out):
    scratch = {
        "qk_hi": nc.dram_tensor("qk_hi", [2 * D, T], F32).ap(),
        "qk_lo": nc.dram_tensor("qk_lo", [2 * D, T], F32).ap(),
        "v": nc.dram_tensor("v_all", [T, D], F32).ap(),
        "routed": nc.dram_tensor("routed", [SLOT_TILES * P, D], F32).ap(),
        "y": nc.dram_tensor("y_all", [SLOT_TILES * P, D], F32).ap(),
        "res": nc.dram_tensor("res_all", [T, D], F32).ap(),
    }
    ctx = ExitStack()
    with ctx:
        m = Memory(nc, ctx)
        keep = {
            "o_t": m.sbuf("o_t", [P, NG, T], F32),
            "slot": m.sbuf("slot", [P, TOPK, NT], U32),
            "weight": m.sbuf("weight", [P, TOPK, NT], F32),
            "tile_expert": m.sbuf("tile_expert", [1, SLOT_TILES], I32),
        }
        with ExitStack() as until_attended:
            m = Memory(nc, until_attended)
            keep["x_rows"] = m.sbuf("x_rows", [P, NT, D], F32)
            keep["logits"] = m.sbuf("logits", [P, NT, E], F32)
            project_qkv(nc, keep, scratch, x, w_attn, bias_qk, bias_qk_pair, bias_v, gate_t, rope_cos, rope_sin,
                        rope_cos_col, rope_sin_col)
            attend(nc, keep, scratch)
        experts(nc, keep, scratch, x, w_proj, b_proj, w1_t, w2_t)
        combine(nc, keep, scratch, out)


def kernel(L0_attn_x, L0_attn_w_attn, L0_attn_b_attn, L0_attn_w_proj, L0_attn_b_proj, L0_ffn_gate_w, L0_ffn_w1, L0_ffn_w2):
    import numpy as np
    import concourse.bacc as bacc
    from concourse.bass_utils import run_bass_kernel_spmd

    half = HD // 2
    freqs = np.float32(10000.0) ** (-(np.arange(0, HD, 2, dtype=np.float32) / np.float32(HD)))
    angle = np.outer(np.arange(H, dtype=np.float32), freqs).astype(np.float32)
    cos = np.repeat(np.cos(angle).reshape(-1), 2).astype(np.float32)
    sin = (np.repeat(np.sin(angle).reshape(-1), 2) * np.tile([-1.0, 1.0], H * half)).astype(np.float32)

    def columns(v):
        return v.reshape(QK_TILES, P).T

    b = np.asarray(L0_attn_b_attn)
    b_qk = b[:2 * D]
    pair = b_qk.reshape(-1, 2)[:, ::-1].reshape(-1)
    laid_out = {
        "x": L0_attn_x, "w_attn": L0_attn_w_attn, "bias_qk": columns(b_qk), "bias_qk_pair": columns(pair),
        "bias_v": b[2 * D:], "w_proj": L0_attn_w_proj, "b_proj": L0_attn_b_proj,
        "gate_t": np.asarray(L0_ffn_gate_w).T, "w1_t": np.asarray(L0_ffn_w1).transpose(0, 2, 1),
        "w2_t": np.asarray(L0_ffn_w2).transpose(0, 2, 1), "rope_cos": cos, "rope_sin": sin,
        "rope_cos_col": columns(np.tile(cos, 2)), "rope_sin_col": columns(np.tile(sin, 2)),
    }
    nc = bacc.Bacc("TRN2", target_bir_lowering=False, num_devices=1)
    arrays, args = {}, []
    for name, value in laid_out.items():
        a = np.ascontiguousarray(value)
        arrays[f"in_{name}"] = a
        args.append(nc.dram_tensor(f"in_{name}", a.shape, mybir.dt.from_np(a.dtype), kind="ExternalInput").ap())
    args.append(nc.dram_tensor("out_0", (B, S, D), F32, kind="ExternalOutput").ap())
    attention_and_experts(nc, *args)
    r = run_bass_kernel_spmd(nc, [arrays], core_ids=[0])
    return r.results[0]["out_0"]
```

```python
import concourse.bass as bass
from concourse import mybir
from contextlib import ExitStack

F32 = mybir.dt.float32
F32R = mybir.dt.float32r
BF16 = mybir.dt.bfloat16
U32 = mybir.dt.uint32
I32 = mybir.dt.int32
ALU = mybir.AluOpType
ACT = mybir.ActivationFunctionType
AX = mybir.AxisListType

P = 128
B, S, D = 2, 1024, 512
T = B * S
H, HD = 16, 32
DK = D // P
CH = 512
NCH = T // CH
TPC = CH // P
NT = T // P
E, I, TOPK = 8, 352, 2
HG = P // HD
NG = H // HG
QK_TILES = 2 * NG
EPS = 1e-5
SCALE = float(D) ** -0.5
NEG = -3.0e38
SLOT_TILES = T * TOPK // P + E - 1
XW = D + 2
CLEARS = 5
CLEAR_TILES = -(-SLOT_TILES // (NCH * CLEARS)) * NCH * CLEARS
I_TILES = [(0, 128), (128, 128), (256, 96)]


def as_f32(ap):
    return ap.bitcast(F32)


class Memory:

    def __init__(self, nc, ctx):
        self.nc, self.ctx = nc, ctx

    def sbuf(self, name, shape, dtype):
        return self.ctx.enter_context(self.nc.sbuf_tensor(name, shape, dtype))

    def psum(self, name, shape, dtype=F32):
        return self.ctx.enter_context(self.nc.psum_tensor(name, shape, dtype))

    def sem(self, name):
        return self.ctx.enter_context(self.nc.semaphore(name))


def project_qkv(nc, keep, scratch, x, w_attn, bias_qk, bias_qk_pair, bias_v, gate_t, rope_cos, rope_sin,
                rope_cos_col, rope_sin_col):
    ctx = ExitStack()
    with ctx:
        m = Memory(nc, ctx)
        w_raw = m.sbuf("w_raw", [P, DK, 3 * D], F32)
        w_hi = m.sbuf("w_hi", [P, DK, 3 * D], F32R)
        w_lo = m.sbuf("w_lo", [P, DK, 3 * D], F32R)
        cos_row = m.sbuf("cos_row", [P, D], F32)
        sin_row = m.sbuf("sin_row", [P, D], F32)
        turned = [keep["o_t"][:, i, :].rearrange("p (k n) -> p k n", n=D) for i in range(2)]
        gate_raw = m.sbuf("gate_raw", [P, DK, E], F32)
        gate_hi = m.sbuf("gate_hi", [P, DK, E], F32R)
        gate_lo = m.sbuf("gate_lo", [P, DK, E], F32R)
        small = m.sbuf("small", [P, 8, QK_TILES], F32)
        bias_col, bias_pair, cos_col, sin_col, bias_rot, bias_tmp = (small[:, i, :] for i in range(6))
        bias_v_row = m.sbuf("bias_v_row", [P, D], F32)
        stats = m.sbuf("stats", [P, NT, 6], F32)
        mean_var = m.sbuf("mean_var", [P, NT, 2], F32)
        blank = m.sbuf("blank_row", [P, XW], F32)
        eps = m.sbuf("eps", [P, 1], F32)
        root = m.sbuf("root", [P, NT], F32)
        newton = m.sbuf("newton", [P, NT], F32)
        rstd = m.sbuf("rstd", [P, NT], F32)
        shift = m.sbuf("shift", [P, TPC], F32)
        xt_hi = m.sbuf("xt_hi", [P, DK, CH], F32R)
        xt_lo = m.sbuf("xt_lo", [P, DK, CH], F32R)
        logits_t = m.sbuf("logits_t", [P, CH], F32)
        STG = 4
        st_hi = m.sbuf("st_hi", [P, STG, CH], F32R)
        st_lo = m.sbuf("st_lo", [P, STG, CH], F32R)
        st_v = m.sbuf("st_v", [P, TPC, D], F32)
        x_raw = keep["x_rows"]
        xn = m.sbuf("xn", [P, TPC, D], F32)
        ident = m.sbuf("ident", [P, P], F32)
        iota_e = m.sbuf("iota_e", [P, E], F32)
        logits = m.sbuf("logits", [P, TPC, E], F32)
        top1 = m.sbuf("top1", [P, TPC], F32)
        shifted = m.sbuf("shifted", [P, TPC, E], F32)
        expd = m.sbuf("expd", [P, TPC, E], F32)
        denom = m.sbuf("denom", [P, 2, TPC], F32)
        prob = m.sbuf("prob", [P, TPC, E], F32)
        best = m.sbuf("best", [P, TPC, 8], F32)
        best_at = m.sbuf("best_at", [P, TPC, 8], U32)
        chosen = m.sbuf("chosen", [P, TPC, TOPK], F32)
        mask = m.sbuf("mask_c", [P, TOPK, TPC, E], F32)
        carrier = m.sbuf("carrier", [P, 1], F32)
        pair_sum = m.sbuf("pair_sum", [P, 2, TPC], F32)
        iota_done, choice = m.sem("iota_done"), m.sem("choice")
        shift_ready, expd_done = m.sem("logits_shifted"), m.sem("logits_exp_done")
        CHOICE_LINKS = 11

        RING = 6
        banks = [m.psum(f"bank{i}", [P, CH]) for i in range(RING)]
        USES = DK + 1 + TPC + QK_TILES + 1
        U_GATE, U_V, U_LT, U_QK = DK, DK + 1, DK + 1 + TPC, DK + 2 + TPC

        x0_in = [m.sem(f"x0_in{a}") for a in range(TPC)]
        x_in = [m.sem(f"x_in{c}") for c in range(NCH)]
        w_in = [m.sem(f"w_in{i}") for i in range(3)]
        rope_in = m.sem("rope_in")
        small_in = m.sem("small_in")
        gate_in = m.sem("gate_in")
        chain = m.sem("dve_chain")
        stats_done = m.sem("stats_done")
        zeros_done, blank_done = m.sem("zeros_done"), m.sem("blank_done")
        cleared = m.sem("cleared")
        eps_done = m.sem("eps_done")
        root_done = m.sem("root_done")
        rstd_done = m.sem("rstd_done")
        shift_done = m.sem("shift_done")
        xn_done = m.sem("xn_done")
        pool_chain = m.sem("pool_chain")
        ident_done = m.sem("ident_done")
        whi_done = m.sem("whi_done")
        wlo_done = m.sem("wlo_done")
        turn_done = m.sem("turn_done")
        sum_done = m.sem("sum_done")
        wqk_hi_done = m.sem("wqk_hi_done")
        wqk_done = m.sem("wqk_done")
        bias_done = m.sem("bias_done")
        bank_full = m.sem("bank_full")
        hi_done = m.sem("hi_done")
        bank_free = m.sem("bank_free")
        xn_stored = m.sem("xn_stored")
        st_free = [m.sem(f"st_free{i}") for i in range(STG)]
        v_free = [m.sem(f"v_free{a}") for a in range(TPC)]
        st_ready = m.sem("st_ready")
        v_ready = m.sem("v_ready")

        w_view = w_attn.rearrange("(k p) n -> p k n", p=P)
        x_view = x.rearrange("b (c a p) d -> (b c) p a d", p=P, a=TPC)
        qk_hi_view = scratch["qk_hi"].rearrange("(m p) t -> m p t", p=P)
        qk_lo_view = scratch["qk_lo"].rearrange("(m p) t -> m p t", p=P)
        v_view = scratch["v"].rearrange("(a p) d -> p a d", p=P)
        clear_rows = scratch["routed"].rearrange("(n j p) d -> n p j d", n=NCH * CLEARS, p=P)
        parts = [(2 * D, 3 * D), (0, D), (D, 2 * D)]
        block = ctx.enter_context(nc.Block())

        @block.sync
        def _(sp):
            sp.sem_inc(st_ready, QK_TILES)
            for s in st_free:
                sp.sem_inc(s, 32)
            for s in v_free:
                sp.sem_inc(s, 16)
            def load_x(c):
                sp.dma_start(x_raw[:, c * TPC:(c + 1) * TPC, 0:D], x_view[c]).then_inc(x_in[c], 16)

            def load_w(i):
                lo, hi = parts[i]
                sp.dma_start(w_raw[:, :, lo:hi], w_view[:, :, lo:hi]).then_inc(w_in[i], 16)

            for a in range(TPC):
                sp.dma_start(x_raw[:, a, 0:D], x_view[0][:, a, :]).then_inc(x0_in[a], 16)
            load_w(1)
            load_w(0)
            sp.wait_ge(x0_in[TPC - 1], 16)
            load_x(1)
            load_w(2)
            for c in range(2, NCH):
                load_x(c)
            with sp.Fori(0, NCH) as c:
                sp.wait_ge(xn_done, (c + 1) * TPC)
                sp.dma_start(x_raw[:, bass.ds(c * TPC, TPC), 0:D], xn[:]).then_inc(xn_stored, 16)
                for a in range(TPC):
                    sp.wait_ge(v_ready, c * TPC + (a + 1))
                    sp.dma_start(v_view[:, bass.ds(c * TPC + a, 1), :], st_v[:, a:a + 1, :]).then_inc(v_free[a], 16)
                for i in range(QK_TILES):
                    sp.wait_ge(st_ready, c * QK_TILES + (i + 1 + QK_TILES))
                    sp.dma_start(qk_hi_view[i, :, bass.ds(c * CH, CH)], as_f32(st_hi[:, i % STG, :])).then_inc(st_free[i % STG], 16)
                    sp.dma_start(qk_lo_view[i, :, bass.ds(c * CH, CH)], as_f32(st_lo[:, i % STG, :])).then_inc(st_free[i % STG], 16)
            for s in st_free:
                sp.wait_ge(s, 32 + 32 * NCH * QK_TILES // STG)
            for s in v_free:
                sp.wait_ge(s, 16 + 16 * NCH)
            sp.wait_ge(cleared, 16 * NCH * CLEARS + 16)
            sp.wait_ge(xn_stored, 16 * NCH)

        @block.gpsimd
        def _(pool):
            nc.gpsimd.iota(iota_e[:], pattern=[[1, E]], base=0, channel_multiplier=0,
                           allow_small_or_imprecise_dtypes=True).then_inc(iota_done, 1)
            pool.wait_ge(iota_done, 1)
            nc.gpsimd.memset(ident[:], 0.0).then_inc(pool_chain, 1)
            pool.wait_ge(pool_chain, 1)
            nc.gpsimd.affine_select(out=ident[:], in_=ident[:], compare_op=ALU.not_equal, fill=1.0, base=0,
                                    pattern=[[-1, P]], channel_multiplier=1).then_inc(ident_done, 1)
            pool.wait_ge(zeros_done, 1)
            nc.gpsimd.iota(blank[:, D:D + 1].bitcast(U32), pattern=[[0, 1]], base=T, channel_multiplier=1).then_inc(blank_done, 1)
            pool.wait_ge(rope_in, 32)
            sign = sin_row[:].rearrange("p (n two) -> p n two", two=2)
            for i, (lo, hi) in enumerate(parts[1:]):
                w = w_raw[:, :, lo:hi]
                pair = w.rearrange("p k (n two) -> p k n two", two=2)
                t = turned[i].rearrange("p k (n two) -> p k n two", two=2)
                pool.wait_ge(w_in[1 + i], 16)
                for k in range(DK):
                    for j in range(2):
                        last = nc.gpsimd.tensor_tensor(t[:, k, :, j], pair[:, k, :, 1 - j], sign[:, :, j], ALU.mult)
                last.then_inc(pool_chain, 1)
                pool.wait_ge(pool_chain, 2 + i)
                for k in range(DK):
                    last = nc.gpsimd.tensor_tensor(w[:, k, :], w[:, k, :], cos_row[:], ALU.mult)
                last.then_inc(turn_done, 1)
            for c in range(1, NCH):
                pool.wait_ge(rstd_done, 2)
                pool.wait_ge(bank_full, (c - 1) * USES + DK)
                pool.wait_ge(xn_stored, c * 16)
                for a in range(TPC):
                    t = c * TPC + a
                    nc.gpsimd.tensor_scalar(xn[:, a, :], x_raw[:, t, 0:D], mean_var[:, t, 0:1], rstd[:, t:t + 1],
                                            ALU.subtract, ALU.mult).then_inc(xn_done, 1)

        @block.scalar
        def _(act):
            act.dma_start(cos_row[:], rope_cos.partition_broadcast(P)).then_inc(rope_in, 16)
            act.dma_start(sin_row[:], rope_sin.partition_broadcast(P)).then_inc(rope_in, 16)
            act.dma_start(gate_raw[:], gate_t.rearrange("(k p) e -> p k e", p=P)).then_inc(gate_in, 16)
            act.dma_start(bias_v_row[:], bias_v.partition_broadcast(P)).then_inc(small_in, 16)
            act.dma_start(small[:, 0, :], bias_qk).then_inc(small_in, 16)
            act.dma_start(small[:, 1, :], bias_qk_pair).then_inc(small_in, 16)
            act.dma_start(small[:, 2, :], rope_cos_col).then_inc(small_in, 16)
            act.dma_start(small[:, 3, :], rope_sin_col).then_inc(small_in, 16)
            act.wait_ge(stats_done, 1)
            act.wait_ge(eps_done, 1)
            nc.scalar.activation(root[:, 0:TPC], mean_var[:, 0:TPC, 1], ACT.Sqrt, bias=eps[:]).then_inc(root_done, 1)
            act.wait_ge(shift_done, 1)
            for a in range(TPC // 2):
                nc.scalar.activation(xn[:, a, :], x_raw[:, a, 0:D], ACT.Identity, bias=shift[:, a:a + 1],
                                     scale=rstd[:, a:a + 1]).then_inc(xn_done, 1)
            act.wait_ge(gate_in, 16)
            nc.scalar.copy(gate_hi[:], gate_raw[:]).then_inc(whi_done, 1)
            act.wait_ge(blank_done, 1)
            act.dma_start(scratch["acc"][T:T + P, :], blank[:, 0:D]).then_inc(cleared, 16)

            def qk_high(i):
                lo, hi = parts[1 + i]
                act.wait_ge(sum_done, i + 1)
                nc.scalar.copy(w_hi[:, :, lo:hi], w_raw[:, :, lo:hi]).then_inc(wqk_hi_done, 1)

            def chunk(c):
                first = isinstance(c, int)
                for k in range(DK):
                    act.wait_ge(bank_full, c * USES + (k + 1))
                    nc.scalar.copy(xt_hi[:, k, :], banks[k % RING][:]).then_inc(hi_done, 1)
                if first:
                    act.wait_ge(w_in[0], 16)
                    nc.scalar.copy(w_hi[:, :, 2 * D:3 * D], w_raw[:, :, 2 * D:3 * D]).then_inc(whi_done, 1)
                    qk_high(0)
                    qk_high(1)
                    act.wait_ge(stats_done, NCH)
                    nc.scalar.activation(root[:, TPC:NT], mean_var[:, TPC:NT, 1], ACT.Sqrt, bias=eps[:]).then_inc(root_done, 1)
                for i in range(QK_TILES):
                    u = U_QK + i
                    act.wait_ge(bank_full, c * USES + (u + 1))
                    act.wait_ge(st_free[i % STG], c * (QK_TILES // STG * 32) + (i // STG + 1) * 32)
                    nc.scalar.activation(st_hi[:, i % STG, :], banks[u % RING][:], ACT.Identity,
                                         bias=bias_rot[:, i:i + 1]).then_inc(hi_done, 1)
                    if i < CLEARS:
                        act.dma_start(clear_rows[bass.ds(c * CLEARS + i, 1)].rearrange("o p j d -> (o p) j d"),
                                      blank[:].unsqueeze(1).to_broadcast([P, CLEAR_TILES // (NCH * CLEARS), XW])).then_inc(cleared, 16)
                    if i == 3:
                        act.wait_ge(shift_ready, c + 1)
                        nc.scalar.activation(expd[:], shifted[:], ACT.Exp).then_inc(expd_done, 1)

            chunk(0)
            with act.Fori(1, NCH) as c:
                chunk(c)

        @block.vector
        def _(dve):
            n = [0]

            def link(ins):
                n[0] += 1
                ins.then_inc(chain, 1)
                dve.wait_ge(chain, n[0])

            def invert(lo, hi, number):
                r, v, t = rstd[:, lo:hi], mean_var[:, lo:hi, 1], newton[:, lo:hi]
                dve.wait_ge(root_done, number)
                link(nc.vector.reciprocal(r, root[:, lo:hi]))
                link(nc.vector.tensor_tensor(t, r, r, ALU.mult))
                link(nc.vector.scalar_tensor_tensor(t, v, EPS, t, ALU.add, ALU.mult))
                link(nc.vector.tensor_scalar(t, t, -0.5, 1.5, ALU.mult, ALU.add))
                nc.vector.tensor_tensor(r, r, t, ALU.mult).then_inc(rstd_done, 1)
                dve.wait_ge(rstd_done, number)

            nc.vector.memset(blank[:], 0.0).then_inc(zeros_done, 1)
            link(nc.vector.memset(logits_t[:], 0.0))
            nc.vector.memset(eps[:], EPS).then_inc(eps_done, 1)
            def statistics(c):
                if c:
                    dve.wait_ge(x_in[c], 16)
                for a in range(TPC):
                    if c == 0:
                        dve.wait_ge(x0_in[a], 16)
                    last = nc.vector.bn_stats(stats[:, c * TPC + a, :], x_raw[:, c * TPC + a, 0:D])
                link(last)
                for a in range(TPC):
                    last = nc.vector.bn_aggr(mean_var[:, c * TPC + a, :], stats[:, c * TPC + a, :])
                last.then_inc(stats_done, 1)

            def qk_sum(i):
                w = w_raw[:, :, parts[1 + i][0]:parts[1 + i][1]]
                dve.wait_ge(turn_done, i + 1)
                nc.vector.tensor_tensor(w, w, turned[i], ALU.add).then_inc(sum_done, 1)

            def qk_low(i):
                lo, hi = parts[1 + i]
                dve.wait_ge(wqk_hi_done, i + 1)
                nc.vector.tensor_tensor(w_lo[:, :, lo:hi], w_raw[:, :, lo:hi], as_f32(w_hi[:, :, lo:hi]), ALU.subtract).then_inc(wqk_done, 1)

            statistics(0)
            invert(0, TPC, 1)
            nc.vector.scalar_tensor_tensor(shift[:], mean_var[:, 0:TPC, 0], -1.0, rstd[:, 0:TPC],
                                           ALU.mult, ALU.mult).then_inc(shift_done, 1)
            for a in range(TPC // 2, TPC):
                nc.vector.tensor_scalar(xn[:, a, :], x_raw[:, a, 0:D], mean_var[:, a, 0:1], rstd[:, a:a + 1],
                                        ALU.subtract, ALU.mult).then_inc(xn_done, 1)
            dve.wait_ge(whi_done, 1)
            nc.vector.tensor_tensor(gate_lo[:], gate_raw[:], as_f32(gate_hi[:]), ALU.subtract).then_inc(wlo_done, 1)

            def link_in_chunk(c, number, ins):
                ins.then_inc(choice, 1)
                dve.wait_ge(choice, c * CHOICE_LINKS + (number + 1))

            def per_token(ap):
                return ap.unsqueeze(2).to_broadcast([P, TPC, E])

            def shift_logits(c):
                dve.wait_ge(bank_free, c * (DK + 2) + (DK + 2))
                link_in_chunk(c, 0, nc.vector.tensor_reduce(top1[:], logits[:], AX.X, ALU.max))
                nc.vector.tensor_tensor(shifted[:], logits[:], per_token(top1[:]), ALU.subtract).then_inc(shift_ready, 1)

            def choose(c):
                V = nc.vector
                n = iter(range(1, CHOICE_LINKS))
                dve.wait_ge(expd_done, c + 1)
                link_in_chunk(c, next(n), V.tensor_reduce(denom[:, 0, :], expd[:], AX.X, ALU.add))
                link_in_chunk(c, next(n), V.reciprocal(denom[:, 1, :], denom[:, 0, :]))
                link_in_chunk(c, next(n), V.tensor_tensor(prob[:], expd[:], per_token(denom[:, 1, :]), ALU.mult))
                V.tensor_copy(carrier[:], prob[:, 0, 0:1])
                for a in range(TPC):
                    last = V.max(best[:, a, :], prob[:, a, :])
                link_in_chunk(c, next(n), last)
                V.tensor_copy(carrier[:], best[:, 0, 0:1])
                for a in range(TPC):
                    last = V.max_index(best_at[:, a, :], best[:, a, :], prob[:, a, :])
                link_in_chunk(c, next(n), last)
                link_in_chunk(c, next(n), V.tensor_copy(chosen[:], best_at[:, :, 0:TOPK]))
                for j in range(TOPK):
                    last = V.tensor_tensor(mask[:, j], iota_e[:].unsqueeze(1).to_broadcast([P, TPC, E]),
                                           per_token(chosen[:, :, j]), ALU.is_equal)
                link_in_chunk(c, next(n), last)
                tiles = bass.ds(c * TPC, TPC)
                V.tensor_tensor(keep["both"][:, tiles, :], mask[:, 0], mask[:, 1], ALU.add)
                for j in range(TOPK):
                    V.tensor_copy(keep["mask"][:, j, tiles, :], mask[:, j])
                link_in_chunk(c, next(n), V.tensor_tensor(pair_sum[:, 0, :], best[:, :, 0], best[:, :, 1], ALU.add))
                link_in_chunk(c, next(n), V.reciprocal(pair_sum[:, 1, :], pair_sum[:, 0, :]))
                for j in range(TOPK):
                    last = V.tensor_tensor(keep["weight"][:, j, tiles], best[:, :, j], pair_sum[:, 1, :], ALU.mult)
                link_in_chunk(c, next(n), last)
                assert next(n, None) is None

            dve.wait_ge(iota_done, 1)

            def chunk(c):
                first = isinstance(c, int)
                HI = DK + QK_TILES
                for k in range(DK):
                    dve.wait_ge(hi_done, c * HI + (k + 1))
                    nc.vector.tensor_tensor(xt_lo[:, k, :], banks[k % RING][:], as_f32(xt_hi[:, k, :]),
                                            ALU.subtract).then_inc(bank_free, 1)
                if first:
                    dve.wait_ge(whi_done, 2)
                    nc.vector.tensor_tensor(w_lo[:, :, 2 * D:3 * D], w_raw[:, :, 2 * D:3 * D], as_f32(w_hi[:, :, 2 * D:3 * D]),
                                            ALU.subtract).then_inc(wlo_done, 1)
                u = U_GATE
                dve.wait_ge(bank_full, c * USES + (u + 1))
                nc.vector.tensor_copy(logits_t[0:E, :], banks[u % RING][0:E, :]).then_inc(bank_free, 1)
                if first:
                    dve.wait_ge(small_in, 80)
                    link(nc.vector.tensor_tensor(bias_tmp, bias_pair, sin_col, ALU.mult))
                    link(nc.vector.tensor_tensor(bias_rot, bias_col, cos_col, ALU.mult))
                    nc.vector.tensor_tensor(bias_rot, bias_rot, bias_tmp, ALU.add).then_inc(bias_done, 1)
                    dve.wait_ge(bias_done, 1)
                    qk_sum(0)
                    statistics(1)
                for a in range(TPC):
                    u = U_V + a
                    dve.wait_ge(bank_full, c * USES + (u + 1))
                    dve.wait_ge(v_free[a], c * 16 + 16)
                    nc.vector.tensor_tensor(st_v[:, a, :], banks[u % RING][:], bias_v_row[:], ALU.add).then_inc(v_ready, 1)
                    if first and a == 0:
                        qk_low(0)
                    if first and a == 1:
                        statistics(2)
                    if first and a == 2:
                        qk_sum(1)
                    if first and a == 3:
                        statistics(3)
                u = U_LT
                dve.wait_ge(bank_full, c * USES + (u + 1))
                nc.vector.tensor_copy(logits[:], banks[u % RING][:].rearrange("p (a q) -> p a q", q=P)[:, :, 0:E]).then_inc(bank_free, 1)
                if first:
                    invert(TPC, NT, 2)
                for i in range(QK_TILES):
                    u = U_QK + i
                    dve.wait_ge(hi_done, c * HI + (DK + i + 1))
                    nc.vector.scalar_tensor_tensor(st_lo[:, i % STG, :], banks[u % RING][:], bias_rot[:, i:i + 1],
                                                   as_f32(st_hi[:, i % STG, :]), ALU.add, ALU.subtract).then_inc(st_ready, 1)
                    if first and i == 0:
                        qk_low(1)
                    if i == 1:
                        shift_logits(c)
                    if i == 4:
                        choose(c)

            chunk(0)
            with dve.Fori(1, NCH) as c:
                chunk(c)

        @block.tensor
        def _(pe):
            reads = ([(bank_free, DK + 2, k + 1) for k in range(DK)] + [(bank_free, DK + 2, DK + 1)]
                     + [(v_ready, TPC, a + 1) for a in range(TPC)] + [(bank_free, DK + 2, DK + 2)]
                     + [(st_ready, QK_TILES, i + 1) for i in range(QK_TILES)])

            def claim(c, u):
                if u >= RING:
                    sem, per, number = reads[u - RING]
                    pe.wait_ge(sem, c * per + (number + (QK_TILES if sem is st_ready else 0)))
                else:
                    pe.wait_ge(st_ready, c * QK_TILES + (QK_TILES - RING + u + 1))

            def split_product(out, a_hi, a_lo, b_hi, b_lo, chunk=None):
                for k in range(DK):
                    if chunk is not None:
                        pe.wait_ge(bank_free, chunk * (DK + 2) + (k + 1))
                    nc.tensor.matmul(out, a_hi(k), b_hi(k), start=(k == 0), stop=False)
                    nc.tensor.matmul(out, a_hi(k), b_lo(k), start=False, stop=False)
                    last = nc.tensor.matmul(out, a_lo(k), b_hi(k), start=False, stop=(k == DK - 1))
                return last

            pe.wait_ge(ident_done, 1)
            with pe.Fori(0, NCH) as c:
                pe.wait_ge(xn_done, (c + 1) * TPC)
                for k in range(DK):
                    claim(c, k)
                    for a in range(TPC):
                        last = nc.tensor.transpose(banks[k % RING][:, a * P:(a + 1) * P], xn[:, a, k * P:(k + 1) * P], ident[:])
                    last.then_inc(bank_full, 1)
                pe.wait_ge(wlo_done, 1)
                u = U_GATE
                claim(c, u)
                split_product(banks[u % RING][0:E, :], lambda k: gate_hi[:, k, :], lambda k: gate_lo[:, k, :],
                              lambda k: xt_hi[:, k, :], lambda k: xt_lo[:, k, :], c).then_inc(bank_full, 1)
                pe.wait_ge(wlo_done, 2)
                for a in range(TPC):
                    u = U_V + a
                    claim(c, u)
                    split_product(banks[u % RING][:], lambda k: xt_hi[:, k, a * P:(a + 1) * P],
                                  lambda k: xt_lo[:, k, a * P:(a + 1) * P], lambda k: w_hi[:, k, 2 * D:3 * D],
                                  lambda k: w_lo[:, k, 2 * D:3 * D]).then_inc(bank_full, 1)
                u = U_LT
                claim(c, u)
                pe.wait_ge(bank_free, c * (DK + 2) + (DK + 1))
                for a in range(TPC):
                    last = nc.tensor.transpose(banks[u % RING][:, a * P:(a + 1) * P], logits_t[:, a * P:(a + 1) * P], ident[:])
                last.then_inc(bank_full, 1)
                for i in range(QK_TILES):
                    u = U_QK + i
                    if i % NG == 0:
                        pe.wait_ge(wqk_done, i // NG + 1)
                    claim(c, u)
                    split_product(banks[u % RING][:], lambda k: w_hi[:, k, i * P:(i + 1) * P],
                                  lambda k: w_lo[:, k, i * P:(i + 1) * P], lambda k: xt_hi[:, k, :],
                                  lambda k: xt_lo[:, k, :]).then_inc(bank_full, 1)


def route(nc, m, keep, count_banks):
    rank_ps, total_ps = count_banks
    iota_rows = m.sbuf("iota_rows", [P, NT], F32)
    iota_tile = m.sbuf("iota_tile", [1, SLOT_TILES], F32)
    before = m.sbuf("before", [P, P], BF16)
    ones = m.sbuf("ones16", [P, P], BF16)
    mask, both = keep["mask"], keep["both"]
    prefix = [m.sbuf(f"prefix{i}", [P, NT // 2 + NT, E], F32) for i in range(2)]
    over = m.sbuf("over", [P, E, NT], F32)
    tiles = m.sbuf("tiles", [P, E], F32)
    upto = m.sbuf("upto", [P, E], F32)
    base = m.sbuf("base", [P, E], F32)
    place = m.sbuf("place", [P, NT, E], F32)
    picked = m.sbuf("picked", [P, TOPK, NT, E], F32)
    slot_f = m.sbuf("slot_f", [P, TOPK, NT], F32)
    passed = m.sbuf("passed", [1, SLOT_TILES, E], F32)
    owner = m.sbuf("owner", [1, 2, SLOT_TILES], F32)
    consts, pool_chain = m.sem("consts_r"), m.sem("pool_chain_r")
    chain, counted = m.sem("chain_r"), m.sem("counted")
    route_done = m.sem("route_done")

    def pool_part(pool):
        nc.gpsimd.iota(iota_rows[:], pattern=[[P, NT]], base=0, channel_multiplier=0,
                       allow_small_or_imprecise_dtypes=True).then_inc(consts, 1)
        nc.gpsimd.iota(iota_tile[:], pattern=[[1, SLOT_TILES]], base=0, channel_multiplier=0,
                       allow_small_or_imprecise_dtypes=True).then_inc(consts, 1)
        pool.wait_ge(consts, 2)
        nc.gpsimd.memset(ones[:], 1.0).then_inc(consts, 1)
        nc.gpsimd.memset(before[:], 0.0).then_inc(pool_chain, 1)
        pool.wait_ge(pool_chain, 1)
        nc.gpsimd.affine_select(out=before[:], in_=before[:], compare_op=ALU.is_ge, fill=1.0, base=0,
                                pattern=[[-1, P]], channel_multiplier=1).then_inc(consts, 1)

    def pe_part(pe):
        pe.wait_ge(consts, 4)
        rows = both[:].rearrange("p a e -> p (a e)")
        nc.tensor.matmul(rank_ps[:, 0:NT * E], before[:], rows, start=True, stop=True).then_inc(counted, 1)
        nc.tensor.matmul(total_ps[:, 0:NT * E], ones[:], rows, start=True, stop=True).then_inc(counted, 1)

    def dve_part(dve):
        n = [0]

        def link(ins):
            n[0] += 1
            ins.then_inc(chain, 1)
            dve.wait_ge(chain, n[0])

        V = nc.vector

        for b in prefix:
            link(V.memset(b[:, 0:NT // 2, :], 0.0))
        dve.wait_ge(consts, 4)
        dve.wait_ge(counted, 2)
        link(V.tensor_copy(prefix[0][:, NT // 2:, :], total_ps[:, 0:NT * E].rearrange("p (a e) -> p a e", e=E)))
        at, step = 0, 1
        while step < NT:
            now, then = prefix[1 - at], prefix[at]
            link(V.tensor_tensor(now[:, NT // 2:, :], then[:, NT // 2:, :], then[:, NT // 2 - step:NT // 2 - step + NT, :], ALU.add))
            at, step = 1 - at, 2 * step
        upto_tile = prefix[at][:, NT // 2:, :]
        before_tile = prefix[at][:, NT // 2 - 1:NT // 2 - 1 + NT, :]
        link(V.tensor_tensor(over[:], upto_tile[:, NT - 1, :].unsqueeze(2).to_broadcast([P, E, NT]),
                             iota_rows[:].unsqueeze(1).to_broadcast([P, E, NT]), ALU.is_gt))
        link(V.tensor_reduce(tiles[:], over[:], AX.X, ALU.add))
        link(V.tensor_copy(upto[:, 0:1], tiles[:, 0:1]))
        for e in range(1, E):
            link(V.tensor_tensor(upto[:, e:e + 1], upto[:, e - 1:e], tiles[:, e:e + 1], ALU.add))
        link(V.tensor_tensor(base[:], upto[:], tiles[:], ALU.subtract))
        link(V.scalar_tensor_tensor(place[:], base[:].unsqueeze(1).to_broadcast([P, NT, E]), float(P),
                                    before_tile, ALU.mult, ALU.add))
        link(V.tensor_tensor(place[:], rank_ps[:, 0:NT * E].rearrange("p (a e) -> p a e", e=E), place[:], ALU.add))
        for j in range(TOPK):
            last = V.tensor_tensor(picked[:, j], mask[:, j], place[:], ALU.mult)
        link(last)
        link(V.tensor_reduce(slot_f[:].rearrange("p j a -> p (j a)"), picked[:].rearrange("p j a e -> p (j a) e"), AX.X, ALU.add))
        V.tensor_copy(keep["slot"][:], slot_f[:])
        link(V.tensor_tensor(passed[:], upto[0:1, :].unsqueeze(1).to_broadcast([1, SLOT_TILES, E]),
                             iota_tile[:].unsqueeze(2).to_broadcast([1, SLOT_TILES, E]), ALU.is_le))
        link(V.tensor_reduce(owner[:, 0, :], passed[:], AX.X, ALU.add))
        link(V.tensor_scalar(owner[:, 1, :], owner[:, 0, :], float(E - 1), None, ALU.min))
        V.tensor_copy(keep["tile_expert"][:], owner[:, 1, :]).then_inc(route_done, 1)

    return pool_part, pe_part, dve_part, route_done


def experts(nc, keep, scratch, x, b_proj, w1_t, w2_t, out):
    ctx = ExitStack()
    with ctx:
        m = Memory(nc, ctx)
        o_t, tile_expert = keep["o_t"], keep["tile_expert"]
        w1 = m.sbuf("w1", [P, E, DK, 2 * I], F32)
        w2 = m.sbuf("w2", [P, E, len(I_TILES), D], F32)
        wp = keep["w_proj"]
        bp = m.sbuf("bp", [P, D], F32)
        ident = m.sbuf("ident3", [P, P], F32)
        RES = 4
        res = m.sbuf("res", [P, RES, D], F32)
        rows = m.sbuf("rows", [P, 2, D], F32)
        rows_t = [m.sbuf(f"rows_t{r}", [P, D], F32) for r in range(2)]
        gated = m.sbuf("gated", [P, I], F32)
        hidden = [m.sbuf(f"hidden{r}", [P, I], F32) for r in range(2)]
        hidden_t = [m.sbuf(f"hidden_t{r}", [P, len(I_TILES), P], F32) for r in range(2)]
        y = m.sbuf("y", [P, 2, D], F32)
        tag = m.sbuf("tag", [P, 2, XW - D], F32)
        carrier = m.sbuf("carrier_y", [P, 2], F32)
        gu = [[m.psum(f"gu{r}{j}", [P, CH]) for j in range(2)] for r in range(2)]
        turn_ps, hid_ps = m.psum("turn_ps", [P, CH]), m.psum("hid_ps", [P, CH])
        down = [m.psum(f"down{r}", [P, CH]) for r in range(2)]

        ident_done, pool_chain = m.sem("ident3_done"), m.sem("pool_chain3")
        bp_in, weights_in = m.sem("bp_in"), [m.sem(f"weights_in{e}") for e in range(E)]
        expert_ready = m.sem("expert_ready")
        res_in = [m.sem(f"res_in{r}") for r in range(RES)]
        biased, proj_full, res_done = m.sem("biased"), m.sem("proj_full"), m.sem("res_done")
        rows_in = [m.sem(f"rows_in{r}") for r in range(2)]
        tag_in = [m.sem(f"tag_in{r}") for r in range(2)]
        acc_started, added, stored = m.sem("acc_started"), m.sem("added"), m.sem("stored")
        carried = m.sem("carried")
        turned, turned_read = m.sem("rows_turned"), m.sem("rows_t_done")
        gu_full, silu_done, hidden_done = m.sem("gu_full"), m.sem("silu_done"), m.sem("hidden_done")
        hid_turned, hid_read = m.sem("hid_turned"), m.sem("hid_t_done")
        y_full, y_read = m.sem("y_full"), m.sem("y_read")

        x_rows = x.rearrange("b (a p) d -> (b a) p d", p=P)
        in_rows = scratch["routed"].rearrange("(a p) d -> a p d", p=P)
        acc_rows = scratch["acc"][0:T, :].rearrange("(a p) (g t) -> a p g t", p=P, t=P)
        block = ctx.enter_context(nc.Block())

        def run_tiles(engine, tile, start=0):
            for i in range(start, 4):
                tile(i, i % 2, i // 2)
            with engine.Fori(2, (SLOT_TILES - 1) // 2) as pairs:
                tile(pairs * 2, 0, pairs)
                tile(pairs * 2 + 1, 1, pairs)
            tile(SLOT_TILES - 1, 0, (SLOT_TILES - 1) // 2)

        def past(i, least):
            return not isinstance(i, int) or i >= least

        def early(i):
            return isinstance(i, int) and i < 2

        @block.sync
        def _(sp):
            def tile(i, r, half):
                if not early(i):
                    sp.wait_ge(turned, i - 1)
                sp.dma_start(rows[:, r:r + 1, :], in_rows[bass.ds(i, 1), :, 0:D].rearrange("a p d -> p a d")).then_inc(rows_in[r], 16)

            tile(0, 0, 0)
            tile(1, 1, 0)
            for a in range(NT + RES - 1):
                if a < NT:
                    sp.dma_start(res[:, a % RES, :], x_rows[a]).then_inc(res_in[a % RES], 16)
                if a >= RES - 1:
                    done = a - (RES - 1)
                    sp.wait_ge(res_done, done + 1)
                    sp.dma_start(acc_rows[done], o_t[:, :, done * P:(done + 1) * P]).then_inc(acc_started, 16)
            run_tiles(sp, tile, 2)
            sp.wait_ge(added, 16 * SLOT_TILES)
            for b in range(B):
                sp.dma_start(out[b], scratch["acc"][b * S:(b + 1) * S, :]).then_inc(stored, 16)
            sp.wait_ge(stored, 16 * B)

        @block.gpsimd
        def _(pool):
            nc.gpsimd.memset(ident[:], 0.0).then_inc(pool_chain, 1)
            pool.wait_ge(pool_chain, 1)
            nc.gpsimd.affine_select(out=ident[:], in_=ident[:], compare_op=ALU.not_equal, fill=1.0, base=0,
                                    pattern=[[-1, P]], channel_multiplier=1).then_inc(ident_done, 1)
            pool.wait_ge(bp_in, 16)
            for a in range(NT):
                pool.wait_ge(res_in[a % RES], 16 * (a // RES + 1))
                nc.gpsimd.tensor_tensor(res[:, a % RES, :], res[:, a % RES, :], bp[:], ALU.add).then_inc(biased, 1)

            for e in range(E):
                pool.wait_ge(weights_in[e], 3 * 16)
                pool.sem_inc(expert_ready, 1)

            def load_tag(i, r):
                pool.dma_start(tag[:, r:r + 1, :], in_rows[bass.ds(i, 1), :, D:XW].rearrange("a p d -> p a d")).then_inc(tag_in[r], 16)

            def tile(i, r, half):
                pool.wait_ge(y_read, i + 1)
                if past(i, 1):
                    pool.wait_ge(added, i * 16)
                if past(i, 2):
                    pool.wait_ge(carried, i - 1)
                nc.gpsimd.tensor_tensor(carrier[:, r:r + 1], ident[:, 0:1], ident[:, 0:1], ALU.mult).then_inc(carried, 1)
                pool.indirect_dma_start(out=scratch["acc"], out_offset=bass.IndirectOffsetOnAxis(
                    ap=tag[:, r, 0:1].bitcast(U32), axis=0), in_=y[:, r, :], in_offset=None, compute_op=ALU.add).then_inc(added, 16)
                if not (isinstance(i, int) and i == SLOT_TILES - 1):
                    load_tag(i + 1, 1 - r)

            load_tag(0, 0)
            pool.wait_ge(acc_started, 16 * NT)
            run_tiles(pool, tile)
            pool.wait_ge(added, 16 * SLOT_TILES)

        @block.scalar
        def _(act):
            act.dma_start(bp[:], b_proj.partition_broadcast(P)).then_inc(bp_in, 16)
            def rows_to_sbuf(i, r):
                act.wait_ge(turned, i + 1)
                if not early(i):
                    act.wait_ge(gu_full, 2 * (i - 1))
                nc.scalar.copy(rows_t[r][:], turn_ps[:]).then_inc(turned_read, 1)

            def y_to_sbuf(i, r, half):
                act.wait_ge(y_full, i + 1)
                act.wait_ge(tag_in[r], half * 16 + 16)
                if not early(i):
                    act.wait_ge(added, i * 16 - 16)
                nc.scalar.activation(y[:, r, :], down[r][:], ACT.Copy, scale=tag[:, r, 1:2]).then_inc(y_read, 1)

            def tile(i, r, half):
                if past(i, 2):
                    y_to_sbuf(i - 2, r, half - 1)
                act.wait_ge(gu_full, i * 2 + 1)
                if past(i, 1):
                    act.wait_ge(hidden_done, i)
                nc.scalar.activation(gated[:], gu[r][0][:, 0:I], ACT.Silu).then_inc(silu_done, 1)
                if not (isinstance(i, int) and i == SLOT_TILES - 1):
                    rows_to_sbuf(i + 1, 1 - r)

            for e in range(E):
                if e:
                    act.wait_ge(res_done, min(3 * e - 1, NT))
                if e == E - 2:
                    rows_to_sbuf(0, 0)
                act.dma_start(w1[:, e], w1_t[e].rearrange("(k p) n -> p k n", p=P)).then_inc(weights_in[e], 16)
                act.dma_start(w2[:, e, 0:2, :], w2_t[e, 0:2 * P, :].rearrange("(k p) n -> p k n", p=P)).then_inc(weights_in[e], 16)
                act.dma_start(w2[0:I - 2 * P, e, 2, :], w2_t[e, 2 * P:I, :]).then_inc(weights_in[e], 16)
            run_tiles(act, tile)
            y_to_sbuf(SLOT_TILES - 2, 1, (SLOT_TILES - 2) // 2)
            y_to_sbuf(SLOT_TILES - 1, 0, (SLOT_TILES - 1) // 2)

        @block.vector
        def _(dve):
            for a in range(NT):
                dve.wait_ge(proj_full, a + 1)
                dve.wait_ge(biased, a + 1)
                nc.vector.tensor_tensor(o_t[:, :, a * P:(a + 1) * P], gu[a % 2][0][:].rearrange("p (g t) -> p g t", t=P),
                                        res[:, a % RES, :].rearrange("p (g t) -> p g t", t=P), ALU.add).then_inc(res_done, 1)

            def hidden_to_sbuf(i, r):
                dve.wait_ge(hid_turned, i + 1)
                if not early(i):
                    dve.wait_ge(y_full, i - 1)
                nc.vector.tensor_copy(hidden_t[r][:, 0:2, :], hid_ps[:, 0:2 * P].rearrange("p (k t) -> p k t", t=P))
                nc.vector.tensor_copy(hidden_t[r][0:I - 2 * P, 2, :], hid_ps[0:I - 2 * P, 2 * P:3 * P]).then_inc(hid_read, 1)

            def tile(i, r, half):
                if not (isinstance(i, int) and i == 0):
                    hidden_to_sbuf(i - 1, 1 - r)
                dve.wait_ge(silu_done, i + 1)
                dve.wait_ge(gu_full, i * 2 + 2)
                if not early(i):
                    dve.wait_ge(hid_turned, i - 1)
                nc.vector.tensor_tensor(hidden[r][:], gu[r][1][:, 0:I], gated[:], ALU.mult).then_inc(hidden_done, 1)

            run_tiles(dve, tile)
            hidden_to_sbuf(SLOT_TILES - 1, 0)

        @block.tensor
        def _(pe):
            def turn_rows(i, r, half):
                pe.wait_ge(rows_in[r], (half + 1) * 16)
                if not (isinstance(i, int) and i == 0):
                    pe.wait_ge(turned_read, i)
                for k in range(DK):
                    last = nc.tensor.transpose(turn_ps[:, k * P:(k + 1) * P], rows[:, r, k * P:(k + 1) * P], ident[:])
                last.then_inc(turned, 1)

            def up(i, r, e, j):
                for k in range(DK):
                    last = nc.tensor.matmul(gu[r][j][:, 0:I], rows_t[r][:, k * P:(k + 1) * P],
                                            w1[:, bass.ds(e, 1), k, j * I:(j + 1) * I].rearrange("p o n -> p (o n)"),
                                            start=(k == 0), stop=(k == DK - 1))
                last.then_inc(gu_full, 1)

            def turn_hidden(i, r):
                pe.wait_ge(hidden_done, i + 1)
                if not (isinstance(i, int) and i == 0):
                    pe.wait_ge(hid_read, i)
                for k, (at, n) in enumerate(I_TILES):
                    last = nc.tensor.transpose(hid_ps[0:n, k * P:(k + 1) * P], hidden[r][:, at:at + n], ident[:])
                last.then_inc(hid_turned, 1)

            def down_product(i, r, e):
                pe.wait_ge(hid_read, i + 1)
                if not early(i):
                    pe.wait_ge(y_read, i - 1)
                for k, (at, n) in enumerate(I_TILES):
                    last = nc.tensor.matmul(down[r][:], hidden_t[r][0:n, k, :],
                                            w2[0:n, bass.ds(e, 1), k, :].rearrange("p o n -> p (o n)"),
                                            start=(k == 0), stop=(k == len(I_TILES) - 1))
                last.then_inc(y_full, 1)

            def expert_of(i):
                return pe.value_load(tile_expert[0:1, bass.ds(i, 1)], min_val=0, max_val=E - 1)

            def tile(i, r, half):
                if past(i, 2):
                    before = expert_of(i - 2)
                e = expert_of(i)
                if past(i, 2):
                    down_product(i - 2, r, before)
                pe.wait_ge(turned_read, i + 1)
                if past(i, 2):
                    pe.wait_ge(hidden_done, i - 1)
                else:
                    pe.wait_ge(res_done, NT - 1 + i)
                pe.wait_ge(expert_ready, e + 1)
                up(i, r, e, 0)
                if past(i, 1):
                    turn_hidden(i - 1, 1 - r)
                if not (isinstance(i, int) and i == SLOT_TILES - 1):
                    turn_rows(i + 1, 1 - r, half if r == 0 else half + 1)
                up(i, r, e, 1)

            pe.wait_ge(ident_done, 1)
            for a in range(NT):
                if a >= 2:
                    pe.wait_ge(res_done, a - 1)
                if a == NT - 1:
                    turn_rows(0, 0, 0)
                for g in range(NG):
                    last = nc.tensor.matmul(gu[a % 2][0][:], o_t[:, g, a * P:(a + 1) * P], wp[:, g, :],
                                            start=(g == 0), stop=(g == NG - 1))
                last.then_inc(proj_full, 1)
            run_tiles(pe, tile)
            down_product(SLOT_TILES - 2, 1, expert_of(SLOT_TILES - 2))
            turn_hidden(SLOT_TILES - 1, 0)
            down_product(SLOT_TILES - 1, 0, expert_of(SLOT_TILES - 1))


def attend(nc, keep, scratch, w_proj):
    PAIR = 2
    PAIRS = HG // PAIR
    SETS = B * PAIRS
    ROUNDS = NG * SETS
    TQ = S // P
    NC = S // CH
    STACK = 3 * HD + 2
    steps = [(c, j) for c in range(NC) for j in range((c + 1) * TPC)]
    NS = len(steps)
    units = [(h, i, c) for h in range(PAIR) for i in range(TQ) for c in range(i // TPC + 1)]
    NU = len(units)
    PER = NU // NS
    LEAD = 1
    RING = 3
    TURN_STEP = 2
    TURN_AT = TURN_STEP * PER
    TURN_BANK = TURN_AT % RING

    def place(u):
        return u + (u >= TURN_AT)

    def bank_at(at):
        return 1 if at == NU else at % RING

    def bank_before(at, turned):
        back, bank = 0, bank_at(at)
        while True:
            at -= 1
            if at < 0:
                back, at = back + 1, NU
            if bank_at(at) == bank and (turned or at != TURN_AT):
                return back, at

    ctx = ExitStack()
    with ctx:
        m = Memory(nc, ctx)
        q_st = [m.sbuf(f"q_stack{i}", [P, PAIR, S], F32R) for i in range(SETS)]
        k_st = [m.sbuf(f"k_stack{i}", [P, PAIR, S], F32R) for i in range(SETS)]
        v_st = [m.sbuf(f"v_ones{i}", [P, TQ, PAIR, 2 * HD], F32) for i in range(SETS)]
        PR = 4
        probs = m.sbuf("probs", [P, PR, PAIR, CH], F32)
        o_raw = m.sbuf("o_raw", [P, NC, CH], F32)
        sums = m.sbuf("sums", [P, NC, CH], F32)
        inv = m.sbuf("inv", [P, NC, CH], F32)
        mx = [m.sbuf(f"mx{i}", [P, PAIR, TQ], F32) for i in range(2)]
        mx_far = m.sbuf("mx_far", [P, PAIR, TQ - TPC], F32)
        row_hi = m.sbuf("row_hi", [PAIR * TQ, P], F32R)
        row_lo = m.sbuf("row_lo", [PAIR * TQ, P], F32R)
        ident = m.sbuf("ident2", [P, P], F32)
        ident16 = m.sbuf("ident16", [P, P], BF16)
        mask_m = m.sbuf("mask_m", [P, P], BF16)
        mask_t = m.sbuf("mask_t", [P, P], BF16)
        carrier = m.sbuf("carrier_p", [P, SETS * NS], F32)
        o_t = keep["o_t"]

        scores_t = [m.psum(f"scores_t{r}", [P, CH]) for r in range(RING)]
        o_acc = [m.psum(f"o_acc{c}", [P, CH]) for c in range(NC)]
        mb = [m.psum(f"maxima{r}", [P, CH]) for r in range(RING)]

        scattered = m.sem("scattered")
        w_proj_in = m.sem("w_proj_in")
        numbered, weighted = m.sem("rows_numbered"), m.sem("rows_weighted")
        masked, v_ones = m.sem("probs_masked"), m.sem("v_ones")
        blank, consts, minus_ones = m.sem("blank"), m.sem("consts"), m.sem("minus_ones")
        loaded = [m.sem(f"stack_in{i}") for i in range(SETS)]
        row_in = m.sem("row_in")
        m_full = m.sem("m_full")
        m_free = m.sem("m_free")
        mx_done, turned = m.sem("mx_done"), m.sem("mx_turned")
        row_hi_done, row_lo_done = m.sem("row_hi_done"), m.sem("row_lo_done")
        st_full = m.sem("st_full")
        exp_done = m.sem("exp_done")
        pv_done = m.sem("pv_done")
        o_read = m.sem("o_read")
        norm_done = m.sem("norm_done")
        inv_done = m.sem("inv_done")
        PIECES = 8
        LOADS = 6 + PAIR
        NORMS = NC * PIECES

        def stack_rows(name):
            return scratch[name].rearrange("(r h d) t -> r d h t", r=2, d=HD)

        v_rows = scratch["v"].rearrange("(a p) (h d) -> h p a d", p=P, d=HD)
        route_pool, route_pe, route_dve, route_done = route(nc, m, keep, scores_t[0:2])
        block = ctx.enter_context(nc.Block())

        def run_rounds(engine, round_):
            round_(0, 0, 0)
            with engine.Fori(0, NG - 1) as g:
                for s in range(1, SETS + 1):
                    round_(g * SETS + s, s % SETS, g + s // SETS)
            for s in range(1, SETS):
                round_((NG - 1) * SETS + s, s, NG - 1)

        def below(n, number):
            return n < number if isinstance(n, int) else number > 1

        PW = CH // PIECES
        NORM_FROM = TPC + 3
        LAG = 1
        NORM_LATE = NS - NORM_FROM

        def norm_number(n, c, q):
            return (n - 1) * (NORMS // PAIRS) + (c * PIECES + q + 1)

        def norm_at(n, i, g, k, norm):
            if isinstance(n, int) and n == ROUNDS - 1:
                for q in range(2 * (k - NORM_FROM), 2 * (k - NORM_FROM) + 2):
                    if 0 <= q < PIECES:
                        norm(n, i, g, 0, q)
            elif i % PAIRS == PAIRS - 1:
                if k >= NORM_FROM:
                    norm(n, i, g, 0, k - NORM_FROM)
            elif not (isinstance(n, int) and n == 0):
                c, q = divmod(k + NORM_LATE, PIECES)
                if c < NC:
                    norm(n - 1, (i - 1) % SETS, g - (i == 0), c, q)

        diagonals = [k for k, (c, j) in enumerate(steps) if j >= c * TPC]

        def diagonal(k):
            return k in diagonals

        @block.sync
        def _(sp):
            for s, n in ((exp_done, RING), (pv_done, PR), (o_read, NC), (norm_done, NORMS)):
                sp.sem_inc(s, n)

            def load(i, g):
                b, pair = i // PAIRS, i % PAIRS
                toks = slice(b * S, (b + 1) * S)
                for part, r, (hi0, hi1, lo) in ((q_st[i], 0, (0, 2, 1)), (k_st[i], 1, (0, 1, 2))):
                    for at, name in ((hi0, "qk_hi"), (lo, "qk_lo"), (hi1, "qk_hi")):
                        sp.dma_start(as_f32(part[at * HD:(at + 1) * HD, :, :]),
                                     stack_rows(name)[r, :, bass.ds(g * HG + pair * PAIR, PAIR), toks]).then_inc(loaded[i], 16)
                for h in range(PAIR):
                    src = v_rows[bass.ds(g * HG + pair * PAIR + h, 1), :, b * TQ:(b + 1) * TQ, :]
                    sp.dma_start(v_st[i][:, :, h, 0:HD], src.rearrange("o p a d -> (o p) a d")).then_inc(loaded[i], 16)

            def rows(n, i):
                sp.wait_ge(row_lo_done, n + 1)
                for at, row in ((3 * HD, row_hi), (3 * HD + 1, row_lo)):
                    sp.dma_start(as_f32(q_st[i][at:at + 1, :, :].rearrange("o h (i t) -> o (h i) t", t=P)),
                                 as_f32(row[:])).then_inc(row_in, 16)

            def round_(n, i, g):
                if below(n, ROUNDS - 3):
                    if not (isinstance(n, int) and n == 0):
                        sp.wait_ge(pv_done, n * NS + PR)
                    load((i + 3) % SETS, g + (i + 3) // SETS)
                if below(n, ROUNDS - 1):
                    rows(n + 1, (i + 1) % SETS)

            for i in range(3):
                load(i, 0)
            rows(0, 0)
            run_rounds(sp, round_)

        @block.gpsimd
        def _(pool):
            route_pool(pool)
            nc.gpsimd.iota(keep["x_rows"][:, :, D].bitcast(U32), pattern=[[P, NT]], base=0, channel_multiplier=1).then_inc(numbered, 1)
            pool.wait_ge(numbered, 1)
            for t in (ident, ident16, mask_m, mask_t):
                nc.gpsimd.memset(t[:], 0.0).then_inc(blank, 1)
            pool.wait_ge(blank, 4)
            for t in (ident, ident16):
                nc.gpsimd.affine_select(out=t[:], in_=t[:], compare_op=ALU.not_equal, fill=1.0, base=0,
                                        pattern=[[-1, P]], channel_multiplier=1).then_inc(consts, 1)
            nc.gpsimd.affine_select(out=mask_m[:], in_=mask_m[:], compare_op=ALU.is_ge, fill=NEG, base=0,
                                    pattern=[[-1, P]], channel_multiplier=1).then_inc(consts, 1)
            nc.gpsimd.affine_select(out=mask_t[:], in_=mask_t[:], compare_op=ALU.is_ge, fill=NEG, base=0,
                                    pattern=[[1, P]], channel_multiplier=-1).then_inc(consts, 1)
            pool.wait_ge(consts, 4)
            for i in range(SETS):
                nc.gpsimd.memset(as_f32(k_st[i][3 * HD:STACK, :, :]), -1.0).then_inc(minus_ones, 1)
            pool.wait_ge(minus_ones, SETS)
            for i in range(SETS):
                nc.gpsimd.memset(v_st[i][:, :, :, HD:2 * HD], 1.0).then_inc(v_ones, 1)
            pool.wait_ge(route_done, 1)
            for j in range(TOPK):
                if j:
                    pool.wait_ge(scattered, 16 * j * NT)
                nc.gpsimd.tensor_copy(keep["x_rows"][:, :, D + 1], keep["weight"][:, j, :]).then_inc(weighted, 1)
                pool.wait_ge(weighted, j + 1)
                for a in range(NT):
                    pool.indirect_dma_start(out=scratch["routed"], out_offset=bass.IndirectOffsetOnAxis(
                        ap=keep["slot"][:, j, a:a + 1], axis=0), in_=keep["x_rows"][:, a, :], in_offset=None).then_inc(scattered, 16)

            def norm(n, i, g, c, q):
                b, cols = i // PAIRS, slice(q * PW, (q + 1) * PW)
                pool.wait_ge(inv_done, norm_number(n, c, q))
                nc.gpsimd.tensor_tensor(o_t[:, bass.ds(g, 1), b * S + c * CH + q * PW:b * S + c * CH + (q + 1) * PW],
                                        o_raw[:, c:c + 1, cols], inv[:, c:c + 1, cols], ALU.mult).then_inc(norm_done, 1)

            def round_(n, i, g):
                for k in range(NS):
                    if diagonal(k) and not (isinstance(n, int) and n == 0):
                        pool.wait_ge(exp_done, n * (PAIR * NS) + (PAIR * (k + 1) + RING))
                        p = probs[:, k % PR, :, 0:P]
                        at = i * len(diagonals) + diagonals.index(k)
                        nc.gpsimd.tensor_tensor(carrier[:, at:at + 1], ident[:, 0:1], ident[:, 0:1], ALU.mult)
                        nc.gpsimd.affine_select(out=p, in_=p, compare_op=ALU.is_ge, fill=0.0, base=0,
                                                pattern=[[0, PAIR], [1, P]], channel_multiplier=-1).then_inc(masked, 1)
                    if k >= LAG:
                        norm_at(n, i, g, k - LAG, norm)
                    elif not (isinstance(n, int) and n == 0):
                        norm_at(n - 1, (i - 1) % SETS, g - (i == 0), k - LAG + NS, norm)

            run_rounds(pool, round_)
            for k in range(NS - LAG, NS):
                norm_at(ROUNDS - 1, SETS - 1, NG - 1, k, norm)
            for q in range(PIECES):
                norm(ROUNDS - 1, SETS - 1, NG - 1, 1, q)
            pool.wait_ge(scattered, 16 * TOPK * NT)

        @block.scalar
        def _(act):
            def row_high(n):
                act.wait_ge(turned, n + 1)
                if not (isinstance(n, int) and n == 0):
                    act.wait_ge(row_in, n * 32)
                nc.scalar.copy(row_hi[:], mb[TURN_BANK][0:PAIR * TQ, 0:P]).then_inc(row_hi_done, 1)

            def o_out(n, i, c, h, row):
                at = (i % PAIRS * PAIR + h) * HD
                to = (o_raw, sums)[row][at:at + HD, c, :]
                if h == 0 and row == 0:
                    act.wait_ge(pv_done, n * NS + ((c + 1) * (c + 2) // 2 * TPC + PR))
                    if i % PAIRS == 0:
                        act.wait_ge(norm_done, n * (NORMS // PAIRS) + (c + 1) * PIECES)
                ins = nc.scalar.activation(to, o_acc[c][(2 * h + row) * HD:(2 * h + row + 1) * HD, :], ACT.Copy,
                                           scale=1.0 if row else SCALE)
                if h == 1 and row == 1:
                    ins.then_inc(o_read, 1)

            def round_(n, i, g):
                for k, (c, j) in enumerate(steps):
                    w = min(CH, (c + 1) * CH - j * P)
                    for h in range(PAIR):
                        e = PAIR * k + h
                        act.wait_ge(st_full, n * (PAIR * NS) + (e + 1))
                        if h == 0:
                            act.wait_ge(pv_done, n * NS + (k + 1))
                        nc.scalar.activation(probs[:, k % PR, h, 0:w], scores_t[e % RING][:, 0:w], ACT.Exp).then_inc(exp_done, 1)
                        if k in (1, 2) and not (isinstance(n, int) and n == 0):
                            o_out(n - 1, (i - 1) % SETS, 1, k - 1, h)
                        if k in (TPC + 1, TPC + 2):
                            o_out(n, i, 0, k - TPC - 1, h)
                    if k == TURN_STEP and below(n, ROUNDS - 1):
                        row_high(n + 1)

            row_high(0)
            act.dma_start(keep["w_proj"][:], w_proj.rearrange("(g p) d -> p g d", p=P)).then_inc(w_proj_in, 16)
            run_rounds(act, round_)
            for h in range(PAIR):
                for row in range(2):
                    o_out(ROUNDS - 1, SETS - 1, 1, h, row)
            act.wait_ge(w_proj_in, 16)

        @block.vector
        def _(dve):
            def unit(n, i, u):
                h, t, c = units[u]
                w = min(CH, (t + 1) * P - c * CH)
                dve.wait_ge(m_full, n * NU + (u + 1))
                to = mx[i % 2][:, h, t:t + 1] if c == 0 else mx_far[:, h, t - TPC:t - TPC + 1]
                nc.vector.tensor_reduce(to, mb[bank_at(place(u))][:, 0:w], AX.X, ALU.max).then_inc(m_free, 1)

            def join(n, i):
                dve.wait_ge(m_free, n * NU + NU)
                far = mx[i % 2][:, :, TPC:TQ]
                nc.vector.tensor_tensor(far, far, mx_far[:], ALU.max).then_inc(mx_done, 1)

            def row_low(n):
                dve.wait_ge(row_hi_done, n + 1)
                nc.vector.tensor_tensor(row_lo[:], mb[TURN_BANK][0:PAIR * TQ, 0:P], as_f32(row_hi[:]), ALU.subtract).then_inc(row_lo_done, 1)

            def invert(n, i, g, c, q):
                cols = slice(q * PW, (q + 1) * PW)
                dve.wait_ge(o_read, n * NC + (c + 1 + NC))
                dve.wait_ge(norm_done, norm_number(n, c, q))
                nc.vector.reciprocal(inv[:, c, cols], sums[:, c, cols]).then_inc(inv_done, 1)

            def round_(n, i, g):
                for k in range(NS):
                    if k == TURN_STEP + 1 and below(n, ROUNDS - 1):
                        row_low(n + 1)
                    if below(n, ROUNDS - 2):
                        for u in range(k * PER, (k + 1) * PER):
                            unit(n + 2, (i + 2) % SETS, u)
                    norm_at(n, i, g, k, invert)
                if below(n, ROUNDS - 2):
                    join(n + 2, (i + 2) % SETS)

            route_dve(dve)
            for u in range(NU):
                unit(0, 0, u)
            join(0, 0)
            for u in range(NU):
                if u == TURN_AT + 2:
                    row_low(0)
                unit(1, 1, u)
            join(1, 1)
            run_rounds(dve, round_)
            for q in range(PIECES):
                invert(ROUNDS - 1, SETS - 1, NG - 1, 1, q)

        @block.tensor
        def _(pe):
            def claim(n, at):
                back, before = bank_before(at, not (isinstance(n, int) and n == 0))
                if isinstance(n, int) and n < back:
                    return
                if before == TURN_AT:
                    pe.wait_ge(row_lo_done, n - back)
                else:
                    number = before - (before > TURN_AT) + 1
                    pe.wait_ge(m_free, min(n * NU - back * NU + number, ROUNDS * NU) if isinstance(n, int) else n * NU + (number - back * NU))

            def unit(n, i, u):
                h, t, c = units[u]
                w = min(CH, (t + 1) * P - c * CH)
                diag = t // TPC == c
                claim(n, place(u))
                out = mb[bank_at(place(u))]
                last = nc.tensor.matmul(out[:, 0:w], q_st[i][0:3 * HD, h, t * P:(t + 1) * P],
                                        k_st[i][0:3 * HD, h, c * CH:c * CH + w], start=True, stop=not diag)
                if diag:
                    last = nc.tensor.matmul(out[:, w - P:w], ident16[:], mask_m[:], start=False, stop=True)
                last.then_inc(m_full, 1)

            def turn(n, i, frame):
                pe.wait_ge(mx_done, n + 1)
                claim(frame, TURN_AT)
                nc.tensor.transpose(mb[TURN_BANK][0:PAIR * TQ, 0:P], mx[i % 2][:].rearrange("p h i -> p (h i)"), ident[:]).then_inc(turned, 1)

            def scores(n, i, k, h):
                c, j = steps[k]
                t0 = max(c * CH, j * P)
                w = (c + 1) * CH - t0
                diag = diagonal(k) and isinstance(n, int) and n == 0
                e = PAIR * k + h
                pe.wait_ge(exp_done, n * (PAIR * NS) + (e + 1))
                out = scores_t[e % RING]
                last = nc.tensor.matmul(out[:, 0:w], k_st[i][0:STACK, h, j * P:(j + 1) * P],
                                        q_st[i][0:STACK, h, t0:t0 + w], start=True, stop=not diag)
                if diag:
                    last = nc.tensor.matmul(out[:, 0:P], ident16[:], mask_t[:], start=False, stop=True)
                last.then_inc(st_full, 1)

            def values(n, i, k):
                c, j = steps[k]
                w = min(CH, (c + 1) * CH - j * P)
                if j == 0:
                    pe.wait_ge(o_read, n * NC + (c + 1))
                if diagonal(k) and not (isinstance(n, int) and n == 0):
                    pe.wait_ge(masked, n * len(diagonals) + (diagonals.index(k) + 1 - len(diagonals)))
                else:
                    pe.wait_ge(exp_done, n * (PAIR * NS) + (PAIR * (k + 1) + RING))
                for h in range(PAIR):
                    last = nc.tensor.matmul(o_acc[c][2 * HD * h:2 * HD * (h + 1), CH - w:CH], v_st[i][:, j, h, :],
                                            probs[:, k % PR, h, 0:w], start=(j == 0), stop=(j == (c + 1) * TPC - 1))
                last.then_inc(pv_done, 1)

            def round_(n, i, g):
                if below(n, ROUNDS - 2):
                    pe.wait_ge(loaded[(i + 2) % SETS], (g + ((i + 2) // SETS + 1)) * 16 * LOADS)
                for k in range(NS):
                    if k == TURN_STEP and below(n, ROUNDS - 1):
                        turn(n + 1, (i + 1) % SETS, n + 2)
                    for h in range(PAIR):
                        if k + LEAD < NS:
                            scores(n, i, k + LEAD, h)
                        elif below(n, ROUNDS - 1):
                            if h == 0 and k + LEAD == NS:
                                pe.wait_ge(row_in, n * 32 + 64)
                            scores(n + 1, (i + 1) % SETS, k + LEAD - NS, h)
                        if below(n, ROUNDS - 2):
                            unit(n + 2, (i + 2) % SETS, k * PER + h)
                    values(n, i, k)

            route_pe(pe)
            pe.wait_ge(consts, 4)
            pe.wait_ge(loaded[0], 16 * LOADS)
            for u in range(NU):
                unit(0, 0, u)
            pe.wait_ge(loaded[1], 16 * LOADS)
            for u in range(NU):
                if u == TURN_AT:
                    turn(0, 0, 1)
                unit(1, 1, u)
            pe.wait_ge(row_in, 32)
            pe.wait_ge(minus_ones, SETS)
            pe.wait_ge(v_ones, SETS)
            pe.wait_ge(route_done, 1)
            for k in range(LEAD):
                for h in range(PAIR):
                    scores(0, 0, k, h)
            nc.disable_value_cache = True
            run_rounds(pe, round_)
            nc.disable_value_cache = False


def attention_and_experts(nc, x, w_attn, bias_qk, bias_qk_pair, bias_v, w_proj, b_proj, gate_t, w1_t, w2_t,
                          rope_cos, rope_sin, rope_cos_col, rope_sin_col, out):
    scratch = {
        "qk_hi": nc.dram_tensor("qk_hi", [2 * D, T], F32).ap(),
        "qk_lo": nc.dram_tensor("qk_lo", [2 * D, T], F32).ap(),
        "v": nc.dram_tensor("v_all", [T, D], F32).ap(),
        "routed": nc.dram_tensor("routed", [CLEAR_TILES * P, XW], F32).ap(),
        "acc": nc.dram_tensor("acc", [T + P, D], F32).ap(),
    }
    ctx = ExitStack()
    with ctx:
        m = Memory(nc, ctx)
        keep = {
            "o_t": m.sbuf("o_t", [P, NG, T], F32),
            "w_proj": m.sbuf("w_proj", [P, NG, D], F32),
            "slot": m.sbuf("slot", [P, TOPK, NT], U32),
            "weight": m.sbuf("weight", [P, TOPK, NT], F32),
            "tile_expert": m.sbuf("tile_expert", [1, SLOT_TILES], I32),
        }
        with ExitStack() as until_attended:
            m = Memory(nc, until_attended)
            keep["x_rows"] = m.sbuf("x_rows", [P, NT, XW], F32)
            keep["mask"] = m.sbuf("mask", [P, TOPK, NT, E], F32)
            keep["both"] = m.sbuf("both", [P, NT, E], BF16)
            project_qkv(nc, keep, scratch, x, w_attn, bias_qk, bias_qk_pair, bias_v, gate_t, rope_cos, rope_sin,
                        rope_cos_col, rope_sin_col)
            attend(nc, keep, scratch, w_proj)
        experts(nc, keep, scratch, x, b_proj, w1_t, w2_t, out)


def kernel(L0_attn_x, L0_attn_w_attn, L0_attn_b_attn, L0_attn_w_proj, L0_attn_b_proj, L0_ffn_gate_w, L0_ffn_w1, L0_ffn_w2):
    import numpy as np
    import concourse.bacc as bacc
    from concourse.bass_utils import run_bass_kernel_spmd

    half = HD // 2
    freqs = np.float32(10000.0) ** (-(np.arange(0, HD, 2, dtype=np.float32) / np.float32(HD)))
    angle = np.outer(np.arange(H, dtype=np.float32), freqs).astype(np.float32)
    cos = np.repeat(np.cos(angle).reshape(-1), 2).astype(np.float32)
    sin = (np.repeat(np.sin(angle).reshape(-1), 2) * np.tile([-1.0, 1.0], H * half)).astype(np.float32)

    def columns(v):
        return v.reshape(QK_TILES, P).T

    b = np.asarray(L0_attn_b_attn)
    b_qk = b[:2 * D]
    pair = b_qk.reshape(-1, 2)[:, ::-1].reshape(-1)
    laid_out = {
        "x": L0_attn_x, "w_attn": L0_attn_w_attn, "bias_qk": columns(b_qk), "bias_qk_pair": columns(pair),
        "bias_v": b[2 * D:], "w_proj": L0_attn_w_proj, "b_proj": L0_attn_b_proj,
        "gate_t": np.asarray(L0_ffn_gate_w).T, "w1_t": np.asarray(L0_ffn_w1).transpose(0, 2, 1),
        "w2_t": np.asarray(L0_ffn_w2).transpose(0, 2, 1), "rope_cos": cos, "rope_sin": sin,
        "rope_cos_col": columns(np.tile(cos, 2)), "rope_sin_col": columns(np.tile(sin, 2)),
    }
    nc = bacc.Bacc("TRN2", target_bir_lowering=False, num_devices=1)
    arrays, args = {}, []
    for name, value in laid_out.items():
        a = np.ascontiguousarray(value)
        arrays[f"in_{name}"] = a
        args.append(nc.dram_tensor(f"in_{name}", a.shape, mybir.dt.from_np(a.dtype), kind="ExternalInput").ap())
    args.append(nc.dram_tensor("out_0", (B, S, D), F32, kind="ExternalOutput").ap())
    attention_and_experts(nc, *args)
    r = run_bass_kernel_spmd(nc, [arrays], core_ids=[0])
    return r.results[0]["out_0"]
```
